# Optimizing a Trainium2 kernel written in Bass

```python
import numpy as np
import jax
import jax.numpy as jnp

def _softmax(x, axis=-1):
    return jax.nn.softmax(x, axis=axis)

def _gelu(x):
    return jax.nn.gelu(x, approximate=True)

def _silu(x):
    return jax.nn.silu(x)

def _sigmoid(x):
    return jax.nn.sigmoid(x)

def _layernorm(x, axis=-1, eps=1e-05):
    m = jnp.mean(x, axis=axis, keepdims=True)
    v = jnp.var(x, axis=axis, keepdims=True)
    return (x - m) / jnp.sqrt(v + eps)

def _scatter_add(tgt, idx, src, axis=0):
    return tgt.at[idx].add(src)

def _segment_sum(src, seg, n):
    return jax.ops.segment_sum(src, seg, n)
kernel_name = 'mk_decoder_postln_d1_seqx_r8_0944d7'

def setup_inputs(seed: int=0):
    np.random.seed(seed)
    _w = jnp.asarray

    def _rec_inputs():
        import jax
        import jax.numpy as jnp
        _rk = jax.random.key(seed)
        x = 4.136e-05 + 0.9999 * jax.random.normal(jax.random.fold_in(_rk, 1), (4, 256, 256), jnp.float32)
        _lenS = 256 - jax.random.randint(jax.random.fold_in(_rk, 7), (4,), 0, max(1, 256 // 4) + 1, jnp.int32)
        _lenS2 = 256 - jax.random.randint(jax.random.fold_in(_rk, 8), (4,), 0, max(1, 256 // 4) + 1, jnp.int32)
        _ctx_1024P = jax.random.normal(jax.random.fold_in(_rk, 11), (4, 16, 128), jnp.float32)
        _ctx_1024c = jax.random.dirichlet(jax.random.fold_in(_rk, 511), 0.3 * jnp.ones((16,), jnp.float32), (4, 256))
        _ctx_1024t = jnp.einsum('bsk,bkd->bsd', _ctx_1024c, _ctx_1024P)
        _ctx_1024t = _ctx_1024t * jax.lax.rsqrt(jnp.mean(jnp.square(_ctx_1024t)) + 1e-12) * 0.953939
        ctx_1024 = -0.000292821 + 1.00034 * (_ctx_1024t + 0.3 * jax.random.normal(jax.random.fold_in(_rk, 611), (4, 256, 128), jnp.float32))
        return (x, ctx_1024)
    x, ctx_1024 = _rec_inputs()

    def _L0_attn_setup():
        import jax, jax.numpy as jnp
        import numpy as np
        B, S, HID, QK, H = (2, 256, 256, 256, 16)
        DK, DV = (QK // H, HID // H)
        EPS = 1e-05
        key = jax.random.key(seed)
        ks = jax.random.split(key, 8)
        sd = 1.0 / np.sqrt(HID)
        inp = {'x': jax.random.normal(ks[0], (B, S, HID), jnp.float32), 'wq': jax.random.normal(ks[1], (HID, QK), jnp.float32) * sd, 'bq': jnp.zeros((QK,), jnp.float32), 'wk': jax.random.normal(ks[2], (HID, QK), jnp.float32) * sd, 'bk': jnp.zeros((QK,), jnp.float32), 'wv': jax.random.normal(ks[3], (HID, HID), jnp.float32) * sd, 'bv': jnp.zeros((HID,), jnp.float32), 'wg': jax.random.normal(ks[4], (HID, HID), jnp.float32) * sd, 'bg': jnp.zeros((HID,), jnp.float32), 'wo': jax.random.normal(ks[5], (HID, HID), jnp.float32) * sd, 'bo': jnp.zeros((HID,), jnp.float32), 'gn_w': jnp.ones((HID,), jnp.float32), 'gn_b': jnp.zeros((HID,), jnp.float32), 'gamma': 1.0 - jnp.exp(jnp.linspace(-np.log(32.0), -np.log(512.0), H)).astype(jnp.float32)}
        return inp
    _L0_attn_all = _L0_attn_setup()
    _L0_attn_in = {k: v for k, v in _L0_attn_all.items() if k in ('wq', 'bq', 'wk', 'bk', 'wv', 'bv', 'wg', 'bg', 'wo', 'bo', 'gn_w', 'gn_b', 'gamma')}
    del _L0_attn_all

    def _L0_xattn_setup():
        import jax, jax.numpy as jnp
        import numpy as np
        import math
        B, L, DM = (2, 256, 128)
        DS, DC, EXP = (16, 4, 2)
        DI = EXP * DM
        DR = math.ceil(DM / 16)
        DT_MIN, DT_MAX, DT_FLOOR = (0.001, 0.1, 0.0001)

        def _ssm_forward(hidden_states, z, in_proj_w, conv_w, conv_b, x_proj_w, dt_proj_w, dt_proj_b, A_log, D):
            b = hidden_states.shape[0]
            x = jnp.einsum('ed,bld->bel', in_proj_w, hidden_states)
            xp = jnp.pad(x, ((0, 0), (0, 0), (DC - 1, 0)))
            xc = jax.lax.conv_general_dilated(xp, conv_w[:, None, :], window_strides=(1,), padding='VALID', dimension_numbers=('NCH', 'OIH', 'NCH'), feature_group_count=DI)
            u = jax.nn.silu(xc + conv_b[None, :, None])
            x_dbl = jnp.einsum('ke,bel->bkl', x_proj_w, u)
            dt_lo = x_dbl[:, :DR]
            Bm = x_dbl[:, DR:DR + DS]
            Cm = x_dbl[:, DR + DS:]
            delta = jax.nn.softplus(jnp.einsum('er,brl->bel', dt_proj_w, dt_lo) + dt_proj_b[None, :, None])
            A = -jnp.exp(A_log)

            def step(state, xs):
                d_t, B_t, C_t, u_t = xs
                dA = jnp.exp(d_t[..., None] * A)
                state = state * dA + (d_t * u_t)[..., None] * B_t[:, None, :]
                y_t = jnp.einsum('ben,bn->be', state, C_t)
                return (state, y_t)
            xs = (jnp.moveaxis(delta, -1, 0), jnp.moveaxis(Bm, -1, 0), jnp.moveaxis(Cm, -1, 0), jnp.moveaxis(u, -1, 0))
            state0 = jnp.zeros((b, DI, DS), delta.dtype)
            _, ys = jax.lax.scan(step, state0, xs)
            y = jnp.moveaxis(ys, 0, -1)
            y = y + D[None, :, None] * u
            y = y * jax.nn.silu(z)
            return jnp.swapaxes(y, 1, 2)
        key = jax.random.key(seed)
        ks = jax.random.split(key, 8)
        hidden_states = jax.random.normal(ks[0], (B, L, DM), jnp.float32)
        z = jax.random.normal(ks[1], (B, DI, L), jnp.float32)
        in_proj_w = jax.random.normal(ks[2], (DI, DM), jnp.float32) * DM ** (-0.5)
        conv_w = jax.random.normal(ks[3], (DI, DC), jnp.float32) * DC ** (-0.5)
        conv_b = jnp.zeros((DI,), jnp.float32)
        x_proj_w = jax.random.normal(ks[4], (DR + 2 * DS, DI), jnp.float32) * DI ** (-0.5)
        dt_std = DR ** (-0.5)
        dt_proj_w = jax.random.uniform(ks[5], (DI, DR), jnp.float32, -dt_std, dt_std)
        dt = jnp.exp(jax.random.uniform(ks[6], (DI,), jnp.float32) * (math.log(DT_MAX) - math.log(DT_MIN)) + math.log(DT_MIN))
        dt = jnp.clip(dt, DT_FLOOR)
        dt_proj_b = dt + jnp.log(-jnp.expm1(-dt))
        A_log = jnp.log(jnp.broadcast_to(jnp.arange(1, DS + 1, dtype=jnp.float32), (DI, DS)))
        D = jnp.ones((DI,), jnp.float32)
        return dict(hidden_states=hidden_states, z=z, in_proj_w=in_proj_w, conv_w=conv_w, conv_b=conv_b, x_proj_w=x_proj_w, dt_proj_w=dt_proj_w, dt_proj_b=dt_proj_b, A_log=A_log, D=D)
    _L0_xattn_all = _L0_xattn_setup()
    _L0_xattn_in = {k: v for k, v in _L0_xattn_all.items() if k in ('in_proj_w', 'conv_w', 'conv_b', 'x_proj_w', 'dt_proj_w', 'dt_proj_b', 'A_log', 'D')}
    del _L0_xattn_all

    def _L0_ffn_setup():
        import jax, jax.numpy as jnp
        import numpy as np
        B, S, H, F, E, R, K = (2, 128, 256, 896, 8, 32, 2)

        def _gather_slot(a_all, e):
            return jnp.take_along_axis(a_all, e[:, None, None], axis=1)[:, 0]
        key = jax.random.key(seed)
        ks = jax.random.split(key, 12)
        sc = 0.02
        n = lambda k, shape, s: jax.random.normal(k, shape, dtype=jnp.float32) * s
        return {'hidden_states': n(ks[0], (B, S, H), 1.0), 'Wg': n(ks[1], (E, H), sc), 'W1': n(ks[2], (F, H), sc), 'W2': n(ks[3], (H, F), sc), 'W3': n(ks[4], (F, H), sc), 'A1': n(ks[5], (E, R, H), sc), 'B1': n(ks[6], (E, F, R), sc), 'A2': n(ks[7], (E, R, F), sc), 'B2': n(ks[8], (E, H, R), sc), 'A3': n(ks[9], (E, R, H), sc), 'B3': n(ks[10], (E, F, R), sc)}
    _L0_ffn_all = _L0_ffn_setup()
    _L0_ffn_in = {k: v for k, v in _L0_ffn_all.items() if k in ('Wg', 'W1', 'W2', 'W3', 'A1', 'B1', 'A2', 'B2', 'A3', 'B3')}
    del _L0_ffn_all
    return {'x': x, 'ctx_1024': ctx_1024, 'L0_attn_wq': _L0_attn_in['wq'], 'L0_attn_bq': _L0_attn_in['bq'], 'L0_attn_wk': _L0_attn_in['wk'], 'L0_attn_bk': _L0_attn_in['bk'], 'L0_attn_wv': _L0_attn_in['wv'], 'L0_attn_bv': _L0_attn_in['bv'], 'L0_attn_wg': _L0_attn_in['wg'], 'L0_attn_bg': _L0_attn_in['bg'], 'L0_attn_wo': _L0_attn_in['wo'], 'L0_attn_bo': _L0_attn_in['bo'], 'L0_attn_gn_w': _L0_attn_in['gn_w'], 'L0_attn_gn_b': _L0_attn_in['gn_b'], 'L0_attn_gamma': _L0_attn_in['gamma'], 'L0_xattn_in_proj_w': _L0_xattn_in['in_proj_w'], 'L0_xattn_conv_w': _L0_xattn_in['conv_w'], 'L0_xattn_conv_b': _L0_xattn_in['conv_b'], 'L0_xattn_x_proj_w': _L0_xattn_in['x_proj_w'], 'L0_xattn_dt_proj_w': _L0_xattn_in['dt_proj_w'], 'L0_xattn_dt_proj_b': _L0_xattn_in['dt_proj_b'], 'L0_xattn_A_log': _L0_xattn_in['A_log'], 'L0_xattn_D': _L0_xattn_in['D'], 'L0_ffn_Wg': _L0_ffn_in['Wg'], 'L0_ffn_W1': _L0_ffn_in['W1'], 'L0_ffn_W2': _L0_ffn_in['W2'], 'L0_ffn_W3': _L0_ffn_in['W3'], 'L0_ffn_A1': _L0_ffn_in['A1'], 'L0_ffn_B1': _L0_ffn_in['B1'], 'L0_ffn_A2': _L0_ffn_in['A2'], 'L0_ffn_B2': _L0_ffn_in['B2'], 'L0_ffn_A3': _L0_ffn_in['A3'], 'L0_ffn_B3': _L0_ffn_in['B3']}

def reference(x, ctx_1024, L0_attn_wq, L0_attn_bq, L0_attn_wk, L0_attn_bk, L0_attn_wv, L0_attn_bv, L0_attn_wg, L0_attn_bg, L0_attn_wo, L0_attn_bo, L0_attn_gn_w, L0_attn_gn_b, L0_attn_gamma, L0_xattn_in_proj_w, L0_xattn_conv_w, L0_xattn_conv_b, L0_xattn_x_proj_w, L0_xattn_dt_proj_w, L0_xattn_dt_proj_b, L0_xattn_A_log, L0_xattn_D, L0_ffn_Wg, L0_ffn_W1, L0_ffn_W2, L0_ffn_W3, L0_ffn_A1, L0_ffn_B1, L0_ffn_A2, L0_ffn_B2, L0_ffn_A3, L0_ffn_B3):
    import jax
    import jax.numpy as jnp

    def _L0_attn_ref(x, wq, bq, wk, bk, wv, bv, wg, bg, wo, bo, gn_w, gn_b, gamma):
        import jax, jax.numpy as jnp
        import numpy as np
        B, S, HID, QK, H = (2, 256, 256, 256, 16)
        DK, DV = (QK // H, HID // H)
        EPS = 1e-05
        b, s, hid = x.shape
        h = gamma.shape[0]
        dk = wq.shape[1] // h
        dv = hid // h
        q = (x @ wq + bq).reshape(b, s, h, dk).transpose(0, 2, 1, 3)
        k = (x @ wk + bk).reshape(b, s, h, dk).transpose(0, 2, 1, 3)
        v = (x @ wv + bv).reshape(b, s, h, dv).transpose(0, 2, 1, 3)
        idx = jnp.arange(s)
        diff = idx[:, None] - idx[None, :]
        expn = jnp.maximum(diff, 0).astype(x.dtype)
        dmask = jnp.where(diff >= 0, gamma[:, None, None] ** expn, 0.0)
        scores = jnp.einsum('bhnd,bhmd->bhnm', q, k) * dmask
        ret = jnp.einsum('bhnm,bhmv->bhnv', scores, v)
        mean = ret.mean(axis=(2, 3), keepdims=True)
        var = ((ret - mean) ** 2).mean(axis=(2, 3), keepdims=True)
        norm = (ret - mean) * jax.lax.rsqrt(var + EPS)
        norm = norm * gn_w.reshape(h, dv)[None, :, None, :] + gn_b.reshape(h, dv)[None, :, None, :]
        ro = norm.transpose(0, 2, 1, 3).reshape(b, s, hid)
        gate = jax.nn.silu(x @ wg + bg)
        out = gate * ro @ wo + bo
        return out

    def _L0_xattn_ref(hidden_states, z, in_proj_w, conv_w, conv_b, x_proj_w, dt_proj_w, dt_proj_b, A_log, D):
        import jax, jax.numpy as jnp
        import numpy as np
        import math
        B, L, DM = (2, 256, 128)
        DS, DC, EXP = (16, 4, 2)
        DI = EXP * DM
        DR = math.ceil(DM / 16)
        DT_MIN, DT_MAX, DT_FLOOR = (0.001, 0.1, 0.0001)

        def _ssm_forward(hidden_states, z, in_proj_w, conv_w, conv_b, x_proj_w, dt_proj_w, dt_proj_b, A_log, D):
            b = hidden_states.shape[0]
            x = jnp.einsum('ed,bld->bel', in_proj_w, hidden_states)
            xp = jnp.pad(x, ((0, 0), (0, 0), (DC - 1, 0)))
            xc = jax.lax.conv_general_dilated(xp, conv_w[:, None, :], window_strides=(1,), padding='VALID', dimension_numbers=('NCH', 'OIH', 'NCH'), feature_group_count=DI)
            u = jax.nn.silu(xc + conv_b[None, :, None])
            x_dbl = jnp.einsum('ke,bel->bkl', x_proj_w, u)
            dt_lo = x_dbl[:, :DR]
            Bm = x_dbl[:, DR:DR + DS]
            Cm = x_dbl[:, DR + DS:]
            delta = jax.nn.softplus(jnp.einsum('er,brl->bel', dt_proj_w, dt_lo) + dt_proj_b[None, :, None])
            A = -jnp.exp(A_log)

            def step(state, xs):
                d_t, B_t, C_t, u_t = xs
                dA = jnp.exp(d_t[..., None] * A)
                state = state * dA + (d_t * u_t)[..., None] * B_t[:, None, :]
                y_t = jnp.einsum('ben,bn->be', state, C_t)
                return (state, y_t)
            xs = (jnp.moveaxis(delta, -1, 0), jnp.moveaxis(Bm, -1, 0), jnp.moveaxis(Cm, -1, 0), jnp.moveaxis(u, -1, 0))
            state0 = jnp.zeros((b, DI, DS), delta.dtype)
            _, ys = jax.lax.scan(step, state0, xs)
            y = jnp.moveaxis(ys, 0, -1)
            y = y + D[None, :, None] * u
            y = y * jax.nn.silu(z)
            return jnp.swapaxes(y, 1, 2)
        return _ssm_forward(hidden_states, z, in_proj_w, conv_w, conv_b, x_proj_w, dt_proj_w, dt_proj_b, A_log, D)

    def _L0_ffn_ref(hidden_states, Wg, W1, W2, W3, A1, B1, A2, B2, A3, B3):
        import jax, jax.numpy as jnp
        import numpy as np
        B, S, H, F, E, R, K = (2, 128, 256, 896, 8, 32, 2)

        def _gather_slot(a_all, e):
            return jnp.take_along_axis(a_all, e[:, None, None], axis=1)[:, 0]
        b, s, h = hidden_states.shape
        x = hidden_states.reshape(-1, h)
        nE = Wg.shape[0]
        logits = x @ Wg.T
        probs = jax.nn.softmax(logits.astype(jnp.float32), axis=-1)
        rw, sel = jax.lax.top_k(probs, K)
        rw = (rw / rw.sum(axis=-1, keepdims=True)).astype(x.dtype)
        base1 = x @ W1.T
        base3 = x @ W3.T
        a1_all = jnp.einsum('th,erh->ter', x, A1)
        a3_all = jnp.einsum('th,erh->ter', x, A3)
        out = jnp.zeros_like(x)
        for k in range(K):
            e = sel[:, k]
            mask = jax.nn.one_hot(e, nE, dtype=x.dtype)
            a1 = _gather_slot(a1_all, e)
            a3 = _gather_slot(a3_all, e)
            lora1 = jnp.einsum('ter,efr->tf', mask[:, :, None] * a1[:, None, :], B1)
            lora3 = jnp.einsum('ter,efr->tf', mask[:, :, None] * a3[:, None, :], B3)
            x1 = base1 + lora1
            x3 = base3 + lora3
            x2 = jax.nn.silu(x1) * x3
            down = x2 @ W2.T
            a2_all = jnp.einsum('tf,erf->ter', x2, A2)
            a2 = _gather_slot(a2_all, e)
            lora2 = jnp.einsum('ter,ehr->th', mask[:, :, None] * a2[:, None, :], B2)
            out = out + (down + lora2) * rw[:, k:k + 1]
        return out.reshape(b, s, h)
    x = _layernorm(x + _L0_attn_ref(x, L0_attn_wq, L0_attn_bq, L0_attn_wk, L0_attn_bk, L0_attn_wv, L0_attn_bv, L0_attn_wg, L0_attn_bg, L0_attn_wo, L0_attn_bo, L0_attn_gn_w, L0_attn_gn_b, L0_attn_gamma), axis=-1)
    x = _layernorm(x + _L0_xattn_ref(ctx_1024, x, L0_xattn_in_proj_w, L0_xattn_conv_w, L0_xattn_conv_b, L0_xattn_x_proj_w, L0_xattn_dt_proj_w, L0_xattn_dt_proj_b, L0_xattn_A_log, L0_xattn_D), axis=-1)
    x = _layernorm(x + _L0_ffn_ref(x, L0_ffn_Wg, L0_ffn_W1, L0_ffn_W2, L0_ffn_W3, L0_ffn_A1, L0_ffn_B1, L0_ffn_A2, L0_ffn_B2, L0_ffn_A3, L0_ffn_B3), axis=-1)
    return x

_drawn_inputs = setup_inputs


def setup_inputs(seed=0):
    import zlib

    import numpy as np

    out = dict(_drawn_inputs(seed))
    spreads = {'L0_attn_bq': (0.0, 0.1),
     'L0_attn_bk': (0.0, 0.1),
     'L0_attn_bv': (0.0, 0.1),
     'L0_attn_bg': (0.0, 0.1),
     'L0_attn_bo': (0.0, 0.1),
     'L0_attn_gn_w': (1.0, 0.2),
     'L0_attn_gn_b': (0.0, 0.1),
     'L0_xattn_conv_b': (0.0, 0.1),
     'L0_xattn_D': (1.0, 0.2)}
    factors = {'L0_xattn_dt_proj_w': 6.554,
     'L0_xattn_dt_proj_b': 2.803,
     'L0_ffn_Wg': 8.0,
     'L0_ffn_A1': 8.0,
     'L0_ffn_B1': 8.0,
     'L0_ffn_A2': 8.0,
     'L0_ffn_B2': 8.0,
     'L0_ffn_A3': 8.0,
     'L0_ffn_B3': 8.0}
    for name, (base, spread) in spreads.items():
        noise = np.random.default_rng([zlib.crc32(name.encode()), seed]).standard_normal(out[name].shape)
        drawn = base * np.exp(spread * noise) if base else spread * noise
        out[name] = jnp.asarray(drawn.astype(out[name].dtype))
    for name, factor in factors.items():
        out[name] = (out[name] * factor).astype(out[name].dtype)
    return out
```

```python
import concourse.bass as bass
from concourse import mybir
from contextlib import ExitStack

B, S, H = 4, 256, 256
P = 128
NT, NH2 = S // P, H // P
HEADS, DH = 16, 16
GH = P // DH
DI, DS, DR, DC = 256, 16, 8, 4
E, R, F = 8, 32, 896
FM = F // P
EPS = 1e-5
UN = 2
UNITS = 2 * DS // UN

VEC = {}
_at = 0
for _n, _w in (("bq", 2), ("bk", 2), ("bg", 2), ("gnw", 2), ("gnb", 2), ("cw", 2 * DC), ("cb", 2),
               ("dtb", 2), ("D", 2), ("alog", 2 * DS)):
    VEC[_n] = (_at, _at + _w)
    _at += _w
NVEC = _at
FFW = {}
_at = 0
for _n, _w in (("A1", 2 * 256), ("A3", 2 * 256), ("W1", 2 * F), ("W3", 2 * F), ("B1", 2 * F), ("B3", 2 * F),
               ("A2", FM * 256), ("W2", FM * H), ("B2", 2 * H)):
    FFW[_n] = (_at, _at + _w)
    _at += _w
NFFW = _at

PER = dict(
    x_in=16, xn_in=16, ctx_in=16, bc_out=16, b_in0=64, b_in1=64, c_in0=64, c_in1=64, y_out=16,
    gen_filled=23,
    conv_in=3, conv_step=6, conv_tanh=1, u_ready=1, dbl_ready=1, dt_parts=4, dt_exp=1, dt_log=1, dt_step=4,
    du_ready=1, decay_ready=2 * DS, drive_ready=UNITS, state_ready=UNITS, out_ready=UNITS, y_part=UNITS,
    yT_ready=3,
    q_ready=6, qd_ready=1, k_ready=2, gate_lin=2, gate_tanh=1, gate_ready=1, v_ready=4, kd_ready=2,
    kv_ready=1, sc_ready=8, av_done=8, gn_step=12, gn_pow=1, ro_lin=2, ro_ready=1, xb_ready=1,
    r1_ready=7, r1_pow=1, x1_ready=2, z_tanh=1, r2_ready=8, r2_pow=1, x2_ready=2, x2T_ready=1,
    lg_ready=1, lg_exp=1, rt_step=21,
    xf_filled=20, rtT_ready=1, mk_ready=2, rw_ready=1, keep_ready=1, mk1_ready=1, am_ready=4,
    th_ready=14, s_ready=14, q3_ready=14, xs_ready=14, xsum_ready=7, xs_used=14, xsum_used=7,
    a2_ready=3, down_done=1, r3_ready=7, r3_pow=1, y_ready=2,
)
GIVEN = ("xs_used", "xsum_used", "xsum_ready", "r3_ready", "a2_ready", "xs_ready", "s_ready", "q3_ready", "y_out")
GEN = [("conv_in", 3), ("q_ready", 6), ("k_ready", 2), ("gate_lin", 2), ("dbl_ready", 1), ("v_ready", 4),
       ("dt_parts", 4), ("kd_ready", 1), ("kv_ready", 1)] + [("sc_ready", i + 1) for i in range(8)] + [
       ("gn_step", 6), ("gn_step", 9), ("r1_ready", 1), ("r2_ready", 2), ("x2T_ready", 1), ("lg_ready", 1)]
(G_IN, G_Q, G_K, G_GATE, G_DBL, G_V, G_DT, G_KN, G_KV, G_SC) = range(10)
(G_MEAN, G_VAR, G_OUT, G_Y, G_X2, G_LG) = range(G_SC + 8, G_SC + 14)
MAIN = [(0, 0), (1, 0), (0, 1), (1, 1), (2, 0), (3, 0), (2, 1), (3, 1), (4, 0), (5, 0), (4, 1), (5, 1), (6, 0), (6, 1)]
XF = [("rtT_ready", 1), ("mk_ready", 1), ("mk_ready", 2), ("rw_ready", 1), ("am_ready", 2), ("am_ready", 4)] + [
      ("q3_ready", n + 1) for n in range(len(MAIN))]
X_RT, X_MK, X_MD, X_RW, X_A1, X_A3, X_MAIN = range(7)
XF_BANK = [1, 0, 1, 0, 1, 0] + [(m + 1) % 2 for m, _ in MAIN]
LAG = 2


def decoder_layer(nc, x, xT, ctxT, vec, rows, gamma, wattn, wssm, wdt, wroute, wff, out):
    f32 = mybir.dt.float32
    ALU = mybir.AluOpType
    ACT = mybir.ActivationFunctionType
    AX = mybir.AxisListType

    with ExitStack() as ctx:
        def sb(name, *shape):
            return ctx.enter_context(nc.sbuf_tensor(name, list(shape), f32))

        def ps(name, *shape):
            return ctx.enter_context(nc.psum_tensor(name, list(shape), f32))

        pow_dram = nc.dram_tensor("pow_dram", (HEADS, P, 2 * P), f32, kind="Internal").ap()
        bc_dram = nc.dram_tensor("bc_dram", (B, 2 * DS, S), f32, kind="Internal").ap()

        vec_sb = sb("vec_sb", P, NVEC)
        rows_sb = sb("rows_sb", P, 3, H)
        bv_row, bk_row, bo_row = (rows_sb[:, i, :] for i in range(3))
        wattn_sb = sb("wattn_sb", P, 5, 2, H)
        wq, wk, wv, wg, wo = (wattn_sb[:, i] for i in range(5))
        wssm_sb = sb("wssm_sb", P, DI + 2 * (DR + 2 * DS))
        w_in = wssm_sb[:, 0:DI]
        w_xp = wssm_sb[:, DI:].rearrange("p (j r) -> p j r", j=2)
        wdt_sb = sb("wdt_sb", DR, DI)
        wroute_sb = sb("wroute_sb", P, 2, E)
        wff_sb = sb("wff_sb", P, NFFW)

        def ffw(name, t):
            a, b_ = FFW[name]
            return wff_sb[:, a:b_].rearrange("p (t n) -> p t n", t=t)

        A1, A3, W1, W3, B1, B3, B2 = (ffw(n, 2) for n in ("A1", "A3", "W1", "W3", "B1", "B3", "B2"))
        A2, W2 = ffw("A2", FM), ffw("W2", FM)

        def v_(name):
            a, b_ = VEC[name]
            return vec_sb[:, a:b_]

        ident = sb("ident", P, P)
        headblk = sb("headblk", P, P)
        headavg = sb("headavg", P, P)
        par = sb("par", P, 2)
        bq2 = sb("bq2", P, 2, 2)
        bgh = sb("bgh", P, 2)
        cwh = sb("cwh", P, 2, DC)
        cbh = sb("cbh", P, 2)
        nega = sb("nega", P, 2, DS)
        slots8 = sb("slots8", P, E)
        mhalf = sb("mhalf", P, 2)
        gamma_sb = sb("gamma_sb", HEADS, 1)
        powrow = sb("powrow", HEADS, 2 * P)
        dmask = sb("dmask", P, HEADS, P)
        qdec = sb("qdec", P, 2, P)

        ctx_sb = sb("ctx_sb", P, S)
        xpad = sb("xpad", P, 2, S + DC - 1)
        cv = sb("cv", P, 2, S)
        u = sb("u", P, 2, S)
        dbl = sb("dbl", DR + 2 * DS, S)
        yT = sb("yT", P, 2, S)
        dt_abs = yT
        dt_pos = sb("dt_pos", P, 2, S)
        dt_e = sb("dt_e", P, 2, S)
        cth = dt_e
        dt_w = sb("dt_w", P, 2, S)
        dt_ln = dt_abs
        delta = dt_w
        du = cv
        brow = sb("brow", P, 2, UN, S)
        crow = sb("crow", P, 2, UN, S)
        decay = sb("decay", P, 2, UN, S)
        drive = sb("drive", P, 2, UN, S)
        state = sb("state", P, 2, UN, S)

        xT_sb = sb("xT_sb", P, 2, S)
        xn_sb = sb("xn_sb", P, NT, H)
        qp = sb("qp", P, 2, 2, S)
        qf = sb("qf", P, 2, P)
        qd = qf
        kT = sb("kT", P, 2, S)
        glin = sb("glin", P, 2, S)
        gth = sb("gth", P, 2, S)
        gate = gth
        vpad = sb("vpad", P, NT, 2, H)
        kd = sb("kd", P, H)
        kv = sb("kv", P, 2, P)
        sc = sb("sc", P, 2, 2, 2, P)
        gst = sb("gst", P, 2, 6)
        gmv = sb("gmv", P, 2, 2)
        geps = sb("geps", P, 2, 2)
        gdev = sb("gdev", P, 2)
        gavg = sb("gavg", P, 2, 2)
        gsq = sb("gsq", P, 2)
        gvar = sb("gvar", P, 2)
        grs = sb("grs", P, 2)
        gscale = sb("gscale", P, 2)
        gms = sb("gms", P, 2)
        gshift = sb("gshift", P, 2)
        rlin = sb("rlin", P, 2, S)
        ro = rlin
        xb = xn_sb
        r1 = sb("r1", P, NT, H)
        st = sb("st", P, NT, 6)
        ve = sb("ve", P, NT)
        mv = sb("mv", P, NT, 2)
        rs = sb("rs", P, NT)
        x1 = sb("x1", P, NT, H)
        zth = sb("zth", P, NT, H)
        zs = zth
        r2 = r1
        x2 = sb("x2", P, NT, H)
        x2T = sb("x2T", P, 2, S)

        lg = sb("lg", P, NT, E)
        le = sb("le", P, NT, E)
        pr = sb("pr", P, NT, E)
        eq = sb("eq", P, NT, E)
        mk1 = sb("mk1", P, NT, E)
        rt = sb("rt", P, NT, 2 * E + 2)
        mk0, md, rw = rt[:, :, 0:E], rt[:, :, E:2 * E], rt[:, :, 2 * E:]
        rtT = sb("rtT", 2 * E + 2, S)
        spreadw = sb("spreadw", 2 * E + 2, 6, P)
        t1 = sb("t1", P, NT)
        t2 = sb("t2", P, NT)
        top = sb("top", P, NT, 2)

        keep = sb("keep", P, NT, H)
        mkT = sb("mkT", P, 2, 2, S)
        mk1T = sb("mk1T", P, 2, S)
        rwT = sb("rwT", P, 2, S)
        am = sb("am", P, 4, 2, S)
        fth = sb("fth", P, 2, S)
        fs = fth
        fq = sb("fq", P, 2, S)
        xs = sb("xs", P, 4, S)
        xsum = sb("xsum", P, 2, S)
        a2m = sb("a2m", P, 2, 2, S)
        r3 = keep
        st3 = sb("st3", P, NT, 6)
        ve3 = sb("ve3", P, NT)
        mv3 = sb("mv3", P, NT, 2)
        rs3 = sb("rs3", P, NT)
        yo = sb("yo", P, NT, H)

        gen = [ps(f"gen{i}", P, 512) for i in range(2)]
        xf = [ps(f"xf{i}", P, 2, S) for i in range(2)]
        a2p = [ps(f"a2p{i}", P, 2, S) for i in range(2)]
        acc = ps("acc", P, 2, S)
        yp = ps("yp", P, 2, S)

        sem = {n: ctx.enter_context(nc.semaphore(n)) for n in PER}
        for n in ("w_vec", "w_rows", "w_gamma", "w_attn", "w_ssm", "w_route", "w_ff", "pow_out", "mask_in",
                  "pool_const", "dve_const", "act_const", "pow_step"):
            sem[n] = ctx.enter_context(nc.semaphore(n))
        block = ctx.enter_context(nc.Block())

        def need(eng, name, b, n):
            value = b * PER[name] + n
            if not (isinstance(value, int) and value == 0):
                eng.wait_ge(sem[name], value + (name in GIVEN))


        def of(ap, b):
            return ap[b] if isinstance(b, int) else ap[bass.ds(b, 1)].squeeze(0)

        def v3(ap, n):
            return ap.rearrange("p (t n) -> p t n", n=n)

        def batches(eng, stage):
            stage(0, None)
            with eng.Fori(1, B) as b:
                stage(b, b - 1)
            stage(None, B - 1)

        @block.sync
        def _(sp):
            for name in GIVEN:
                sp.sem_inc(sem[name], 1)
            sp.dma_start(vec_sb[:], vec).then_inc(sem["w_vec"], 16)
            sp.dma_start(gamma_sb[:], gamma).then_inc(sem["w_gamma"], 16)
            sp.dma_start(wssm_sb[:], wssm).then_inc(sem["w_ssm"], 16)
            sp.dma_start(wdt_sb[:], wdt).then_inc(sem["w_ssm"], 16)
            sp.dma_start(ctx_sb[:], ctxT[0]).then_inc(sem["ctx_in"], 16)
            sp.dma_start(xT_sb[:], xT[0]).then_inc(sem["x_in"], 16)
            sp.dma_start(wattn_sb[:], wattn).then_inc(sem["w_attn"], 16)
            sp.dma_start(rows_sb[:], rows.partition_broadcast(P)).then_inc(sem["w_rows"], 16)
            sp.dma_start(xn_sb[:], x[0]).then_inc(sem["xn_in"], 16)
            sp.wait_ge(sem["pow_step"], 9)
            sp.dma_start(pow_dram, powrow[:].unsqueeze(1).broadcast_to([HEADS, P, 2 * P])).then_inc(sem["pow_out"], 16)
            sp.wait_ge(sem["pow_out"], 16)
            sp.dma_start(dmask[:], bass.AP(tensor=pow_dram.tensor, offset=P - 1,
                                           ap=[[2 * P - 1, P], [2 * P * P, HEADS], [1, P]])).then_inc(sem["mask_in"], 16)
            for t in range(2):
                sp.dma_start(qdec[:, t], bass.AP(tensor=pow_dram.tensor, offset=t * GH * 2 * P * P + P,
                                                 ap=[[2 * P * P, GH], [2 * P, DH], [1, P]])).then_inc(sem["mask_in"], 16)
            sp.dma_start(wroute_sb[:], wroute).then_inc(sem["w_route"], 16)
            sp.dma_start(wff_sb[:], wff).then_inc(sem["w_ff"], 16)

            def spread(b):
                need(sp, "dbl_ready", b, 1)
                sp.dma_start(of(bc_dram, b), dbl[DR:, :]).then_inc(sem["bc_out"], 16)
                need(sp, "bc_out", b, 16)
                for c in range(DS // UN):
                    need(sp, "drive_ready", b, max(2 * c - 2, 0))
                    sp.dma_start(brow[:, c % 2], of(bc_dram, b)[c * UN:(c + 1) * UN].partition_broadcast(P)
                                 ).then_inc(sem[f"b_in{c % 2}"], 16)
                    need(sp, "out_ready", b, max(2 * c - 2, 0))
                    sp.dma_start(crow[:, c % 2], of(bc_dram, b)[DS + c * UN:DS + (c + 1) * UN].partition_broadcast(P)
                                 ).then_inc(sem[f"c_in{c % 2}"], 16)

            def reload(b):
                need(sp, "gen_filled", b - 1, G_IN + 1)
                sp.dma_start(ctx_sb[:], of(ctxT, b)).then_inc(sem["ctx_in"], 16)
                need(sp, "gen_filled", b - 1, G_KN + 1)
                sp.dma_start(xT_sb[:], of(xT, b)).then_inc(sem["x_in"], 16)
                need(sp, "r1_ready", b - 1, 1)
                sp.dma_start(xn_sb[:], of(x, b)).then_inc(sem["xn_in"], 16)

            def store(fb):
                need(sp, "y_ready", fb, 2)
                sp.dma_start(of(out, fb), yo[:]).then_inc(sem["y_out"], 16)

            spread(0)
            reload(1)
            with sp.Fori(1, B - 1) as b:
                spread(b)
                reload(b + 1)
                store(b - 1)
            spread(B - 1)
            store(B - 2)
            store(B - 1)
            need(sp, "y_out", B, 0)

        @block.gpsimd
        def _(pool):
            pc = sem["pool_const"]
            pool.memset(powrow[:], 0.0).then_inc(sem["pow_step"], 1)
            pool.memset(ident[:], 0.0).then_inc(pc, 1)
            pool.memset(headblk[:], 1.0).then_inc(pc, 1)
            pool.memset(mhalf[:], -0.5).then_inc(pc, 1)
            pool.memset(xpad[:], 0.0).then_inc(pc, 1)
            pool.memset(decay[:], 0.0).then_inc(pc, 1)
            pool.wait_ge(pc, 5)
            pool.affine_select(out=ident[:], in_=ident[:], compare_op=ALU.not_equal, fill=1.0, base=0,
                               pattern=[[-1, P]], channel_multiplier=1).then_inc(pc, 1)
            blk = headblk[:].rearrange("p (g r) -> p g r", r=DH)
            pool.affine_select(out=blk, in_=blk, compare_op=ALU.is_ge, fill=0.0, base=0,
                               pattern=[[-DH, GH], [0, DH]], channel_multiplier=1).then_inc(pc, 1)
            pool.memset(spreadw[:], 0.0).then_inc(pc, 1)
            pool.wait_ge(pc, 8)
            pool.affine_select(out=blk, in_=blk, compare_op=ALU.is_ge, fill=0.0, base=DH - 1,
                               pattern=[[DH, GH], [0, DH]], channel_multiplier=-1).then_inc(pc, 1)
            pool.memset(vpad[:], 0.0).then_inc(pc, 1)
            pool.memset(geps[:], 0.0).then_inc(pc, 1)
            for e_ in range(E):
                pool.memset(slots8[:, e_:e_ + 1], float(E - e_)).then_inc(pc, 1)
            for i in range(6):
                view = spreadw[:, i].rearrange("q (e r) -> q e r", r=R)
                step, base = (-1, -(E * (i // 2) + 4 * (i % 2))) if i < 4 else (0, -(2 * E + i - 4))
                pool.affine_select(out=view, in_=view, compare_op=ALU.not_equal, fill=1.0, base=base,
                                   pattern=[[step, 4], [0, R]], channel_multiplier=1).then_inc(pc, 1)
            pool.wait_ge(pc, 17 + E)
            pool.tensor_scalar_mul(headavg[:], headblk[:], 1.0 / DH).then_inc(pc, 1)

            def drive_unit(b, i):
                j, c = i % 2, i // 2
                if i == 0:
                    need(pool, "du_ready", b, 1)
                if j == 0:
                    need(pool, f"b_in{c % 2}", b, 16 * (c // 2 + 1))
                need(pool, "state_ready", b, max(i - 1, 0))
                pool.tensor_tensor(drive[:, i % 2], du[:, j].unsqueeze(1).broadcast_to([P, UN, S]),
                                   brow[:, c % 2], ALU.mult).then_inc(sem["drive_ready"], 1)

            def root(b, src, dst, ready, n, done):
                need(pool, ready, b, n)
                pool.tensor_tensor(dst[:], src[:], mhalf[:], ALU.pow).then_inc(sem[done], 1)

            def stage(b, fb):
                if b is not None:
                    need(pool, "q_ready", b, 6)
                    if isinstance(b, int):
                        pool.wait_ge(sem["mask_in"], 48)
                        pool.wait_ge(sem["w_rows"], 16)
                    need(pool, "av_done", b, 0)
                    pool.tensor_tensor(qd[:], qf[:], qdec[:], ALU.mult).then_inc(sem["qd_ready"], 1)
                    need(pool, "dt_step", b, 4)
                    pool.tensor_tensor(du[:], delta[:], u[:], ALU.mult).then_inc(sem["du_ready"], 1)
                    need(pool, "xn_in", b, 16)
                    pool.tensor_tensor(xb[:], xn_sb[:], bo_row.unsqueeze(1).broadcast_to([P, NT, H]), ALU.add
                                       ).then_inc(sem["xb_ready"], 1)
                    root(b, gvar, grs, "gn_step", 9, "gn_pow")
                if fb is not None:
                    need(pool, "mk_ready", fb, 2)
                    pool.tensor_tensor(mk1T[:], mkT[:, 0], mkT[:, 1], ALU.add).then_inc(sem["mk1_ready"], 1)
                if b is not None:
                    need(pool, "ro_lin", b, 2)
                    need(pool, "gate_ready", b, 1)
                    pool.tensor_tensor(ro[:], rlin[:], gate[:], ALU.mult).then_inc(sem["ro_ready"], 1)
                    root(b, ve, rs, "r1_ready", 7, "r1_pow")
                    drive_unit(b, 0)
                    drive_unit(b, 1)
                for n, (m, k) in enumerate(MAIN):
                    if b is not None:
                        drive_unit(b, n + 2)
                    if fb is not None:
                        need(pool, "q3_ready", fb, n + 1)
                        if n == 0:
                            need(pool, "rw_ready", fb, 1)
                        need(pool, "xs_used", fb, max(n - 3, 0))
                        need(pool, "xsum_ready", fb, MAIN[n - 4][0] + 1 if n >= 4 else 0)
                        pool.tensor_tensor(xs[:, n % 4], fq[:, n % 2], rwT[:, k], ALU.mult).then_inc(sem["xs_ready"], 1)
                        if k == 1:
                            first = MAIN.index((m, 0))
                            need(pool, "xs_ready", fb, n + 1)
                            need(pool, "xsum_used", fb, max(m - 1, 0))
                            pool.tensor_tensor(xsum[:, m % 2], xs[:, first % 4], xs[:, n % 4], ALU.add
                                               ).then_inc(sem["xsum_ready"], 1)
                if fb is not None:
                    root(fb, ve3, rs3, "r3_ready", 7, "r3_pow")
                if b is not None:
                    root(b, ve, rs, "r2_ready", 8, "r2_pow")

            pool.wait_ge(pc, 18 + E)
            batches(pool, stage)

        @block.scalar
        def _(act):
            act.wait_ge(sem["w_vec"], 16)
            act.activation(nega[:], v_("alog").rearrange("p (j n) -> p j n", j=2), ACT.Exp).then_inc(sem["act_const"], 1)
            act.wait_ge(sem["dve_const"], 8)
            act.wait_ge(sem["pool_const"], 18 + E)

            def decays(b, i):
                j, c = i % 2, i // 2
                if i == 0:
                    need(act, "dt_step", b, 4)
                need(act, "state_ready", b, max(i - 1, 0))
                for n in range(UN):
                    s_ = c * UN + n
                    act.activation(decay[:, i % 2, n, 1:], delta[:, j, 1:], ACT.Exp, scale=nega[:, j, s_:s_ + 1]
                                   ).then_inc(sem["decay_ready"], 1)

            def bank(b, i):
                need(act, "gen_filled", b, i + 1)
                return v3(gen[i % 2][:], S)

            def stage(b, fb):
                if b is not None:
                    g = bank(b, G_IN)
                    act.activation(xpad[:, :, DC - 1:], g, ACT.Copy).then_inc(sem["conv_in"], 1)
                    for j in range(2):
                        act.activation(cv[:, j], g[:, j], ACT.Identity, bias=cbh[:, j:j + 1],
                                       scale=cwh[:, j, DC - 1:DC]).then_inc(sem["conv_in"], 1)
                    g = bank(b, G_Q)
                    need(act, "qd_ready", b, 0)
                    for t in range(2):
                        for p_ in range(2):
                            act.activation(qp[:, p_, t], g[:, t], ACT.Identity, bias=bq2[:, p_, t:t + 1],
                                           scale=par[:, p_:p_ + 1]).then_inc(sem["q_ready"], 1)
                    for t in range(2):
                        act.activation(qf[:, t], g[:, t, P:], ACT.Identity, bias=v_("bq")[:, t:t + 1]
                                       ).then_inc(sem["q_ready"], 1)
                    g = bank(b, G_K)
                    for t in range(2):
                        act.activation(kT[:, t], g[:, t], ACT.Identity, bias=v_("bk")[:, t:t + 1]
                                       ).then_inc(sem["k_ready"], 1)
                    need(act, "conv_step", b, 6)
                    act.activation(cth[:], cv[:], ACT.Tanh).then_inc(sem["conv_tanh"], 1)
                    g = bank(b, G_GATE)
                    for t in range(2):
                        act.activation(glin[:, t], g[:, t], ACT.Identity, bias=bgh[:, t:t + 1], scale=0.5
                                       ).then_inc(sem["gate_lin"], 1)
                    need(act, "gate_lin", b, 2)
                    act.activation(gth[:], glin[:], ACT.Tanh).then_inc(sem["gate_tanh"], 1)
                    need(act, "gen_filled", b, G_DBL + 1)
                    need(act, "bc_out", b, 0)
                    act.activation(dbl[:], gen[G_DBL % 2][0:DR + 2 * DS, 0:S], ACT.Copy).then_inc(sem["dbl_ready"], 1)
                    g = bank(b, G_DT)
                    for func, dst in ((ACT.Abs, dt_abs), (ACT.Relu, dt_pos)):
                        for j in range(2):
                            act.activation(dst[:, j], g[:, j], func, bias=v_("dtb")[:, j:j + 1]
                                           ).then_inc(sem["dt_parts"], 1)
                    need(act, "dt_parts", b, 2)
                    act.activation(dt_e[:], dt_abs[:], ACT.Exp, scale=-1.0).then_inc(sem["dt_exp"], 1)
                    need(act, "dt_exp", b, 1)
                    act.activation(dt_ln[:], dt_e[:], ACT.Ln, bias=1.0).then_inc(sem["dt_log"], 1)
                    decays(b, 0)
                    decays(b, 1)
                if fb is not None:
                    need(act, "xf_filled", fb, X_RT + 1)
                    act.activation(rtT[:], xf[XF_BANK[X_RT]][0:2 * E + 2, 0], ACT.Copy).then_inc(sem["rtT_ready"], 1)
                    need(act, "x2_ready", fb, 2)
                    need(act, "r3_ready", fb, 0)
                    act.activation(keep[:], x2[:], ACT.Copy).then_inc(sem["keep_ready"], 1)
                    need(act, "a2_ready", fb, 0)
                    for i in range(2):
                        need(act, "xf_filled", fb, X_MK + i + 1)
                        act.activation(mkT[:, i], xf[XF_BANK[X_MK + i]][:], ACT.Copy).then_inc(sem["mk_ready"], 1)
                    need(act, "xf_filled", fb, X_RW + 1)
                    need(act, "xs_ready", fb, 0)
                    act.activation(rwT[:], xf[XF_BANK[X_RW]][:], ACT.Copy).then_inc(sem["rw_ready"], 1)
                if b is not None:
                    need(act, "gn_step", b, 12)
                    for t in range(2):
                        act.activation(rlin[:, t], acc[:, t], ACT.Identity, bias=gshift[:, t:t + 1],
                                       scale=gscale[:, t:t + 1]).then_inc(sem["ro_lin"], 1)
                    need(act, "x1_ready", b, 2)
                    act.activation(zth[:], x1[:], ACT.Tanh, scale=0.5).then_inc(sem["z_tanh"], 1)
                for n in range(len(MAIN)):
                    if fb is not None:
                        need(act, "xf_filled", fb, X_MAIN + n + 1)
                        need(act, "s_ready", fb, max(n - 1, 0))
                        act.activation(fth[:, n % 2], xf[XF_BANK[X_MAIN + n]][:, 0], ACT.Tanh, scale=0.5
                                       ).then_inc(sem["th_ready"], 1)
                    if b is not None:
                        decays(b, n + 2)
                if b is not None:
                    g = bank(b, G_X2)
                    act.activation(x2T[:], g, ACT.Copy).then_inc(sem["x2T_ready"], 1)
                    need(act, "rt_step", b, 2)
                    act.activation(le[:], lg[:], ACT.Exp).then_inc(sem["lg_exp"], 1)

            batches(act, stage)

        @block.tensor
        def _(pe):
            def mm(o, l, r, **kw):
                return pe.matmul(o, l, r, skip_group_check=True, **kw)

            def gen_free(b, i):
                if i >= 2:
                    name, n = GEN[i - 2]
                    need(pe, name, b, n)
                else:
                    last = max(k for k in range(len(GEN)) if k % 2 == i % 2)
                    need(pe, GEN[last][0], b, 0)

            def xf_free(fb, i):
                before = [k for k in range(i) if XF_BANK[k] == XF_BANK[i]]
                if before:
                    name, n = XF[before[-1]]
                    need(pe, name, fb, n)
                else:
                    need(pe, "q3_ready", fb, 0)

            def project(b, i, w, src):
                gen_free(b, i)
                g = v3(gen[i % 2][:], S)
                for t in range(2):
                    for k in range(2):
                        last = mm(g[:, t], w[:, k, t * P:(t + 1) * P], src[:, k], start=(k == 0), stop=(k == 1))
                last.then_inc(sem["gen_filled"], 1)

            def outputs(b, i):
                j, c = i % 2, i // 2
                need(pe, "out_ready", b, i + 1)
                if i == 0:
                    need(pe, "yT_ready", b, 0)
                for n in range(UN):
                    s_ = c * UN + n
                    last = mm(yp[:, j], ident[:], state[:, i % 2, n], start=(i == 0 and n == 0), stop=(s_ == DS - 1))
                last.then_inc(sem["y_part"], 1)

            def hidden(fb, n):
                m, k = MAIN[n]
                xf_free(fb, X_MAIN + n)
                if n == 0:
                    need(pe, "am_ready", fb, 4)
                o = xf[XF_BANK[X_MAIN + n]]
                fs_ = slice(m * P, (m + 1) * P)
                for half, (W, B_) in enumerate(((W1, B1), (W3, B3))):
                    terms = [(B_[:, t, fs_], am[:, 2 * half + k, t]) for t in range(2)]
                    if k == 0:
                        terms = [(W[:, t, fs_], x2T[:, t]) for t in range(2)] + terms
                    for i, (l, r) in enumerate(terms):
                        last = mm(o[:, half], l, r, start=(k == 0 and half == 0 and i == 0), stop=(i == len(terms) - 1))
                last.then_inc(sem["xf_filled"], 1)

            def shrink(fb, n):
                m, k = MAIN[n]
                need(pe, "xs_ready", fb, n + 1)
                if n == 0:
                    need(pe, "a2_ready", fb, 0)
                for t in range(2):
                    last = mm(a2p[k][:, t], A2[:, m, t * P:(t + 1) * P], xs[:, n % 4], start=(m == 0 and t == 0),
                              stop=(m == FM - 1))
                last.then_inc(sem["xs_used"], 1)
                if k == 1:
                    need(pe, "xsum_ready", fb, m + 1)
                    for t in range(NT):
                        last = mm(acc[:, t], xsum[:, m % 2, t * P:(t + 1) * P], W2[:, m], start=(m == 0 and t == 0),
                                  stop=False)
                    last.then_inc(sem["xsum_used"], 1)

            def spread_rows(fb, i):
                xf_free(fb, i)
                for t in range(2):
                    last = mm(xf[XF_BANK[i]][:, t], spreadw[:, 2 * (i - X_MK) + t], rtT[:], start=True, stop=True)
                last.then_inc(sem["xf_filled"], 1)

            def stage(b, fb):
                if b is not None:
                    if isinstance(b, int):
                        pe.wait_ge(sem["w_ssm"], 32)
                    need(pe, "ctx_in", b, 16)
                    gen_free(b, G_IN)
                    g = v3(gen[G_IN % 2][:], S)
                    for j in range(2):
                        last = mm(g[:, j], w_in[:, j * P:(j + 1) * P], ctx_sb[:], start=True, stop=True)
                    last.then_inc(sem["gen_filled"], 1)
                    if isinstance(b, int):
                        pe.wait_ge(sem["w_attn"], 16)
                    need(pe, "x_in", b, 16)
                    project(b, G_Q, wq, xT_sb)
                    project(b, G_K, wk, xT_sb)
                    project(b, G_GATE, wg, xT_sb)
                    gen_free(b, G_DBL)
                    need(pe, "u_ready", b, 1)
                    for j in range(2):
                        last = mm(gen[G_DBL % 2][0:DR + 2 * DS, 0:S], w_xp[:, j], u[:, j], start=(j == 0), stop=(j == 1))
                    last.then_inc(sem["gen_filled"], 1)
                    gen_free(b, G_V)
                    g = v3(gen[G_V % 2][:], H)
                    for t in range(NT):
                        for k in range(2):
                            last = mm(g[:, t], xT_sb[:, k, t * P:(t + 1) * P], wv[:, k], start=(k == 0), stop=(k == 1))
                    last.then_inc(sem["gen_filled"], 1)
                    gen_free(b, G_DT)
                    need(pe, "dbl_ready", b, 1)
                    g = v3(gen[G_DT % 2][:], S)
                    for j in range(2):
                        last = mm(g[:, j], wdt_sb[:, j * P:(j + 1) * P], dbl[0:DR, :], start=True, stop=True)
                    last.then_inc(sem["gen_filled"], 1)
                    gen_free(b, G_KN)
                    for k in range(2):
                        last = mm(gen[G_KN % 2][:, 0:H], xT_sb[:, k, 0:P], wk[:, k], start=(k == 0), stop=(k == 1))
                    last.then_inc(sem["gen_filled"], 1)
                    gen_free(b, G_KV)
                    need(pe, "kd_ready", b, 2)
                    need(pe, "v_ready", b, 4)
                    g = v3(gen[G_KV % 2][:], P)
                    for t in range(2):
                        for p_ in range(2):
                            last = mm(g[:, t], kd[:, t * P:(t + 1) * P], vpad[:, 0, p_, t * P:(t + 1) * P],
                                      start=(p_ == 0), stop=(p_ == 1))
                    last.then_inc(sem["gen_filled"], 1)

                    def scores(i):
                        t, w = i // 4, i % 4
                        gen_free(b, G_SC + i)
                        if i == 0:
                            need(pe, "q_ready", b, 6)
                            need(pe, "k_ready", b, 2)
                        g = gen[(G_SC + i) % 2][:].rearrange("p (a c i) -> p a c i", a=2, c=2)
                        rows_ = slice(32 * w, 32 * w + 32)
                        for p_ in range(2):
                            for c in range(2):
                                cs = slice(c * P, (c + 1) * P)
                                last = mm(g[:, p_, c], kT[rows_, t, cs], qp[rows_, p_, t, cs], start=True, stop=True)
                        last.then_inc(sem["gen_filled"], 1)

                    def values(i):
                        t, w = i // 4, i % 4
                        need(pe, "sc_ready", b, i + 1)
                        if i == 0 and fb is not None:
                            need(pe, "r3_ready", fb, 0)
                        rows_ = slice(32 * w, 32 * w + 32)
                        for p_ in range(2):
                            for c in range(2):
                                last = mm(acc[rows_, t, c * P:(c + 1) * P], vpad[:, c, p_, i * 32:(i + 1) * 32],
                                          sc[:, i % 2, p_, c], start=(t == 0 and p_ == 0 and c == 0),
                                          stop=(w == 3 and p_ == 1 and c == 0))
                        if w == 3:
                            if i == 3:
                                need(pe, "kv_ready", b, 1)
                                need(pe, "qd_ready", b, 1)
                            last = mm(acc[:, t, P:], kv[:, t], qd[:, t], start=False, stop=True)
                        last.then_inc(sem["av_done"], 1)

                    scores(0)
                    for i in range(1, 8):
                        scores(i)
                        values(i - 1)
                    values(7)
                    gen_free(b, G_MEAN)
                    need(pe, "gn_step", b, 5)
                    mm(gen[G_MEAN % 2][:, 0:4], headavg[:], gmv[:].rearrange("p t s -> p (t s)"), start=True, stop=True
                       ).then_inc(sem["gen_filled"], 1)
                if fb is not None:
                    xf_free(fb, X_RT)
                    need(pe, "rt_step", fb, 21)
                    for n in range(NT):
                        last = mm(xf[XF_BANK[X_RT]][0:2 * E + 2, 0, n * P:(n + 1) * P], rt[:, n], ident[:], start=True, stop=True)
                    last.then_inc(sem["xf_filled"], 1)
                    need(pe, "rtT_ready", fb, 1)
                    for i in (X_MK, X_MD):
                        spread_rows(fb, i)
                if b is not None:
                    gen_free(b, G_VAR)
                    need(pe, "gn_step", b, 8)
                    mm(gen[G_VAR % 2][:, 0:2], headavg[:], gsq[:], start=True, stop=True).then_inc(sem["gen_filled"], 1)
                if fb is not None:
                    spread_rows(fb, X_RW)
                    need(pe, "x2T_ready", fb, 1)
                    pe.wait_ge(sem["w_ff"], 16)
                    for i, w in ((X_A1, A1), (X_A3, A3)):
                        xf_free(fb, i)
                        for t in range(2):
                            for k in range(2):
                                last = mm(xf[XF_BANK[i]][:, t], w[:, k, t * P:(t + 1) * P], x2T[:, k], start=(k == 0),
                                          stop=(k == 1))
                        last.then_inc(sem["xf_filled"], 1)
                for n in range(len(MAIN)):
                    if fb is not None:
                        hidden(fb, n)
                    if b is not None and n == 1:
                        gen_free(b, G_OUT)
                        need(pe, "ro_ready", b, 1)
                        g = v3(gen[G_OUT % 2][:], H)
                        for t in range(NT):
                            for k in range(2):
                                last = mm(g[:, t], ro[:, k, t * P:(t + 1) * P], wo[:, k], start=(k == 0), stop=(k == 1))
                        last.then_inc(sem["gen_filled"], 1)
                    if fb is not None and n >= LAG:
                        shrink(fb, n - LAG)
                    if b is not None and n >= 1:
                        outputs(b, n - 1)
                if b is not None:
                    for i in range(len(MAIN) - 1, UNITS):
                        outputs(b, i)
                if fb is not None:
                    for n in range(len(MAIN) - LAG, len(MAIN)):
                        shrink(fb, n)
                    need(pe, "a2_ready", fb, 3)
                    for t in range(NT):
                        for k in range(2):
                            last = mm(acc[:, t], a2m[:, 0, k, t * P:(t + 1) * P], B2[:, k], start=False, stop=(k == 1))
                    last.then_inc(sem["down_done"], 1)
                if b is not None:
                    gen_free(b, G_Y)
                    need(pe, "yT_ready", b, 3)
                    g = v3(gen[G_Y % 2][:], H)
                    for t in range(NT):
                        for j in range(2):
                            last = pe.transpose(g[:, t, j * P:(j + 1) * P], yT[:, j, t * P:(t + 1) * P], ident[:])
                    last.then_inc(sem["gen_filled"], 1)
                    gen_free(b, G_X2)
                    need(pe, "x2_ready", b, 2)
                    g = v3(gen[G_X2 % 2][:], S)
                    for t in range(NT):
                        for k in range(2):
                            last = pe.transpose(g[:, k, t * P:(t + 1) * P], x2[:, t, k * P:(k + 1) * P], ident[:])
                    last.then_inc(sem["gen_filled"], 1)
                    gen_free(b, G_LG)
                    need(pe, "x2T_ready", b, 1)
                    if isinstance(b, int):
                        pe.wait_ge(sem["w_route"], 16)
                    for t in range(NT):
                        for k in range(2):
                            last = mm(gen[G_LG % 2][:, t * E:(t + 1) * E], x2T[:, k, t * P:(t + 1) * P], wroute_sb[:, k],
                                      start=(k == 0), stop=(k == 1))
                    last.then_inc(sem["gen_filled"], 1)

            pe.wait_ge(sem["pool_const"], 18 + E)
            batches(pe, stage)

        @block.vector
        def _(dve):
            dc = sem["dve_const"]
            dve.wait_ge(sem["w_gamma"], 16)
            dve.wait_ge(sem["pow_step"], 1)
            one = P - 1
            dve.memset(powrow[:, one:one + 1], 1.0)
            dve.tensor_copy(powrow[:, one + 1:one + 2], gamma_sb[:]).then_inc(sem["pow_step"], 1)
            known = 1
            while known < P:
                dve.wait_ge(sem["pow_step"], 2 + known.bit_length() - 1)
                dve.tensor_scalar(powrow[:, one + 1 + known:one + 1 + 2 * known], powrow[:, one + 1:one + 1 + known],
                                  powrow[:, one + known:one + known + 1], None, ALU.mult).then_inc(sem["pow_step"], 1)
                known *= 2
            dve.wait_ge(sem["w_vec"], 16)
            dve.wait_ge(sem["pool_const"], 18 + E)
            dve.tensor_reduce(par[:, 0:1], headblk[:, 0:P:2 * DH], AX.X, ALU.add).then_inc(dc, 1)
            dve.wait_ge(dc, 1)
            dve.tensor_scalar(par[:, 1:2], par[:, 0:1], -1.0, 1.0, ALU.mult, ALU.add).then_inc(dc, 1)
            dve.wait_ge(dc, 2)
            for p_ in range(2):
                dve.tensor_scalar(bq2[:, p_], v_("bq"), par[:, p_:p_ + 1], None, ALU.mult).then_inc(dc, 1)
            dve.tensor_scalar(bgh[:], v_("bg"), 0.5, None, ALU.mult).then_inc(dc, 1)
            dve.tensor_scalar(cwh[:].rearrange("p j k -> p (j k)"), v_("cw"), 0.5, None, ALU.mult).then_inc(dc, 1)
            dve.tensor_scalar(cbh[:], v_("cb"), 0.5, None, ALU.mult).then_inc(dc, 1)
            dve.wait_ge(sem["act_const"], 1)
            dve.tensor_scalar(nega[:], nega[:], -1.0, None, ALU.mult).then_inc(dc, 1)
            dve.wait_ge(dc, 8)

            def bank(b, i, n):
                need(dve, "gen_filled", b, i + 1)
                return v3(gen[i % 2][:], n)

            def scan_unit(b, i):
                j, c = i % 2, i // 2
                flat = lambda ap: ap.rearrange("p n t -> p (n t)")
                need(dve, "decay_ready", b, UN * (i + 1))
                need(dve, "drive_ready", b, i + 1)
                need(dve, "y_part", b, max(i - 1, 0))
                dve.tensor_tensor_scan(flat(state[:, i % 2]), flat(decay[:, i % 2]), flat(drive[:, i % 2]), 0.0,
                                       ALU.mult, ALU.add).then_inc(sem["state_ready"], 1)
                if j == 0:
                    need(dve, f"c_in{c % 2}", b, 16 * (c // 2 + 1))
                need(dve, "state_ready", b, i + 1)
                dve.tensor_tensor(state[:, i % 2], state[:, i % 2], crow[:, c % 2], ALU.mult
                                  ).then_inc(sem["out_ready"], 1)

            def layernorm(b, src, st_, mv_, ve_, rs_, dst, ready, n, pow_, done):
                need(dve, ready, b, n)
                for t in range(NT):
                    dve.bn_stats(st_[:, t], src[:, t]).then_inc(sem[ready], 1)
                need(dve, ready, b, n + 2)
                dve.memset(ve_[:], EPS).then_inc(sem[ready], 1)
                for t in range(NT):
                    dve.bn_aggr(mv_[:, t], st_[:, t]).then_inc(sem[ready], 1)
                need(dve, ready, b, n + 5)
                dve.tensor_tensor(ve_[:], mv_[:, :, 1], ve_[:], ALU.add).then_inc(sem[ready], 1)
                need(dve, pow_, b, 1)
                for t in range(NT):
                    dve.tensor_scalar(dst[:, t], src[:, t], mv_[:, t, 0:1], rs_[:, t:t + 1], ALU.subtract, ALU.mult
                                      ).then_inc(sem[done], 1)

            def stage(b, fb):
                if b is not None:
                    need(dve, "conv_in", b, 3)
                    for k in range(DC - 1):
                        for j in range(2):
                            i = 2 * k + j
                            if i >= 2:
                                need(dve, "conv_step", b, i - 1)
                            dve.scalar_tensor_tensor(cv[:, j], xpad[:, j, k:k + S], cwh[:, j, k:k + 1], cv[:, j],
                                                     ALU.mult, ALU.add).then_inc(sem["conv_step"], 1)
                    need(dve, "conv_tanh", b, 1)
                    dve.scalar_tensor_tensor(u[:], cth[:], 1.0, cv[:], ALU.add, ALU.mult).then_inc(sem["u_ready"], 1)
                    need(dve, "gate_tanh", b, 1)
                    dve.scalar_tensor_tensor(gate[:], gth[:], 1.0, glin[:], ALU.add, ALU.mult).then_inc(sem["gate_ready"], 1)
                    if isinstance(b, int):
                        dve.wait_ge(sem["w_rows"], 16)
                        dve.wait_ge(sem["mask_in"], 48)
                    g = bank(b, G_V, H)
                    pairs = lambda ap: ap.rearrange("p (w a d) -> p w a d", a=2, d=DH)
                    for t in range(NT):
                        for p_ in range(2):
                            dve.tensor_tensor(pairs(vpad[:, t, p_])[:, :, p_], pairs(g[:, t])[:, :, p_],
                                              pairs(bv_row)[:, :, p_], ALU.add).then_inc(sem["v_ready"], 1)
                    need(dve, "dt_exp", b, 1)
                    dve.tensor_scalar(dt_w[:], dt_e[:], 1.0, -1.0, ALU.add, ALU.add).then_inc(sem["dt_step"], 1)
                    need(dve, "dt_step", b, 1)
                    dve.tensor_tensor(dt_w[:], dt_e[:], dt_w[:], ALU.subtract).then_inc(sem["dt_step"], 1)
                    need(dve, "dt_step", b, 2)
                    need(dve, "dt_log", b, 1)
                    dve.tensor_tensor(dt_w[:], dt_w[:], dt_ln[:], ALU.add).then_inc(sem["dt_step"], 1)
                    need(dve, "dt_step", b, 3)
                    dve.tensor_tensor(delta[:], dt_w[:], dt_pos[:], ALU.add).then_inc(sem["dt_step"], 1)
                    g = bank(b, G_KN, H)
                    dve.tensor_tensor(kd[:], g[:, 0], bk_row, ALU.add).then_inc(sem["kd_ready"], 1)
                    need(dve, "kd_ready", b, 1)
                    kdh = kd[:].rearrange("p (h d) -> p h d", d=DH)
                    dve.tensor_tensor(kdh, kdh, dmask[:, :, P - 1:P].broadcast_to([P, HEADS, DH]), ALU.mult
                                      ).then_inc(sem["kd_ready"], 1)
                    need(dve, "gen_filled", b, G_KV + 1)
                    dve.tensor_tensor(kv[:], v3(gen[G_KV % 2][:, 0:2 * P], P), headblk[:].unsqueeze(1).broadcast_to([P, 2, P]),
                                      ALU.mult).then_inc(sem["kv_ready"], 1)
                    for i in range(8):
                        need(dve, "gen_filled", b, G_SC + i + 1)
                        need(dve, "av_done", b, max(i - 1, 0))
                        dve.tensor_tensor(sc[:, i % 2], gen[(G_SC + i) % 2][:].rearrange("p (a c i) -> p a c i", a=2, c=2),
                                          dmask[:, 2 * i:2 * i + 2].unsqueeze(2).broadcast_to([P, 2, 2, P]), ALU.mult
                                          ).then_inc(sem["sc_ready"], 1)
                    need(dve, "av_done", b, 8)
                    for t in range(2):
                        dve.bn_stats(gst[:, t], acc[:, t]).then_inc(sem["gn_step"], 1)
                    need(dve, "gn_step", b, 2)
                    dve.memset(geps[:, :, 1], EPS).then_inc(sem["gn_step"], 1)
                    for t in range(2):
                        dve.bn_aggr(gmv[:, t], gst[:, t]).then_inc(sem["gn_step"], 1)
                    need(dve, "gen_filled", b, G_MEAN + 1)
                    dve.tensor_tensor(gavg[:], gen[G_MEAN % 2][:, 0:4].rearrange("p (t s) -> p t s", t=2), geps[:], ALU.add).then_inc(sem["gn_step"], 1)
                    need(dve, "gn_step", b, 6)
                    dve.tensor_tensor(gdev[:], gmv[:, :, 0], gavg[:, :, 0], ALU.subtract).then_inc(sem["gn_step"], 1)
                    need(dve, "gn_step", b, 7)
                    dve.tensor_tensor(gsq[:], gdev[:], gdev[:], ALU.mult).then_inc(sem["gn_step"], 1)
                    need(dve, "gen_filled", b, G_VAR + 1)
                    dve.tensor_tensor(gvar[:], gen[G_VAR % 2][:, 0:2], gavg[:, :, 1], ALU.add).then_inc(sem["gn_step"], 1)
                if fb is not None:
                    for half, i in enumerate((X_A1, X_A3)):
                        need(dve, "xf_filled", fb, i + 1)
                        need(dve, "mk_ready", fb, 2)
                        for k in range(2):
                            dve.tensor_tensor(am[:, 2 * half + k], xf[XF_BANK[i]][:], mkT[:, k], ALU.mult
                                              ).then_inc(sem["am_ready"], 1)
                if b is not None:
                    need(dve, "gn_pow", b, 1)
                    dve.tensor_tensor(gscale[:], grs[:], v_("gnw"), ALU.mult).then_inc(sem["gn_step"], 1)
                    need(dve, "gn_step", b, 10)
                    dve.tensor_tensor(gms[:], gscale[:], gavg[:, :, 0], ALU.mult).then_inc(sem["gn_step"], 1)
                    need(dve, "gn_step", b, 11)
                    dve.tensor_tensor(gshift[:], v_("gnb"), gms[:], ALU.subtract).then_inc(sem["gn_step"], 1)
                    g = bank(b, G_OUT, H)
                    need(dve, "xb_ready", b, 1)
                    dve.tensor_tensor(r1[:], g, xb[:], ALU.add).then_inc(sem["r1_ready"], 1)
                    layernorm(b, r1, st, mv, ve, rs, x1, "r1_ready", 1, "r1_pow", "x1_ready")
                    need(dve, "z_tanh", b, 1)
                    dve.scalar_tensor_tensor(zs[:], zth[:], 1.0, x1[:], ALU.add, ALU.mult).then_inc(sem["r2_ready"], 1)
                for n in range(len(MAIN)):
                    if b is not None:
                        scan_unit(b, n)
                    if fb is not None:
                        o = xf[XF_BANK[X_MAIN + n]]
                        need(dve, "th_ready", fb, n + 1)
                        dve.scalar_tensor_tensor(fs[:, n % 2], fth[:, n % 2], 1.0, o[:, 0], ALU.add, ALU.mult
                                                 ).then_inc(sem["s_ready"], 1)
                        need(dve, "s_ready", fb, n + 1)
                        need(dve, "xs_ready", fb, max(n - 1, 0))
                        dve.tensor_tensor(fq[:, n % 2], fs[:, n % 2], o[:, 1], ALU.mult).then_inc(sem["q3_ready"], 1)
                if b is not None:
                    for i in range(len(MAIN), UNITS):
                        scan_unit(b, i)
                if fb is not None:
                    need(dve, "xs_used", fb, 14)
                    need(dve, "mk1_ready", fb, 1)
                    dve.tensor_tensor(a2m[:, 0], a2p[0][:], mkT[:, 0], ALU.mult).then_inc(sem["a2_ready"], 1)
                    dve.tensor_tensor(a2m[:, 1], a2p[1][:], mk1T[:], ALU.mult).then_inc(sem["a2_ready"], 1)
                    need(dve, "a2_ready", fb, 2)
                    dve.tensor_tensor(a2m[:, 0], a2m[:, 0], a2m[:, 1], ALU.add).then_inc(sem["a2_ready"], 1)
                if b is not None:
                    need(dve, "y_part", b, UNITS)
                    for j in range(2):
                        dve.scalar_tensor_tensor(yT[:, j], u[:, j], v_("D")[:, j:j + 1], yp[:, j], ALU.mult, ALU.add
                                                 ).then_inc(sem["yT_ready"], 1)
                    need(dve, "yT_ready", b, 2)
                    dve.scalar_tensor_tensor(yT[:], zs[:], 0.5, yT[:], ALU.mult, ALU.mult).then_inc(sem["yT_ready"], 1)
                if fb is not None:
                    need(dve, "down_done", fb, 1)
                    need(dve, "keep_ready", fb, 1)
                    dve.tensor_tensor(r3[:], acc[:], keep[:], ALU.add).then_inc(sem["r3_ready"], 1)
                    need(dve, "y_out", fb, 0)
                    layernorm(fb, r3, st3, mv3, ve3, rs3, yo, "r3_ready", 1, "r3_pow", "y_ready")
                if b is not None:
                    g = bank(b, G_Y, H)
                    dve.tensor_tensor(r2[:], g, x1[:], ALU.add).then_inc(sem["r2_ready"], 1)
                    need(dve, "keep_ready", b, 0)
                    layernorm(b, r2, st, mv, ve, rs, x2, "r2_ready", 2, "r2_pow", "x2_ready")
                    route(b)

            def route(b):
                step = [0]

                def did(ins):
                    step[0] += 1
                    ins.then_inc(sem["rt_step"], 1)
                    need(dve, "rt_step", b, step[0])

                wide = lambda ap: ap.unsqueeze(2).broadcast_to([P, NT, E])
                need(dve, "gen_filled", b, G_LG + 1)
                dve.tensor_copy(lg[:], gen[G_LG % 2][:, 0:NT * E].rearrange("p (t e) -> p t e", t=NT)).then_inc(sem["lg_ready"], 1)
                need(dve, "lg_ready", b, 1)
                did(dve.tensor_reduce(t1[:], lg[:], AX.X, ALU.max))
                did(dve.tensor_tensor(lg[:], lg[:], wide(t1[:]), ALU.subtract))
                need(dve, "lg_exp", b, 1)
                did(dve.tensor_reduce(t1[:], le[:], AX.X, ALU.add))
                did(dve.reciprocal(t2[:], t1[:]))
                did(dve.tensor_tensor(pr[:], le[:], wide(t2[:]), ALU.mult))
                for k in range(2):
                    did(dve.tensor_reduce(top[:, :, k], pr[:], AX.X, ALU.max))
                    did(dve.tensor_tensor(eq[:], pr[:], wide(top[:, :, k]), ALU.is_equal))
                    did(dve.tensor_tensor(eq[:], eq[:], slots8[:].unsqueeze(1).broadcast_to([P, NT, E]), ALU.mult))
                    did(dve.tensor_reduce(t1[:], eq[:], AX.X, ALU.max))
                    did(dve.tensor_tensor((mk0, mk1[:])[k], eq[:], wide(t1[:]), ALU.is_equal))
                    if k == 0:
                        did(dve.scalar_tensor_tensor(pr[:], mk0, -4.0, pr[:], ALU.mult, ALU.add))
                did(dve.tensor_tensor(md, mk1[:], mk0, ALU.subtract))
                did(dve.tensor_tensor(t1[:], top[:, :, 0], top[:, :, 1], ALU.add))
                did(dve.reciprocal(t2[:], t1[:]))
                for k in range(2):
                    did(dve.scalar_tensor_tensor(rw[:, :, k], top[:, :, k], 0.5, t2[:], ALU.mult, ALU.mult))

            batches(dve, stage)


def kernel(**inputs):
    import numpy as np
    import concourse.bacc as bacc
    from concourse import mybir
    from concourse.bass_utils import run_bass_kernel_spmd

    a = {k: np.asarray(v) for k, v in inputs.items()}
    g = lambda n: a["L0_" + n]

    def cols(m):
        m = m.reshape(m.shape[0], -1)
        return m.reshape(-1, P, m.shape[1]).transpose(1, 0, 2).reshape(P, -1)

    flatT = lambda m: m.reshape(-1, m.shape[-1]).T
    vecs = np.concatenate([cols(g(n)) for n in ("attn_bq", "attn_bk", "attn_bg", "attn_gn_w", "attn_gn_b", "xattn_conv_w",
                                                "xattn_conv_b", "xattn_dt_proj_b", "xattn_D", "xattn_A_log")], axis=1)
    rows = np.stack([g("attn_bv"), g("attn_bk"), g("attn_bo")])
    wattn = np.concatenate([cols(g(n)) for n in ("attn_wq", "attn_wk", "attn_wv", "attn_wg", "attn_wo")], axis=1)
    wssm = np.concatenate([flatT(g("xattn_in_proj_w")), cols(flatT(g("xattn_x_proj_w")))], axis=1)
    lora = lambda m: m.transpose(0, 2, 1).reshape(E * R, -1)
    wff = np.concatenate([cols(m) for m in (
        flatT(g("ffn_A1")), flatT(g("ffn_A3")), flatT(g("ffn_W1")), flatT(g("ffn_W3")), lora(g("ffn_B1")), lora(g("ffn_B3")),
        flatT(g("ffn_A2")), flatT(g("ffn_W2")), lora(g("ffn_B2")))], axis=1)
    x = a["x"]
    arrays = {
        "x": x.reshape(B, NT, P, H).transpose(0, 2, 1, 3),
        "xT": x.transpose(0, 2, 1).reshape(B, 2, P, S).transpose(0, 2, 1, 3),
        "ctxT": a["ctx_1024"].transpose(0, 2, 1),
        "vec": vecs, "rows": rows, "gamma": g("attn_gamma").reshape(HEADS, 1), "wattn": wattn, "wssm": wssm,
        "wdt": flatT(g("xattn_dt_proj_w")), "wroute": cols(flatT(g("ffn_Wg"))), "wff": wff,
    }
    arrays = {"in_" + k: np.ascontiguousarray(v) for k, v in arrays.items()}
    nc = bacc.Bacc("TRN2", target_bir_lowering=False, num_devices=1)
    args = [nc.dram_tensor(k, v.shape, mybir.dt.from_np(v.dtype), kind="ExternalInput").ap() for k, v in arrays.items()]
    out = nc.dram_tensor("out_y", (B, P, NT, H), mybir.dt.float32, kind="ExternalOutput").ap()
    decoder_layer(nc, *args, out)
    got = run_bass_kernel_spmd(nc, [arrays], core_ids=[0]).results[0]["out_y"]
    return got.transpose(0, 2, 1, 3).reshape(B, S, H)
```

```python
import concourse.bass as bass
from concourse import mybir
from contextlib import ExitStack

B, S, H = 4, 256, 256
P = 128
NT, NH2 = S // P, H // P
HEADS, DH = 16, 16
GH = P // DH
DI, DS, DR, DC = 256, 16, 8, 4
E, R, F = 8, 32, 896
FM = F // P
EPS = 1e-5
UN = 2
UNITS = 2 * DS // UN
CONSTS = 18 + E

VEC = {}
_at = 0
for _n, _w in (("bq", 2), ("bk", 2), ("bg", 2), ("gnw", 2), ("gnb", 2), ("cw", 2 * DC), ("cb", 2),
               ("dtb", 2), ("D", 2), ("alog", 2 * DS)):
    VEC[_n] = (_at, _at + _w)
    _at += _w
NVEC = _at
FFW = {}
_at = 0
for _n, _w in (("A1", 2 * 256), ("A3", 2 * 256), ("W1", 2 * F), ("W3", 2 * F), ("B1", 2 * F), ("B3", 2 * F),
               ("A2", FM * 256), ("W2", FM * H), ("B2", 2 * H)):
    FFW[_n] = (_at, _at + _w)
    _at += _w
NFFW = _at
FF_PIECES = [(), ("A1", "A3"), ("W1",), ("W3",), ("B1",), ("B3",), ("A2",), ("W2", "B2")]

PER = dict(
    x_in=16, xn_in=16, ctx_in=16, bc_out=16, b_in0=64, b_in1=64, c_in0=64, c_in1=64, y_out=16,
    gen_filled=21,
    conv_in=3, conv_step=6, conv_tanh=1, u_ready=1, dbl_ready=1, dt_parts=4, dt_exp=1, dt_log=1, dt_step=4,
    du_ready=1, decay_ready=2 * DS, drive_ready=UNITS, state_ready=UNITS, out_ready=UNITS, part_ready=UNITS,
    y_init=2, y_part=UNITS, yT_ready=1,
    q_ready=2, qm_ready=4, qd_ready=1, k_ready=2, gate_lin=2, gate_tanh=1, gate_ready=1, v_ready=4, kd_ready=2,
    kv_ready=1, sc_ready=8, av_done=8, gn_step=12, gn_pow=1, ro_lin=2, ro_ready=1, xb_ready=1,
    r1_ready=7, r1_pow=1, x1_ready=2, z_tanh=1, r2_ready=8, r2_pow=1, x2_ready=2, x2T_ready=1,
    lg_ready=1, lg_exp=1, rt_step=21,
    xf_filled=20, a_filled=2, rtT_ready=1, mk_ready=2, rw_ready=1, keep_ready=1, mk1_ready=1, am_ready=4,
    th_ready=14, s_ready=14, q3_ready=14, xs_ready=14, xsum_ready=7, xs_used=14, xsum_used=7,
    a2_ready=3, down_done=1, r3_ready=7, r3_pow=1, y_ready=2,
)
GIVEN = ("xs_used", "xsum_used", "xsum_ready", "r3_ready", "a2_ready", "xs_ready", "s_ready", "q3_ready", "y_out")
GEN = [("conv_in", 3), ("q_ready", 2), ("k_ready", 2), ("v_ready", 4), ("dbl_ready", 1), ("kd_ready", 1),
       ("gate_lin", 2), ("dt_parts", 4), ("kv_ready", 1)] + [("sc_ready", i + 1) for i in range(8)] + [
       ("gn_step", 6), ("gn_step", 9), ("r1_ready", 1), ("r2_ready", 2)]
(G_IN, G_Q, G_K, G_V, G_DBL, G_KN, G_GATE, G_DT, G_KV, G_SC) = range(10)
(G_MEAN, G_VAR, G_OUT, G_Y) = range(G_SC + 8, G_SC + 12)
MAIN = [(0, 0), (1, 0), (0, 1), (1, 1), (2, 0), (3, 0), (2, 1), (3, 1), (4, 0), (5, 0), (4, 1), (5, 1), (6, 0), (6, 1)]
XF = [("x2T_ready", 1), ("lg_ready", 1), ("rtT_ready", 1), ("mk_ready", 1), ("mk_ready", 2), ("rw_ready", 1)] + [("q3_ready", n + 1) for n in range(len(MAIN))]
X_X2, X_LG, X_RT, X_MK, X_MD, X_RW, X_MAIN = range(7)
XF_BANK = [1, 0, 1, 0, 1, 0] + [(m + 1) % 2 for m, _ in MAIN]
SCANS = [[0], [1], [2], [3, 4], [5], [6], [7], [8, 9], [10], [11, 12], [13, 14], [15], [], []]
LAG = 2


def decoder_layer(nc, x, xT, ctxT, vec, rows, gamma, wattn, wssm, wdt, wroute, wff, out):
    f32 = mybir.dt.float32
    ALU = mybir.AluOpType
    ACT = mybir.ActivationFunctionType
    AX = mybir.AxisListType

    with ExitStack() as ctx:
        def sb(name, *shape):
            return ctx.enter_context(nc.sbuf_tensor(name, list(shape), f32))

        def ps(name, *shape):
            return ctx.enter_context(nc.psum_tensor(name, list(shape), f32))

        pow_dram = nc.dram_tensor("pow_dram", (HEADS, P, 2 * P), f32, kind="Internal").ap()
        bc_dram = nc.dram_tensor("bc_dram", (B, 2 * DS, S), f32, kind="Internal").ap()

        vec_sb = sb("vec_sb", P, NVEC)
        rows_sb = sb("rows_sb", P, 3, H)
        bv_row, bk_row, bo_row = (rows_sb[:, i, :] for i in range(3))
        wattn_sb = sb("wattn_sb", P, 5, 2, H)
        wq, wk, wv, wg, wo = (wattn_sb[:, i] for i in range(5))
        wssm_sb = sb("wssm_sb", P, DI + 2 * (DR + 2 * DS))
        w_in = wssm_sb[:, 0:DI]
        w_xp = wssm_sb[:, DI:].rearrange("p (j r) -> p j r", j=2)
        wdt_sb = sb("wdt_sb", DR, DI)
        wroute_sb = sb("wroute_sb", P, 2, E)
        wff_sb = sb("wff_sb", P, NFFW)

        def ffw(name, t):
            a, b_ = FFW[name]
            return wff_sb[:, a:b_].rearrange("p (t n) -> p t n", t=t)

        A1, A3, W1, W3, B1, B3, B2 = (ffw(n, 2) for n in ("A1", "A3", "W1", "W3", "B1", "B3", "B2"))
        A2, W2 = ffw("A2", FM), ffw("W2", FM)

        def v_(name):
            a, b_ = VEC[name]
            return vec_sb[:, a:b_]

        ident = sb("ident", P, P)
        headblk = sb("headblk", P, P)
        headavg = sb("headavg", P, P)
        bgh = sb("bgh", P, 2)
        cwh = sb("cwh", P, 2, DC)
        cbh = sb("cbh", P, 2)
        nega = sb("nega", P, 2, DS)
        slots8 = sb("slots8", P, E)
        mhalf = sb("mhalf", P, 2)
        gamma_sb = sb("gamma_sb", HEADS, 1)
        powrow = sb("powrow", HEADS, 2 * P)
        dmask = sb("dmask", P, HEADS, P)
        qdec = sb("qdec", P, 2, P)

        ctx_sb = sb("ctx_sb", P, S)
        xpad = sb("xpad", P, 2, S + DC - 1)
        cv = sb("cv", P, 2, S)
        u = sb("u", P, 2, S)
        dbl = sb("dbl", DR + 2 * DS, S)
        yT = sb("yT", P, 2, S)
        dt_abs = yT
        dt_pos = sb("dt_pos", P, 2, S)
        dt_e = sb("dt_e", P, 2, S)
        cth = dt_e
        dt_w = sb("dt_w", P, 2, S)
        dt_ln = dt_abs
        delta = dt_w
        du = cv
        brow = sb("brow", P, 2, UN, S)
        crow = sb("crow", P, 2, UN, S)
        decay = sb("decay", P, 2, UN, S)
        drive = sb("drive", P, 2, UN, S)
        state = sb("state", P, 2, UN, S)
        part = sb("part", P, 2, S)

        xT_sb = sb("xT_sb", P, 2, S)
        xn_sb = sb("xn_sb", P, NT, H)
        q_sb = sb("q_sb", P, 2, S)
        qm = sb("qm", P, 2, 4, S)
        qd = sb("qd", P, 2, P)
        kT = sb("kT", P, 2, S)
        glin = sb("glin", P, 2, S)
        gth = sb("gth", P, 2, S)
        gate = gth
        vpad = sb("vpad", P, NT, 2, H)
        kd = sb("kd", P, H)
        kv = sb("kv", P, 2, P)
        sc = sb("sc", P, 2, 4, P)
        gst = sb("gst", P, 2, 6)
        gmv = sb("gmv", P, 2, 2)
        geps = sb("geps", P, 2, 2)
        gdev = sb("gdev", P, 2)
        gavg = sb("gavg", P, 2, 2)
        gsq = sb("gsq", P, 2)
        gvar = sb("gvar", P, 2)
        grs = sb("grs", P, 2)
        gscale = sb("gscale", P, 2)
        gms = sb("gms", P, 2)
        gshift = sb("gshift", P, 2)
        rlin = sb("rlin", P, 2, S)
        ro = rlin
        xb = xn_sb
        r1 = sb("r1", P, NT, H)
        st = sb("st", P, NT, 6)
        ve = sb("ve", P, NT)
        mv = sb("mv", P, NT, 2)
        rs = sb("rs", P, NT)
        x1 = sb("x1", P, NT, H)
        zth = sb("zth", P, NT, H)
        zs = zth
        r2 = r1
        x2 = sb("x2", P, NT, H)
        x2T = sb("x2T", P, 2, S)

        lg = sb("lg", P, NT, E)
        le = sb("le", P, NT, E)
        pr = sb("pr", P, NT, E)
        eq = sb("eq", P, NT, E)
        mk1 = sb("mk1", P, NT, E)
        rt = sb("rt", P, NT, 2 * E + 2)
        mk0, md, rw = rt[:, :, 0:E], rt[:, :, E:2 * E], rt[:, :, 2 * E:]
        rtT = sb("rtT", 2 * E + 2, S)
        spreadw = sb("spreadw", 2 * E + 2, 6, P)
        t1 = sb("t1", P, NT)
        t2 = sb("t2", P, NT)
        top = sb("top", P, NT, 2)

        keep = sb("keep", P, NT, H)
        mkT = sb("mkT", P, 2, 2, S)
        mk1T = sb("mk1T", P, 2, S)
        rwT = sb("rwT", P, 2, S)
        am = sb("am", P, 4, 2, S)
        fth = sb("fth", P, 2, S)
        fs = fth
        fq = sb("fq", P, 2, S)
        xs = sb("xs", P, 4, S)
        xsum = sb("xsum", P, 2, S)
        a2m = sb("a2m", P, 2, 2, S)
        r3 = keep
        st3 = sb("st3", P, NT, 6)
        ve3 = sb("ve3", P, NT)
        mv3 = sb("mv3", P, NT, 2)
        rs3 = sb("rs3", P, NT)
        yo = sb("yo", P, NT, H)

        gen = [ps(f"gen{i}", P, 512) for i in range(2)]
        xf = [ps(f"xf{i}", P, 2, S) for i in range(2)]
        a2p = [ps(f"a2p{i}", P, 2, S) for i in range(2)]
        ret = ps("ret", P, 2, S)
        acc = ps("acc", P, 2, S)

        sem = {n: ctx.enter_context(nc.semaphore(n)) for n in PER}
        for n in ("w_vec", "w_rows", "w_gamma", "w_attn", "w_ssm", "w_route", "w_ff", "pow_out", "mask_in",
                  "pool_const", "dve_const", "act_const", "pow_step"):
            sem[n] = ctx.enter_context(nc.semaphore(n))
        block = ctx.enter_context(nc.Block())

        def need(eng, name, b, n):
            value = b * PER[name] + n
            if not (isinstance(value, int) and value == 0):
                eng.wait_ge(sem[name], value + (name in GIVEN))


        def of(ap, b):
            return ap[b] if isinstance(b, int) else ap[bass.ds(b, 1)].squeeze(0)

        def v3(ap, n):
            return ap.rearrange("p (t n) -> p t n", n=n)

        def batches(eng, stage):
            stage(0, None)
            with eng.Fori(1, B) as b:
                stage(b, b - 1)
            stage(None, B - 1)

        @block.sync
        def _(sp):
            for name in GIVEN:
                sp.sem_inc(sem[name], 1)
            sp.dma_start(vec_sb[:], vec).then_inc(sem["w_vec"], 16)
            sp.dma_start(gamma_sb[:], gamma).then_inc(sem["w_gamma"], 16)
            sp.dma_start(wssm_sb[:], wssm).then_inc(sem["w_ssm"], 16)
            sp.dma_start(wdt_sb[:], wdt).then_inc(sem["w_ssm"], 16)
            sp.dma_start(ctx_sb[:], ctxT[0]).then_inc(sem["ctx_in"], 16)
            sp.dma_start(xT_sb[:], xT[0]).then_inc(sem["x_in"], 16)
            sp.dma_start(wattn_sb[:], wattn).then_inc(sem["w_attn"], 16)
            sp.dma_start(rows_sb[:], rows.partition_broadcast(P)).then_inc(sem["w_rows"], 16)
            sp.dma_start(xn_sb[:], x[0]).then_inc(sem["xn_in"], 16)
            sp.wait_ge(sem["pow_step"], 9)
            sp.dma_start(pow_dram, powrow[:].unsqueeze(1).broadcast_to([HEADS, P, 2 * P])).then_inc(sem["pow_out"], 16)
            sp.wait_ge(sem["pow_out"], 16)
            sp.dma_start(dmask[:], bass.AP(tensor=pow_dram.tensor, offset=P - 1,
                                           ap=[[2 * P - 1, P], [2 * P * P, HEADS], [1, P]])).then_inc(sem["mask_in"], 16)
            for t in range(2):
                sp.dma_start(qdec[:, t], bass.AP(tensor=pow_dram.tensor, offset=t * GH * 2 * P * P + P,
                                                 ap=[[2 * P * P, GH], [2 * P, DH], [1, P]])).then_inc(sem["mask_in"], 16)
            sp.dma_start(wroute_sb[:], wroute).then_inc(sem["w_route"], 16)

            def spread(b):
                need(sp, "dbl_ready", b, 1)
                sp.dma_start(of(bc_dram, b), dbl[DR:, :]).then_inc(sem["bc_out"], 16)
                need(sp, "bc_out", b, 16)
                for c in range(DS // UN):
                    need(sp, "drive_ready", b, max(2 * c - 2, 0))
                    sp.dma_start(brow[:, c % 2], of(bc_dram, b)[c * UN:(c + 1) * UN].partition_broadcast(P)
                                 ).then_inc(sem[f"b_in{c % 2}"], 16)
                    need(sp, "out_ready", b, max(2 * c - 2, 0))
                    sp.dma_start(crow[:, c % 2], of(bc_dram, b)[DS + c * UN:DS + (c + 1) * UN].partition_broadcast(P)
                                 ).then_inc(sem[f"c_in{c % 2}"], 16)
                    if isinstance(b, int) and b == 0:
                        for name in FF_PIECES[c]:
                            a, z = FFW[name]
                            sp.dma_start(wff_sb[:, a:z], wff[:, a:z]).then_inc(sem["w_ff"], 16)

            def reload(b):
                need(sp, "gen_filled", b - 1, G_IN + 1)
                sp.dma_start(ctx_sb[:], of(ctxT, b)).then_inc(sem["ctx_in"], 16)
                need(sp, "gen_filled", b - 1, G_KN + 1)
                sp.dma_start(xT_sb[:], of(xT, b)).then_inc(sem["x_in"], 16)
                need(sp, "r1_ready", b - 1, 1)
                sp.dma_start(xn_sb[:], of(x, b)).then_inc(sem["xn_in"], 16)

            def store(fb):
                need(sp, "y_ready", fb, 2)
                sp.dma_start(of(out, fb), yo[:]).then_inc(sem["y_out"], 16)

            spread(0)
            reload(1)
            with sp.Fori(1, B - 1) as b:
                spread(b)
                reload(b + 1)
                store(b - 1)
            spread(B - 1)
            store(B - 2)
            store(B - 1)
            need(sp, "y_out", B, 0)

        @block.gpsimd
        def _(pool):
            pc = sem["pool_const"]
            pool.memset(powrow[:], 0.0).then_inc(sem["pow_step"], 1)
            pool.memset(xpad[:], 0.0).then_inc(pc, 1)
            pool.memset(ident[:], 0.0).then_inc(pc, 1)
            pool.memset(headblk[:], 1.0).then_inc(pc, 1)
            pool.memset(mhalf[:], -0.5).then_inc(pc, 1)
            pool.memset(decay[:], 0.0).then_inc(pc, 1)
            pool.wait_ge(pc, 5)
            pool.affine_select(out=ident[:], in_=ident[:], compare_op=ALU.not_equal, fill=1.0, base=0,
                               pattern=[[-1, P]], channel_multiplier=1).then_inc(pc, 1)
            blk = headblk[:].rearrange("p (g r) -> p g r", r=DH)
            pool.affine_select(out=blk, in_=blk, compare_op=ALU.is_ge, fill=0.0, base=0,
                               pattern=[[-DH, GH], [0, DH]], channel_multiplier=1).then_inc(pc, 1)
            pool.memset(spreadw[:], 0.0).then_inc(pc, 1)
            pool.wait_ge(pc, 8)
            pool.affine_select(out=blk, in_=blk, compare_op=ALU.is_ge, fill=0.0, base=DH - 1,
                               pattern=[[DH, GH], [0, DH]], channel_multiplier=-1).then_inc(pc, 1)
            pool.memset(vpad[:], 0.0).then_inc(pc, 1)
            pool.memset(geps[:], 0.0).then_inc(pc, 1)
            for e_ in range(E):
                pool.memset(slots8[:, e_:e_ + 1], float(E - e_)).then_inc(pc, 1)
            for i in range(6):
                view = spreadw[:, i].rearrange("q (e r) -> q e r", r=R)
                step, base = (-1, -(E * (i // 2) + 4 * (i % 2))) if i < 4 else (0, -(2 * E + i - 4))
                pool.affine_select(out=view, in_=view, compare_op=ALU.not_equal, fill=1.0, base=base,
                                   pattern=[[step, 4], [0, R]], channel_multiplier=1).then_inc(pc, 1)
            pool.wait_ge(pc, 17 + E)
            pool.tensor_scalar_mul(headavg[:], headblk[:], 1.0 / DH).then_inc(pc, 1)

            def drive_unit(b, i):
                j, c = i % 2, i // 2
                if i == 0:
                    need(pool, "du_ready", b, 1)
                if j == 0:
                    need(pool, f"b_in{c % 2}", b, 16 * (c // 2 + 1))
                need(pool, "state_ready", b, max(i - 1, 0))
                pool.tensor_tensor(drive[:, i % 2], du[:, j].unsqueeze(1).broadcast_to([P, UN, S]),
                                   brow[:, c % 2], ALU.mult).then_inc(sem["drive_ready"], 1)

            def add_part(b, i):
                j = i % 2
                if i == 0:
                    need(pool, "y_init", b, 2)
                need(pool, "part_ready", b, i + 1)
                if i >= 2:
                    need(pool, "y_part", b, i - 1)
                pool.tensor_tensor(yT[:, j], yT[:, j], part[:, i % 2], ALU.add).then_inc(sem["y_part"], 1)

            def root(b, src, dst, ready, n, done):
                need(pool, ready, b, n)
                pool.tensor_tensor(dst[:], src[:], mhalf[:], ALU.pow).then_inc(sem[done], 1)

            def stage(b, fb):
                if b is not None:
                    need(pool, "q_ready", b, 2)
                    if isinstance(b, int):
                        pool.wait_ge(sem["mask_in"], 48)
                        pool.wait_ge(sem["w_rows"], 16)
                    pool.tensor_tensor(qd[:], q_sb[:, :, P:], qdec[:], ALU.mult).then_inc(sem["qd_ready"], 1)
                    need(pool, "xn_in", b, 16)
                    pool.tensor_tensor(xb[:], xn_sb[:], bo_row.unsqueeze(1).broadcast_to([P, NT, H]), ALU.add
                                       ).then_inc(sem["xb_ready"], 1)
                if fb is not None:
                    need(pool, "mk_ready", fb, 2)
                    pool.tensor_tensor(mk1T[:], mkT[:, 0], mkT[:, 1], ALU.add).then_inc(sem["mk1_ready"], 1)
                if b is not None:
                    need(pool, "dt_step", b, 4)
                    pool.tensor_tensor(du[:], delta[:], u[:], ALU.mult).then_inc(sem["du_ready"], 1)
                    drive_unit(b, 0)
                    drive_unit(b, 1)
                for n, (m, k) in enumerate(MAIN):
                    if b is not None:
                        if n == 7:
                            root(b, gvar, grs, "gn_step", 9, "gn_pow")
                        if n == 11:
                            root(b, ve, rs, "r1_ready", 7, "r1_pow")
                        for i in SCANS[n]:
                            if i + 2 < UNITS:
                                drive_unit(b, i + 2)
                            add_part(b, i)
                        if n == 8:
                            need(pool, "ro_lin", b, 2)
                            need(pool, "gate_ready", b, 1)
                            pool.tensor_tensor(ro[:], rlin[:], gate[:], ALU.mult).then_inc(sem["ro_ready"], 1)
                    if fb is not None:
                        need(pool, "q3_ready", fb, n + 1)
                        if n == 0:
                            need(pool, "rw_ready", fb, 1)
                        need(pool, "xs_used", fb, max(n - 3, 0))
                        need(pool, "xsum_ready", fb, MAIN[n - 4][0] + 1 if n >= 4 else 0)
                        pool.tensor_tensor(xs[:, n % 4], fq[:, n % 2], rwT[:, k], ALU.mult).then_inc(sem["xs_ready"], 1)
                    if b is not None and n == 13:
                        root(b, ve, rs, "r2_ready", 8, "r2_pow")
                    if fb is not None:
                        if k == 1:
                            first = MAIN.index((m, 0))
                            need(pool, "xs_ready", fb, n + 1)
                            need(pool, "xsum_used", fb, max(m - 1, 0))
                            pool.tensor_tensor(xsum[:, m % 2], xs[:, first % 4], xs[:, n % 4], ALU.add
                                               ).then_inc(sem["xsum_ready"], 1)
                if fb is not None:
                    root(fb, ve3, rs3, "r3_ready", 7, "r3_pow")

            pool.wait_ge(pc, CONSTS)
            batches(pool, stage)

        @block.scalar
        def _(act):
            act.wait_ge(sem["w_vec"], 16)
            act.activation(nega[:], v_("alog").rearrange("p (j n) -> p j n", j=2), ACT.Exp).then_inc(sem["act_const"], 1)
            act.wait_ge(sem["dve_const"], 4)
            act.wait_ge(sem["pool_const"], 1)

            def decays(b, i):
                j, c = i % 2, i // 2
                if i == 0:
                    need(act, "dt_step", b, 4)
                need(act, "state_ready", b, max(i - 1, 0))
                for n in range(UN):
                    s_ = c * UN + n
                    act.activation(decay[:, i % 2, n, 1:], delta[:, j, 1:], ACT.Exp, scale=nega[:, j, s_:s_ + 1]
                                   ).then_inc(sem["decay_ready"], 1)

            def bank(b, i):
                need(act, "gen_filled", b, i + 1)
                return v3(gen[i % 2][:], S)

            def masked(b, g):
                t = g // 2
                need(act, "gen_filled", b, G_SC + 2 * g - 2 if g >= 2 else 0)
                if g == 0:
                    need(act, "q_ready", b, 2)
                for h in range(4):
                    row = DH * (4 * (g % 2) + h)
                    last = act.activation(qm[:, g % 2, h], q_sb[:, t], ACT.Copy, scale=headblk[:, row:row + 1])
                last.then_inc(sem["qm_ready"], 1)

            def stage(b, fb):
                if b is not None:
                    g = bank(b, G_IN)
                    act.activation(xpad[:, :, DC - 1:], g, ACT.Copy).then_inc(sem["conv_in"], 1)
                    for j in range(2):
                        act.activation(cv[:, j], g[:, j], ACT.Identity, bias=cbh[:, j:j + 1],
                                       scale=cwh[:, j, DC - 1:DC]).then_inc(sem["conv_in"], 1)
                    g = bank(b, G_Q)
                    need(act, "qd_ready", b, 0)
                    for t in range(2):
                        act.activation(q_sb[:, t], g[:, t], ACT.Identity, bias=v_("bq")[:, t:t + 1]
                                       ).then_inc(sem["q_ready"], 1)
                if fb is not None:
                    need(act, "xf_filled", fb, X_X2 + 1)
                    act.activation(x2T[:], xf[XF_BANK[X_X2]][:], ACT.Copy).then_inc(sem["x2T_ready"], 1)
                if b is not None:
                    need(act, "conv_step", b, 6)
                    act.activation(cth[:], cv[:], ACT.Tanh).then_inc(sem["conv_tanh"], 1)
                    g = bank(b, G_K)
                    for t in range(2):
                        act.activation(kT[:, t], g[:, t], ACT.Identity, bias=v_("bk")[:, t:t + 1]
                                       ).then_inc(sem["k_ready"], 1)
                if fb is not None:
                    need(act, "rt_step", fb, 2)
                    act.activation(le[:], lg[:], ACT.Exp).then_inc(sem["lg_exp"], 1)
                if b is not None:
                    need(act, "gen_filled", b, G_DBL + 1)
                    need(act, "bc_out", b, 0)
                    act.activation(dbl[:], gen[G_DBL % 2][0:DR + 2 * DS, 0:S], ACT.Copy).then_inc(sem["dbl_ready"], 1)
                    g = bank(b, G_GATE)
                    for t in range(2):
                        act.activation(glin[:, t], g[:, t], ACT.Identity, bias=bgh[:, t:t + 1], scale=0.5
                                       ).then_inc(sem["gate_lin"], 1)
                    need(act, "gate_lin", b, 2)
                    act.activation(gth[:], glin[:], ACT.Tanh).then_inc(sem["gate_tanh"], 1)
                if fb is not None:
                    need(act, "xf_filled", fb, X_RT + 1)
                    act.activation(rtT[:], xf[XF_BANK[X_RT]][0:2 * E + 2, 0], ACT.Copy).then_inc(sem["rtT_ready"], 1)
                if b is not None:
                    g = bank(b, G_DT)
                    for func, dst in ((ACT.Abs, dt_abs), (ACT.Relu, dt_pos)):
                        for j in range(2):
                            act.activation(dst[:, j], g[:, j], func, bias=v_("dtb")[:, j:j + 1]
                                           ).then_inc(sem["dt_parts"], 1)
                if fb is not None:
                    need(act, "a2_ready", fb, 0)
                    for i in range(2):
                        need(act, "xf_filled", fb, X_MK + i + 1)
                        act.activation(mkT[:, i], xf[XF_BANK[X_MK + i]][:], ACT.Copy).then_inc(sem["mk_ready"], 1)
                if b is not None:
                    need(act, "dt_parts", b, 2)
                    act.activation(dt_e[:], dt_abs[:], ACT.Exp, scale=-1.0).then_inc(sem["dt_exp"], 1)
                    need(act, "dt_exp", b, 1)
                    act.activation(dt_ln[:], dt_e[:], ACT.Ln, bias=1.0).then_inc(sem["dt_log"], 1)
                if fb is not None:
                    need(act, "xf_filled", fb, X_RW + 1)
                    need(act, "xs_ready", fb, 0)
                    act.activation(rwT[:], xf[XF_BANK[X_RW]][:], ACT.Copy).then_inc(sem["rw_ready"], 1)
                if b is not None:
                    if isinstance(b, int):
                        act.wait_ge(sem["pool_const"], CONSTS)
                    decays(b, 0)
                    decays(b, 1)
                    masked(b, 0)
                    for j in range(2):
                        act.activation(yT[:, j], u[:, j], ACT.Copy, scale=v_("D")[:, j:j + 1]).then_inc(sem["y_init"], 1)
                for n in range(len(MAIN)):
                    if fb is not None:
                        need(act, "xf_filled", fb, X_MAIN + n + 1)
                        need(act, "s_ready", fb, max(n - 1, 0))
                        act.activation(fth[:, n % 2], xf[XF_BANK[X_MAIN + n]][:, 0], ACT.Tanh, scale=0.5
                                       ).then_inc(sem["th_ready"], 1)
                    if b is not None:
                        if n < 3:
                            masked(b, n + 1)
                        if n == 7:
                            need(act, "gn_step", b, 12)
                            for t in range(2):
                                act.activation(rlin[:, t], ret[:, t], ACT.Identity, bias=gshift[:, t:t + 1],
                                               scale=gscale[:, t:t + 1]).then_inc(sem["ro_lin"], 1)
                        for i in SCANS[n]:
                            if i + 2 < UNITS:
                                decays(b, i + 2)
                        if n == 11:
                            need(act, "x1_ready", b, 2)
                            act.activation(zth[:], x1[:], ACT.Tanh, scale=0.5).then_inc(sem["z_tanh"], 1)
                    if fb is not None and n == 4:
                        need(act, "r3_ready", fb, 0)
                        act.activation(keep[:], x2[:], ACT.Copy).then_inc(sem["keep_ready"], 1)

            batches(act, stage)

        @block.tensor
        def _(pe):
            def mm(o, l, r, **kw):
                return pe.matmul(o, l, r, skip_group_check=True, **kw)

            def gen_free(b, i):
                if i >= 2:
                    name, n = GEN[i - 2]
                    need(pe, name, b, n)
                else:
                    last = max(k for k in range(len(GEN)) if k % 2 == i % 2)
                    need(pe, GEN[last][0], b, 0)

            def xf_free(fb, i):
                before = [k for k in range(i) if XF_BANK[k] == XF_BANK[i]]
                if before:
                    name, n = XF[before[-1]]
                    need(pe, name, fb, n)
                else:
                    need(pe, "q3_ready", fb, 0)

            def project(b, i, w, src):
                gen_free(b, i)
                g = v3(gen[i % 2][:], S)
                for t in range(2):
                    for k in range(2):
                        last = mm(g[:, t], w[:, k, t * P:(t + 1) * P], src[:, k], start=(k == 0), stop=(k == 1))
                last.then_inc(sem["gen_filled"], 1)

            def hidden(fb, n):
                m, k = MAIN[n]
                xf_free(fb, X_MAIN + n)
                o = xf[XF_BANK[X_MAIN + n]]
                fs_ = slice(m * P, (m + 1) * P)
                if k == 0:
                    for half, W in enumerate((W1, W3)):
                        for t in range(2):
                            mm(o[:, half], W[:, t, fs_], x2T[:, t], start=(half == 0 and t == 0), stop=False)
                for half, B_ in enumerate((B1, B3)):
                    if n in (0, 2):
                        need(pe, "am_ready", fb, n + half + 1)
                    for t in range(2):
                        last = mm(o[:, half], B_[:, t, fs_], am[:, 2 * half + k, t], start=False, stop=(t == 1))
                last.then_inc(sem["xf_filled"], 1)

            def shrink(fb, n):
                m, k = MAIN[n]
                need(pe, "xs_ready", fb, n + 1)
                if n == 0:
                    need(pe, "am_ready", fb, 4)
                for t in range(2):
                    last = mm(a2p[k][:, t], A2[:, m, t * P:(t + 1) * P], xs[:, n % 4], start=(m == 0 and t == 0),
                              stop=(m == FM - 1))
                last.then_inc(sem["xs_used"], 1)
                if k == 1:
                    need(pe, "xsum_ready", fb, m + 1)
                    if m == 0:
                        need(pe, "r3_ready", fb, 0)
                    for t in range(NT):
                        last = mm(acc[:, t], xsum[:, m % 2, t * P:(t + 1) * P], W2[:, m], start=(m == 0 and t == 0),
                                  stop=False)
                    last.then_inc(sem["xsum_used"], 1)

            def spread_rows(fb, i):
                xf_free(fb, i)
                for t in range(2):
                    last = mm(xf[XF_BANK[i]][:, t], spreadw[:, 2 * (i - X_MK) + t], rtT[:], start=True, stop=True)
                last.then_inc(sem["xf_filled"], 1)

            def scores(b, i):
                t, chunk, g = i // 4, i % 2, i // 2
                gen_free(b, G_SC + i)
                if i == 0:
                    need(pe, "k_ready", b, 2)
                if chunk == 0:
                    need(pe, "qm_ready", b, g + 1)
                cs = slice(chunk * P, (chunk + 1) * P)
                mm(gen[(G_SC + i) % 2][:].rearrange("p (h i) -> p h i", h=4), kT[:, t, cs], qm[:, g % 2, :, cs],
                   start=True, stop=True).then_inc(sem["gen_filled"], 1)

            def values(b, i):
                t, chunk, g = i // 4, i % 2, i // 2
                need(pe, "sc_ready", b, i + 1)
                if i == 0:
                    need(pe, "ro_lin", b, 0)
                    need(pe, "v_ready", b, 4)
                cs = slice(chunk * P, (chunk + 1) * P)
                for p_ in range(2):
                    for pair in range(2):
                        w = 2 * (g % 2) + pair
                        last = mm(ret[32 * w:32 * w + 32, t, cs], vpad[:, chunk, p_, t * P + 32 * w:t * P + 32 * w + 32],
                                  sc[:, i % 2, 2 * pair + p_], start=(t == 0 and chunk == 0 and p_ == 0),
                                  stop=(p_ == 1 and chunk == 0))
                if i % 4 == 3:
                    if i == 3:
                        need(pe, "kv_ready", b, 1)
                        need(pe, "qd_ready", b, 1)
                    last = mm(ret[:, t, P:], kv[:, t], qd[:, t], start=False, stop=True)
                last.then_inc(sem["av_done"], 1)

            def stage(b, fb):
                if b is not None:
                    if isinstance(b, int):
                        pe.wait_ge(sem["w_ssm"], 32)
                    need(pe, "ctx_in", b, 16)
                    gen_free(b, G_IN)
                    g = v3(gen[G_IN % 2][:], S)
                    for j in range(2):
                        last = mm(g[:, j], w_in[:, j * P:(j + 1) * P], ctx_sb[:], start=True, stop=True)
                    last.then_inc(sem["gen_filled"], 1)
                    if isinstance(b, int):
                        pe.wait_ge(sem["w_attn"], 16)
                    need(pe, "x_in", b, 16)
                    project(b, G_Q, wq, xT_sb)
                if fb is not None:
                    xf_free(fb, X_X2)
                    need(pe, "x2_ready", fb, 2)
                    o = xf[XF_BANK[X_X2]]
                    for t in range(NT):
                        for k in range(2):
                            last = pe.transpose(o[:, k, t * P:(t + 1) * P], x2[:, t, k * P:(k + 1) * P], ident[:])
                    last.then_inc(sem["xf_filled"], 1)
                if b is not None:
                    project(b, G_K, wk, xT_sb)
                if fb is not None:
                    xf_free(fb, X_LG)
                    need(pe, "x2T_ready", fb, 1)
                    pe.wait_ge(sem["w_route"], 16)
                    for t in range(NT):
                        for k in range(2):
                            last = mm(xf[XF_BANK[X_LG]][:, 0, t * E:(t + 1) * E], x2T[:, k, t * P:(t + 1) * P], wroute_sb[:, k],
                                      start=(k == 0), stop=(k == 1))
                    last.then_inc(sem["xf_filled"], 1)
                if b is not None:
                    gen_free(b, G_V)
                    g = v3(gen[G_V % 2][:], H)
                    for t in range(NT):
                        for k in range(2):
                            last = mm(g[:, t], xT_sb[:, k, t * P:(t + 1) * P], wv[:, k], start=(k == 0), stop=(k == 1))
                    last.then_inc(sem["gen_filled"], 1)
                if fb is not None:
                    pe.wait_ge(sem["w_ff"], 16 * len(FFW))
                    need(pe, "a2_ready", fb, 0)
                    for half, w in enumerate((A1, A3)):
                        for t in range(2):
                            for k in range(2):
                                last = mm(a2p[half][:, t], w[:, k, t * P:(t + 1) * P], x2T[:, k], start=(k == 0),
                                          stop=(k == 1))
                        last.then_inc(sem["a_filled"], 1)
                if b is not None:
                    gen_free(b, G_DBL)
                    need(pe, "u_ready", b, 1)
                    for j in range(2):
                        last = mm(gen[G_DBL % 2][0:DR + 2 * DS, 0:S], w_xp[:, j], u[:, j], start=(j == 0), stop=(j == 1))
                    last.then_inc(sem["gen_filled"], 1)
                    gen_free(b, G_KN)
                    for k in range(2):
                        last = mm(gen[G_KN % 2][:, 0:H], xT_sb[:, k, 0:P], wk[:, k], start=(k == 0), stop=(k == 1))
                    last.then_inc(sem["gen_filled"], 1)
                    project(b, G_GATE, wg, xT_sb)
                    gen_free(b, G_DT)
                    need(pe, "dbl_ready", b, 1)
                    g = v3(gen[G_DT % 2][:], S)
                    for j in range(2):
                        last = mm(g[:, j], wdt_sb[:, j * P:(j + 1) * P], dbl[0:DR, :], start=True, stop=True)
                    last.then_inc(sem["gen_filled"], 1)
                    if isinstance(b, int):
                        pe.wait_ge(sem["pool_const"], CONSTS)
                    gen_free(b, G_KV)
                    need(pe, "kd_ready", b, 2)
                    need(pe, "v_ready", b, 4)
                    g = v3(gen[G_KV % 2][:], P)
                    for t in range(2):
                        for p_ in range(2):
                            last = mm(g[:, t], kd[:, t * P:(t + 1) * P], vpad[:, 0, p_, t * P:(t + 1) * P],
                                      start=(p_ == 0), stop=(p_ == 1))
                    last.then_inc(sem["gen_filled"], 1)
                if fb is not None:
                    xf_free(fb, X_RT)
                    need(pe, "rt_step", fb, 21)
                    for n in range(NT):
                        last = mm(xf[XF_BANK[X_RT]][0:2 * E + 2, 0, n * P:(n + 1) * P], rt[:, n], ident[:], start=True, stop=True)
                    last.then_inc(sem["xf_filled"], 1)
                if fb is not None:
                    need(pe, "rtT_ready", fb, 1)
                    for i in (X_MK, X_MD, X_RW):
                        spread_rows(fb, i)
                for n in range(len(MAIN)):
                    if fb is not None:
                        hidden(fb, n)
                    if b is not None and n == 13:
                        gen_free(b, G_Y)
                        need(pe, "yT_ready", b, 1)
                        g = v3(gen[G_Y % 2][:], H)
                        for t in range(NT):
                            for j in range(2):
                                last = pe.transpose(g[:, t, j * P:(j + 1) * P], yT[:, j, t * P:(t + 1) * P], ident[:])
                        last.then_inc(sem["gen_filled"], 1)
                    if b is not None and n < 4:
                        scores(b, 2 * n)
                    if fb is not None and n >= LAG:
                        shrink(fb, n - LAG)
                    if b is not None:
                        if 1 <= n <= 4:
                            values(b, 2 * n - 1)
                        if n < 4:
                            scores(b, 2 * n + 1)
                            values(b, 2 * n)
                        if n == 5:
                            gen_free(b, G_MEAN)
                            need(pe, "gn_step", b, 5)
                            mm(gen[G_MEAN % 2][:, 0:4], headavg[:], gmv[:].rearrange("p t s -> p (t s)"), start=True, stop=True
                               ).then_inc(sem["gen_filled"], 1)
                        if n == 6:
                            gen_free(b, G_VAR)
                            need(pe, "gn_step", b, 8)
                            mm(gen[G_VAR % 2][:, 0:2], headavg[:], gsq[:], start=True, stop=True).then_inc(sem["gen_filled"], 1)
                        if n == 9:
                            gen_free(b, G_OUT)
                            need(pe, "ro_ready", b, 1)
                            g = v3(gen[G_OUT % 2][:], H)
                            for t in range(NT):
                                for k in range(2):
                                    last = mm(g[:, t], ro[:, k, t * P:(t + 1) * P], wo[:, k], start=(k == 0), stop=(k == 1))
                            last.then_inc(sem["gen_filled"], 1)
                if fb is not None:
                    for n in range(len(MAIN) - LAG, len(MAIN)):
                        shrink(fb, n)
                if fb is not None:
                    need(pe, "a2_ready", fb, 3)
                    for t in range(NT):
                        for k in range(2):
                            last = mm(acc[:, t], a2m[:, 0, k, t * P:(t + 1) * P], B2[:, k], start=False, stop=(k == 1))
                    last.then_inc(sem["down_done"], 1)

            batches(pe, stage)

        @block.vector
        def _(dve):
            dc = sem["dve_const"]
            dve.wait_ge(sem["w_gamma"], 16)
            dve.wait_ge(sem["pow_step"], 1)
            one = P - 1
            dve.memset(powrow[:, one:one + 1], 1.0)
            dve.tensor_copy(powrow[:, one + 1:one + 2], gamma_sb[:]).then_inc(sem["pow_step"], 1)
            known = 1
            while known < P:
                dve.wait_ge(sem["pow_step"], 2 + known.bit_length() - 1)
                dve.tensor_scalar(powrow[:, one + 1 + known:one + 1 + 2 * known], powrow[:, one + 1:one + 1 + known],
                                  powrow[:, one + known:one + known + 1], None, ALU.mult).then_inc(sem["pow_step"], 1)
                known *= 2
            dve.wait_ge(sem["w_vec"], 16)
            dve.tensor_scalar(bgh[:], v_("bg"), 0.5, None, ALU.mult).then_inc(dc, 1)
            dve.tensor_scalar(cwh[:].rearrange("p j k -> p (j k)"), v_("cw"), 0.5, None, ALU.mult).then_inc(dc, 1)
            dve.tensor_scalar(cbh[:], v_("cb"), 0.5, None, ALU.mult).then_inc(dc, 1)
            dve.wait_ge(sem["act_const"], 1)
            dve.tensor_scalar(nega[:], nega[:], -1.0, None, ALU.mult).then_inc(dc, 1)
            dve.wait_ge(dc, 4)

            def bank(b, i, n):
                need(dve, "gen_filled", b, i + 1)
                return v3(gen[i % 2][:], n)

            def scan(b, i):
                flat = lambda ap: ap.rearrange("p n t -> p (n t)")
                need(dve, "decay_ready", b, UN * (i + 1))
                need(dve, "drive_ready", b, i + 1)
                need(dve, "part_ready", b, max(i - 1, 0))
                dve.tensor_tensor_scan(flat(state[:, i % 2]), flat(decay[:, i % 2]), flat(drive[:, i % 2]), 0.0,
                                       ALU.mult, ALU.add).then_inc(sem["state_ready"], 1)

            def times_c(b, i):
                j, c = i % 2, i // 2
                if j == 0:
                    need(dve, f"c_in{c % 2}", b, 16 * (c // 2 + 1))
                need(dve, "state_ready", b, i + 1)
                dve.tensor_tensor(state[:, i % 2], state[:, i % 2], crow[:, c % 2], ALU.mult
                                  ).then_inc(sem["out_ready"], 1)

            def pair(b, i):
                need(dve, "out_ready", b, i + 1)
                need(dve, "y_part", b, max(i - 1, 0))
                dve.tensor_tensor(part[:, i % 2], state[:, i % 2, 0], state[:, i % 2, 1], ALU.add
                                  ).then_inc(sem["part_ready"], 1)

            def decayed(b, i):
                need(dve, "gen_filled", b, G_SC + i + 1)
                need(dve, "av_done", b, max(i - 1, 0))
                h0 = 4 * (i // 2)
                dve.tensor_tensor(sc[:, i % 2], gen[(G_SC + i) % 2][:].rearrange("p (h i) -> p h i", h=4),
                                  dmask[:, h0:h0 + 4], ALU.mult).then_inc(sem["sc_ready"], 1)

            def norm_stats(b, src, st_, mv_, ve_, ready, n):
                need(dve, ready, b, n)
                for t in range(NT):
                    dve.bn_stats(st_[:, t], src[:, t]).then_inc(sem[ready], 1)
                need(dve, ready, b, n + 2)
                dve.memset(ve_[:], EPS).then_inc(sem[ready], 1)
                for t in range(NT):
                    dve.bn_aggr(mv_[:, t], st_[:, t]).then_inc(sem[ready], 1)
                need(dve, ready, b, n + 5)
                dve.tensor_tensor(ve_[:], mv_[:, :, 1], ve_[:], ALU.add).then_inc(sem[ready], 1)

            def norm_apply(b, src, mv_, rs_, dst, pow_, done):
                need(dve, pow_, b, 1)
                for t in range(NT):
                    dve.tensor_scalar(dst[:, t], src[:, t], mv_[:, t, 0:1], rs_[:, t:t + 1], ALU.subtract, ALU.mult
                                      ).then_inc(sem[done], 1)

            def stage(b, fb):
                if b is not None:
                    need(dve, "conv_in", b, 3)
                    for k in range(DC - 1):
                        for j in range(2):
                            i = 2 * k + j
                            if i >= 2:
                                need(dve, "conv_step", b, i - 1)
                            dve.scalar_tensor_tensor(cv[:, j], xpad[:, j, k:k + S], cwh[:, j, k:k + 1], cv[:, j],
                                                     ALU.mult, ALU.add).then_inc(sem["conv_step"], 1)
                    need(dve, "conv_tanh", b, 1)
                    dve.scalar_tensor_tensor(u[:], cth[:], 1.0, cv[:], ALU.add, ALU.mult).then_inc(sem["u_ready"], 1)
                if fb is not None:
                    route(fb, 0)
                if b is not None:
                    if isinstance(b, int):
                        dve.wait_ge(sem["w_rows"], 16)
                        dve.wait_ge(sem["pool_const"], CONSTS)
                    g = bank(b, G_V, H)
                    pairs = lambda ap: ap.rearrange("p (w a d) -> p w a d", a=2, d=DH)
                    for t in range(NT):
                        for p_ in range(2):
                            dve.tensor_tensor(pairs(vpad[:, t, p_])[:, :, p_], pairs(g[:, t])[:, :, p_],
                                              pairs(bv_row)[:, :, p_], ALU.add).then_inc(sem["v_ready"], 1)
                if fb is not None:
                    route(fb, 1)
                if b is not None:
                    g = bank(b, G_KN, H)
                    dve.tensor_tensor(kd[:], g[:, 0], bk_row, ALU.add).then_inc(sem["kd_ready"], 1)
                    need(dve, "kd_ready", b, 1)
                    if isinstance(b, int):
                        dve.wait_ge(sem["mask_in"], 48)
                    kdh = kd[:].rearrange("p (h d) -> p h d", d=DH)
                    dve.tensor_tensor(kdh, kdh, dmask[:, :, P - 1:P].broadcast_to([P, HEADS, DH]), ALU.mult
                                      ).then_inc(sem["kd_ready"], 1)
                if b is not None:
                    need(dve, "gate_tanh", b, 1)
                    dve.scalar_tensor_tensor(gate[:], gth[:], 1.0, glin[:], ALU.add, ALU.mult).then_inc(sem["gate_ready"], 1)
                    need(dve, "gen_filled", b, G_KV + 1)
                    dve.tensor_tensor(kv[:], v3(gen[G_KV % 2][:, 0:2 * P], P), headblk[:].unsqueeze(1).broadcast_to([P, 2, P]),
                                      ALU.mult).then_inc(sem["kv_ready"], 1)
                    need(dve, "dt_exp", b, 1)
                    dve.tensor_scalar(dt_w[:], dt_e[:], 1.0, -1.0, ALU.add, ALU.add).then_inc(sem["dt_step"], 1)
                    need(dve, "dt_step", b, 1)
                    dve.tensor_tensor(dt_w[:], dt_e[:], dt_w[:], ALU.subtract).then_inc(sem["dt_step"], 1)
                    need(dve, "dt_step", b, 2)
                    need(dve, "dt_log", b, 1)
                    dve.tensor_tensor(dt_w[:], dt_w[:], dt_ln[:], ALU.add).then_inc(sem["dt_step"], 1)
                    need(dve, "dt_step", b, 3)
                    dve.tensor_tensor(delta[:], dt_w[:], dt_pos[:], ALU.add).then_inc(sem["dt_step"], 1)
                if fb is not None:
                    need(dve, "a_filled", fb, 2)
                    for k in range(2):
                        need(dve, "mk_ready", fb, k + 1)
                        for half in range(2):
                            dve.tensor_tensor(am[:, 2 * half + k], a2p[half][:], mkT[:, k], ALU.mult
                                              ).then_inc(sem["am_ready"], 1)
                for n in range(len(MAIN)):
                    units = SCANS[n] if b is not None else []
                    if units:
                        scan(b, units[0])
                    if b is not None and n < 4:
                        decayed(b, 2 * n)
                    if units:
                        times_c(b, units[0])
                    if fb is not None:
                        o = xf[XF_BANK[X_MAIN + n]]
                        need(dve, "th_ready", fb, n + 1)
                        dve.scalar_tensor_tensor(fs[:, n % 2], fth[:, n % 2], 1.0, o[:, 0], ALU.add, ALU.mult
                                                 ).then_inc(sem["s_ready"], 1)
                    if units:
                        pair(b, units[0])
                    if fb is not None:
                        need(dve, "s_ready", fb, n + 1)
                        need(dve, "xs_ready", fb, max(n - 1, 0))
                        dve.tensor_tensor(fq[:, n % 2], fs[:, n % 2], o[:, 1], ALU.mult).then_inc(sem["q3_ready"], 1)
                    if b is not None and n < 4:
                        decayed(b, 2 * n + 1)
                    for i in units[1:]:
                        scan(b, i)
                        times_c(b, i)
                        pair(b, i)
                    if b is not None:
                        if n == 4:
                            need(dve, "av_done", b, 8)
                            for t in range(2):
                                dve.bn_stats(gst[:, t], ret[:, t]).then_inc(sem["gn_step"], 1)
                            need(dve, "gn_step", b, 2)
                            dve.memset(geps[:, :, 1], EPS).then_inc(sem["gn_step"], 1)
                            for t in range(2):
                                dve.bn_aggr(gmv[:, t], gst[:, t]).then_inc(sem["gn_step"], 1)
                        if n == 5:
                            need(dve, "gen_filled", b, G_MEAN + 1)
                            dve.tensor_tensor(gavg[:], gen[G_MEAN % 2][:, 0:4].rearrange("p (t s) -> p t s", t=2), geps[:],
                                              ALU.add).then_inc(sem["gn_step"], 1)
                            need(dve, "gn_step", b, 6)
                            dve.tensor_tensor(gdev[:], gmv[:, :, 0], gavg[:, :, 0], ALU.subtract).then_inc(sem["gn_step"], 1)
                            need(dve, "gn_step", b, 7)
                            dve.tensor_tensor(gsq[:], gdev[:], gdev[:], ALU.mult).then_inc(sem["gn_step"], 1)
                        if n == 6:
                            need(dve, "gen_filled", b, G_VAR + 1)
                            dve.tensor_tensor(gvar[:], gen[G_VAR % 2][:, 0:2], gavg[:, :, 1], ALU.add).then_inc(sem["gn_step"], 1)
                        if n == 7:
                            need(dve, "gn_pow", b, 1)
                            dve.tensor_tensor(gscale[:], grs[:], v_("gnw"), ALU.mult).then_inc(sem["gn_step"], 1)
                            need(dve, "gn_step", b, 10)
                            dve.tensor_tensor(gms[:], gscale[:], gavg[:, :, 0], ALU.mult).then_inc(sem["gn_step"], 1)
                            need(dve, "gn_step", b, 11)
                            dve.tensor_tensor(gshift[:], v_("gnb"), gms[:], ALU.subtract).then_inc(sem["gn_step"], 1)
                        if n == 10:
                            g = bank(b, G_OUT, H)
                            need(dve, "xb_ready", b, 1)
                            dve.tensor_tensor(r1[:], g, xb[:], ALU.add).then_inc(sem["r1_ready"], 1)
                            norm_stats(b, r1, st, mv, ve, "r1_ready", 1)
                        if n == 11:
                            norm_apply(b, r1, mv, rs, x1, "r1_pow", "x1_ready")
                        if n == 12:
                            need(dve, "z_tanh", b, 1)
                            dve.scalar_tensor_tensor(zs[:], zth[:], 1.0, x1[:], ALU.add, ALU.mult).then_inc(sem["r2_ready"], 1)
                            need(dve, "y_part", b, UNITS)
                            need(dve, "r2_ready", b, 1)
                            dve.scalar_tensor_tensor(yT[:], zs[:], 0.5, yT[:], ALU.mult, ALU.mult).then_inc(sem["yT_ready"], 1)
                        if n == 13:
                            g = bank(b, G_Y, H)
                            dve.tensor_tensor(r2[:], g, x1[:], ALU.add).then_inc(sem["r2_ready"], 1)
                            norm_stats(b, r2, st, mv, ve, "r2_ready", 2)
                if b is not None:
                    need(dve, "keep_ready", b, 0)
                    norm_apply(b, r2, mv, rs, x2, "r2_pow", "x2_ready")
                if fb is not None:
                    need(dve, "xs_used", fb, 14)
                    need(dve, "mk1_ready", fb, 1)
                    dve.tensor_tensor(a2m[:, 0], a2p[0][:], mkT[:, 0], ALU.mult).then_inc(sem["a2_ready"], 1)
                    dve.tensor_tensor(a2m[:, 1], a2p[1][:], mk1T[:], ALU.mult).then_inc(sem["a2_ready"], 1)
                    need(dve, "a2_ready", fb, 2)
                    dve.tensor_tensor(a2m[:, 0], a2m[:, 0], a2m[:, 1], ALU.add).then_inc(sem["a2_ready"], 1)
                if fb is not None:
                    need(dve, "down_done", fb, 1)
                    need(dve, "keep_ready", fb, 1)
                    dve.tensor_tensor(r3[:], acc[:], keep[:], ALU.add).then_inc(sem["r3_ready"], 1)
                    norm_stats(fb, r3, st3, mv3, ve3, "r3_ready", 1)
                    need(dve, "y_out", fb, 0)
                    norm_apply(fb, r3, mv3, rs3, yo, "r3_pow", "y_ready")

            def route(b, part_):
                step = [2 * part_]

                def did(ins):
                    step[0] += 1
                    ins.then_inc(sem["rt_step"], 1)
                    need(dve, "rt_step", b, step[0])

                wide = lambda ap: ap.unsqueeze(2).broadcast_to([P, NT, E])
                if part_ == 0:
                    need(dve, "xf_filled", b, X_LG + 1)
                    dve.tensor_copy(lg[:], xf[XF_BANK[X_LG]][:, 0, 0:NT * E].rearrange("p (t e) -> p t e", t=NT)
                                    ).then_inc(sem["lg_ready"], 1)
                    need(dve, "lg_ready", b, 1)
                    did(dve.tensor_reduce(t1[:], lg[:], AX.X, ALU.max))
                    did(dve.tensor_tensor(lg[:], lg[:], wide(t1[:]), ALU.subtract))
                if part_ == 1:
                    need(dve, "lg_exp", b, 1)
                    did(dve.tensor_reduce(t1[:], le[:], AX.X, ALU.add))
                    did(dve.reciprocal(t2[:], t1[:]))
                    did(dve.tensor_tensor(pr[:], le[:], wide(t2[:]), ALU.mult))
                    for k in range(2):
                        did(dve.tensor_reduce(top[:, :, k], pr[:], AX.X, ALU.max))
                        did(dve.tensor_tensor(eq[:], pr[:], wide(top[:, :, k]), ALU.is_equal))
                        did(dve.tensor_tensor(eq[:], eq[:], slots8[:].unsqueeze(1).broadcast_to([P, NT, E]), ALU.mult))
                        did(dve.tensor_reduce(t1[:], eq[:], AX.X, ALU.max))
                        did(dve.tensor_tensor((mk0, mk1[:])[k], eq[:], wide(t1[:]), ALU.is_equal))
                        if k == 0:
                            did(dve.scalar_tensor_tensor(pr[:], mk0, -4.0, pr[:], ALU.mult, ALU.add))
                    did(dve.tensor_tensor(md, mk1[:], mk0, ALU.subtract))
                    did(dve.tensor_tensor(t1[:], top[:, :, 0], top[:, :, 1], ALU.add))
                    did(dve.reciprocal(t2[:], t1[:]))
                    for k in range(2):
                        did(dve.scalar_tensor_tensor(rw[:, :, k], top[:, :, k], 0.5, t2[:], ALU.mult, ALU.mult))

            batches(dve, stage)


def kernel(**inputs):
    import numpy as np
    import concourse.bacc as bacc
    from concourse import mybir
    from concourse.bass_utils import run_bass_kernel_spmd

    a = {k: np.asarray(v) for k, v in inputs.items()}
    g = lambda n: a["L0_" + n]

    def cols(m):
        m = m.reshape(m.shape[0], -1)
        return m.reshape(-1, P, m.shape[1]).transpose(1, 0, 2).reshape(P, -1)

    flatT = lambda m: m.reshape(-1, m.shape[-1]).T
    vecs = np.concatenate([cols(g(n)) for n in ("attn_bq", "attn_bk", "attn_bg", "attn_gn_w", "attn_gn_b", "xattn_conv_w",
                                                "xattn_conv_b", "xattn_dt_proj_b", "xattn_D", "xattn_A_log")], axis=1)
    rows = np.stack([g("attn_bv"), g("attn_bk"), g("attn_bo")])
    wattn = np.concatenate([cols(g(n)) for n in ("attn_wq", "attn_wk", "attn_wv", "attn_wg", "attn_wo")], axis=1)
    wssm = np.concatenate([flatT(g("xattn_in_proj_w")), cols(flatT(g("xattn_x_proj_w")))], axis=1)
    lora = lambda m: m.transpose(0, 2, 1).reshape(E * R, -1)
    wff = np.concatenate([cols(m) for m in (
        flatT(g("ffn_A1")), flatT(g("ffn_A3")), flatT(g("ffn_W1")), flatT(g("ffn_W3")), lora(g("ffn_B1")), lora(g("ffn_B3")),
        flatT(g("ffn_A2")), flatT(g("ffn_W2")), lora(g("ffn_B2")))], axis=1)
    x = a["x"]
    arrays = {
        "x": x.reshape(B, NT, P, H).transpose(0, 2, 1, 3),
        "xT": x.transpose(0, 2, 1).reshape(B, 2, P, S).transpose(0, 2, 1, 3),
        "ctxT": a["ctx_1024"].transpose(0, 2, 1),
        "vec": vecs, "rows": rows, "gamma": g("attn_gamma").reshape(HEADS, 1), "wattn": wattn, "wssm": wssm,
        "wdt": flatT(g("xattn_dt_proj_w")), "wroute": cols(flatT(g("ffn_Wg"))), "wff": wff,
    }
    arrays = {"in_" + k: np.ascontiguousarray(v) for k, v in arrays.items()}
    nc = bacc.Bacc("TRN2", target_bir_lowering=False, num_devices=1)
    args = [nc.dram_tensor(k, v.shape, mybir.dt.from_np(v.dtype), kind="ExternalInput").ap() for k, v in arrays.items()]
    out = nc.dram_tensor("out_y", (B, P, NT, H), mybir.dt.float32, kind="ExternalOutput").ap()
    decoder_layer(nc, *args, out)
    got = run_bass_kernel_spmd(nc, [arrays], core_ids=[0]).results[0]["out_y"]
    return got.transpose(0, 2, 1, 3).reshape(B, S, H)
```

```python
import concourse.bass as bass
from concourse import mybir
from contextlib import ExitStack

B, S, H = 4, 256, 256
P = 128
NT, NH2 = S // P, H // P
HEADS, DH = 16, 16
GH = P // DH
DI, DS, DR, DC = 256, 16, 8, 4
E, R, F = 8, 32, 896
FM = F // P
EPS = 1e-5
NR = 2 * E + 4
UN = 2
UNITS = 2 * DS // UN
CONSTS = 20 + E

VEC = {}
_at = 0
for _n, _w in (("bq", 2), ("bk", 2), ("bg", 2), ("gnw", 2), ("gnb", 2), ("cw", 2 * DC), ("cb", 2),
               ("dtb", 2), ("D", 2), ("alog", 2 * DS)):
    VEC[_n] = (_at, _at + _w)
    _at += _w
NVEC = _at
FFW = {}
_at = 0
for _n, _w in (("A1", 2 * 256), ("A3", 2 * 256), ("A2", FM * 256), ("W2", FM * H), ("B2", 2 * H)):
    FFW[_n] = (_at, _at + _w)
    _at += _w
NFFW = _at
SPLIT = ("W1", "W3", "B1", "B3")
BLOCK = F // 2
BLOCKS = len(SPLIT) * 2 * F // BLOCK
PER_W = 2 * F // BLOCK
SPLIT_ORDER = list(range(2 * PER_W)) + list(range(3 * PER_W, 4 * PER_W)) + list(range(2 * PER_W, 3 * PER_W))
FF_PIECES = [("W1",), ("W3",), ("A1", "A3"), (), ("A2",), (), ("W2",), ("B2",)]

PER = dict(
    x_in=16, xn_in=16, ctx_in=16, bc_out=16, b_in0=64, b_in1=64, c_in0=64, c_in1=64, y_out=16,
    gen_filled=21,
    conv_in=3, conv_step=6, conv_tanh=1, u_ready=1, dbl_ready=1, dt_parts=4, dt_exp=1, dt_log=1, dt_step=4,
    du_ready=1, decay_ready=2 * DS, drive_ready=UNITS, state_ready=UNITS, out_ready=UNITS, part_ready=UNITS,
    y_init=2, y_part=UNITS, yT_ready=1,
    q_ready=2, qm_ready=6, qm_pool=2, qd_ready=1, k_ready=2, gate_lin=2, gate_tanh=1, gate_ready=1, v_ready=4, kd_ready=1,
    kv_ready=1, sc_ready=8, av_done=8, gn_step=12, gn_pow=1, ro_lin=2, ro_ready=1, xb_ready=1,
    r1_ready=7, r1_pow=1, r1_shift=1, r2_shift=1, x1_ready=2, z_tanh=1, r2_ready=8, r2_pow=1, x2_ready=2, x2T_ready=2,
    lg_ready=1, lg_exp=1, rt_step=24,
    xf_filled=20, a_filled=2, rtT_ready=1, mk_ready=2, rw_ready=1, keep_ready=1, mk1_ready=1,
    xl_ready=1, am_ready=4, amh_ready=4, aml_ready=2, aml_pool=2,
    th_ready=14, s_ready=14, q3_ready=14, xs_ready=14, xsum_ready=7, xs_used=14, xsum_used=7,
    a2_ready=3, down_done=1, r3_ready=7, r3_pow=1, y_ready=2,
)
GIVEN = ("xs_used", "xsum_used", "xsum_ready", "r3_ready", "a2_ready", "xs_ready", "s_ready", "q3_ready", "y_out")
READ = dict(IN=("conv_in", 3), Q=("q_ready", 2), K=("k_ready", 2), V=("v_ready", 4), DBL=("dbl_ready", 1),
            KN=("kd_ready", 1), DT=("dt_parts", 4), GATE=("gate_lin", 2), KV=("kv_ready", 1))
FIRST = ("IN", "Q", "DBL", "DT", "K", "V", "KN", "GATE", "KV")
LATER = ("IN", "Q", "K", "V", "DBL", "KN", "DT", "GATE", "KV")
GEN_END = [("sc_ready", i + 1) for i in range(8)] + [("gn_step", 6), ("gn_step", 9), ("r1_ready", 1), ("r2_ready", 2)]
G_SC = len(LATER)
(G_MEAN, G_VAR, G_OUT, G_Y) = range(G_SC + 8, G_SC + 12)


def order(b):
    return FIRST if isinstance(b, int) else LATER


MAIN = [(0, 0), (1, 0), (0, 1), (1, 1), (2, 0), (3, 0), (2, 1), (3, 1), (4, 0), (5, 0), (4, 1), (5, 1), (6, 0), (6, 1)]
XF = [("xl_ready", 1), ("lg_ready", 1), ("rtT_ready", 1), ("mk_ready", 1), ("mk_ready", 2), ("rw_ready", 1)] + [("q3_ready", n + 1) for n in range(len(MAIN))]
X_X2, X_LG, X_RT, X_MK, X_MD, X_RW, X_MAIN = range(7)
XF_BANK = [1, 0, 2, 0, 2, 0] + [(m + 1) % 2 for m, _ in MAIN]
SPLITS = {0: 0, 1: 2, 2: 4, 3: 6, 7: 8, 9: 10, 11: 12, 12: 14}
SCANS = [[0], [1], [2], [3, 4], [5], [6], [7], [8, 9], [10], [11, 12], [13, 14], [15], [], []]
PARTS = ((0, 0), (0, 1), (1, 0))
POOL_MASKED = (2, 3)
AM_ORDER = [0, 2, 1, 3]
LAG = 2


def decoder_layer(nc, x, xT, ctxT, vec, rows, gamma, wattn, wssm, wdt, wroute, wff, wsp, out):
    f32 = mybir.dt.float32
    f32r = mybir.dt.float32r
    ALU = mybir.AluOpType
    ACT = mybir.ActivationFunctionType
    AX = mybir.AxisListType

    with ExitStack() as ctx:
        def sb(name, *shape, dtype=f32):
            return ctx.enter_context(nc.sbuf_tensor(name, list(shape), dtype))

        def ps(name, *shape):
            return ctx.enter_context(nc.psum_tensor(name, list(shape), f32))

        pow_dram = nc.dram_tensor("pow_dram", (HEADS, P, 2 * P), f32, kind="Internal").ap()
        bc_dram = nc.dram_tensor("bc_dram", (B, 2 * DS, S), f32, kind="Internal").ap()

        vec_sb = sb("vec_sb", P, NVEC)
        rows_sb = sb("rows_sb", P, 2, H)
        bv_row, bo_row = (rows_sb[:, i, :] for i in range(2))
        wattn_sb = sb("wattn_sb", P, 5, 2, H)
        wq, wk, wv, wg, wo = (wattn_sb[:, i] for i in range(5))
        wssm_sb = sb("wssm_sb", P, DI + 2 * (DR + 2 * DS))
        w_in = wssm_sb[:, 0:DI]
        w_xp = wssm_sb[:, DI:].rearrange("p (j r) -> p j r", j=2)
        wdt_sb = sb("wdt_sb", DR, DI)
        wroute_sb = sb("wroute_sb", P, 2, E)
        wff_sb = sb("wff_sb", P, NFFW)

        def ffw(name, t):
            a, b_ = FFW[name]
            return wff_sb[:, a:b_].rearrange("p (t n) -> p t n", t=t)

        A1, A3, B2 = (ffw(n, 2) for n in ("A1", "A3", "B2"))
        A2, W2 = ffw("A2", FM), ffw("W2", FM)

        def v_(name):
            a, b_ = VEC[name]
            return vec_sb[:, a:b_]

        wsplit = sb("wsplit", P, 2, len(SPLIT), 2, F, dtype=f32r)

        ident = sb("ident", P, P)
        headblk = sb("headblk", P, P)
        headavg = sb("headavg", P, P)
        bgh = sb("bgh", P, 2)
        cwh = sb("cwh", P, 2, DC)
        cbh = sb("cbh", P, 2)
        nega = sb("nega", P, 2, DS)
        slots8 = sb("slots8", P, E)
        mhalf = sb("mhalf", P, 2)
        gamma_sb = sb("gamma_sb", HEADS, 1)
        dmask = sb("dmask", P, HEADS, P)
        qdec = sb("qdec", P, 2, P)

        ctx_sb = sb("ctx_sb", P, S)
        xpad = sb("xpad", P, 2, S + DC - 1)
        cv = sb("cv", P, 2, S)
        u = sb("u", P, 2, S)
        dbl = sb("dbl", DR + 2 * DS, S)
        yT = sb("yT", P, 2, S)
        dt_abs = yT
        dt_w = sb("dt_w", P, 2, S)
        dt_ln = dt_abs
        delta = dt_w
        du = cv
        brow = sb("brow", P, 2, UN, S)
        crow = sb("crow", P, 2, UN, S)
        decay = sb("decay", P, 2, UN, S)
        drive = sb("drive", P, 2, UN, S)
        state = sb("state", P, UN, S)
        part = sb("part", P, 2, S)
        dt_pos = part
        dt_e = drive[:, 1]
        cth = drive[:, 1]

        xT_sb = sb("xT_sb", P, 2, S)
        xn_sb = sb("xn_sb", P, NT, H)
        q_sb = sb("q_sb", P, 2, S)
        qm = sb("qm", P, 2, 4, P)
        qd = sb("qd", P, 2, P)
        kT = sb("kT", P, 2, S)
        fth = sb("fth", P, 2, S)
        glin = fth
        gth = sb("gth", P, 2, S)
        gate = gth
        vpad = sb("vpad", P, NT, 2, H)
        kv = sb("kv", P, 2, P)
        sc = sb("sc", P, 2, 4, P)
        kd = sc[:, 0, 0:2].rearrange("p a i -> p (a i)")
        gst = sb("gst", P, 2, 6)
        gmv = sb("gmv", P, 2, 2)
        geps = sb("geps", P, 2, 2)
        gdev = sb("gdev", P, 2)
        gavg = sb("gavg", P, 2, 2)
        gsq = sb("gsq", P, 2)
        gvar = sb("gvar", P, 2)
        grs = sb("grs", P, 2)
        gscale = sb("gscale", P, 2)
        gms = sb("gms", P, 2)
        gshift = sb("gshift", P, 2)
        rlin = kT
        ro = rlin
        xb = xn_sb
        r1 = dt_w
        st = sb("st", P, NT, 6)
        ve = sb("ve", P, NT)
        mv = sb("mv", P, NT, 2)
        rs = sb("rs", P, NT)
        nm = sb("nm", P, NT)
        x1 = q_sb
        zth = rlin
        zs = zth
        r2 = r1
        x2 = sb("x2", P, NT, H)
        x2s = sb("x2s", P, 2, 2, S, dtype=f32r)

        lg = sb("lg", P, NT, E)
        le = sb("le", P, NT, E)
        pr = sb("pr", P, NT, E)
        eq = sb("eq", P, NT, E)
        mk1 = sb("mk1", P, NT, E)
        rt = sb("rt", P, NT, NR)
        mk0, md, rwh, rwl = rt[:, :, 0:E], rt[:, :, E:2 * E], rt[:, :, 2 * E:2 * E + 2], rt[:, :, 2 * E + 2:]
        rw = sb("rw", P, NT, 2)
        rwr = sb("rwr", P, NT, 2, dtype=f32r)
        rtT = sb("rtT", NR, S, dtype=f32r)
        spreadw = sb("spreadw", NR, 6, P, dtype=f32r)
        t1 = sb("t1", P, NT)
        t2 = sb("t2", P, NT)
        top = sb("top", P, NT, 2)

        keep = sb("keep", P, NT, H)
        powrow = keep[0:HEADS, 0]
        work = sb("work", P, 14 * S)
        raw = [work[:, i * 2 * F:(i + 1) * 2 * F] for i in range(2)]
        spread_raw = work[0:NR, 4 * 2 * S:4 * 2 * S + 6 * P]
        tiles = lambda i, n: work[:, 2 * S * i:2 * S * (i + n)]
        xs = tiles(0, 2).rearrange("p (n t) -> p n t", n=4)
        a2m = tiles(2, 2).rearrange("p (k n t) -> p k n t", k=2, n=2)
        am_full = tiles(0, 4).rearrange("p (k n t) -> p k n t", k=4, n=2)
        mkT = tiles(4, 2).rearrange("p (k n t) -> p k n t", k=2, n=2)
        fq = tiles(6, 1).rearrange("p (n t) -> p n t", n=2)
        x2T = fq
        rwT = sb("rwT", P, 2, S)
        am = sb("am", P, 2, 4, 2, S, dtype=f32r)
        fs = fth
        xsum = sb("xsum", P, 2, S)
        r3 = keep
        st3 = sb("st3", P, NT, 6)
        ve3 = sb("ve3", P, NT)
        mv3 = sb("mv3", P, NT, 2)
        rs3 = sb("rs3", P, NT)
        yo = keep

        gen = [ps(f"gen{i}", P, 512) for i in range(2)]
        xf = [ps(f"xf{i}", P, 2, S) for i in range(2)]
        a2p = [ps(f"a2p{i}", P, 2, S) for i in range(2)]
        ret = ps("ret", P, 2, S)
        acc = ps("acc", P, 2, S)
        xf.append(acc)

        wflat = wsplit[:].rearrange("p q w t f -> p q w (t f)")

        sem = {n: ctx.enter_context(nc.semaphore(n)) for n in PER}
        for n in ("w_vec", "w_rows", "w_gamma", "w_attn", "w_ssm", "w_dt", "w_route", "w_ff", "pow_out", "mask_in",
                  "pool_const", "dve_const", "act_const", "pow_step", "spread_const", "w_raw0", "w_raw1", "w_high", "w_low", "w_low_b3"):
            sem[n] = ctx.enter_context(nc.semaphore(n))
        block = ctx.enter_context(nc.Block())

        def need(eng, name, b, n):
            value = b * PER[name] + n
            if not (isinstance(value, int) and value == 0):
                eng.wait_ge(sem[name], value + (name in GIVEN))


        def of(ap, b):
            return ap[b] if isinstance(b, int) else ap[bass.ds(b, 1)].squeeze(0)

        def v3(ap, n):
            return ap.rearrange("p (t n) -> p t n", n=n)

        def batches(eng, stage):
            stage(0, None)
            with eng.Fori(1, B) as b:
                stage(b, b - 1)
            stage(None, B - 1)

        @block.sync
        def _(sp):
            for name in GIVEN:
                sp.sem_inc(sem[name], 1)
            sp.dma_start(vec_sb[:], vec).then_inc(sem["w_vec"], 16)
            sp.dma_start(ctx_sb[:], ctxT[0]).then_inc(sem["ctx_in"], 16)
            sp.dma_start(wssm_sb[:], wssm).then_inc(sem["w_ssm"], 16)
            sp.dma_start(gamma_sb[:], gamma).then_inc(sem["w_gamma"], 16)
            sp.dma_start(wdt_sb[:], wdt).then_inc(sem["w_dt"], 16)
            sp.dma_start(xT_sb[:], xT[0]).then_inc(sem["x_in"], 16)
            sp.dma_start(wattn_sb[:], wattn).then_inc(sem["w_attn"], 16)
            sp.dma_start(rows_sb[:], rows.partition_broadcast(P)).then_inc(sem["w_rows"], 16)
            sp.dma_start(xn_sb[:], x[0]).then_inc(sem["xn_in"], 16)
            sp.wait_ge(sem["pow_step"], 9)
            sp.dma_start(pow_dram, powrow.unsqueeze(1).broadcast_to([HEADS, P, 2 * P])).then_inc(sem["pow_out"], 16)

            def masks():
                sp.wait_ge(sem["pow_out"], 16)
                sp.dma_start(dmask[:], bass.AP(tensor=pow_dram.tensor, offset=P - 1,
                                               ap=[[2 * P - 1, P], [2 * P * P, HEADS], [1, P]])).then_inc(sem["mask_in"], 16)
                for t in range(2):
                    sp.dma_start(qdec[:, t], bass.AP(tensor=pow_dram.tensor, offset=t * GH * 2 * P * P + P,
                                                     ap=[[2 * P * P, GH], [2 * P, DH], [1, P]])).then_inc(sem["mask_in"], 16)
                sp.dma_start(wroute_sb[:], wroute).then_inc(sem["w_route"], 16)

            def feed_forward_weights(piece):
                for name in FF_PIECES[piece]:
                    if name in SPLIT:
                        i = SPLIT.index(name)
                        if i == 1:
                            sp.wait_ge(sem["spread_const"], 1)
                        sp.dma_start(raw[i % 2], wsp[i]).then_inc(sem[f"w_raw{i % 2}"], 16)
                    else:
                        a, z = FFW[name]
                        sp.dma_start(wff_sb[:, a:z], wff[:, a:z]).then_inc(sem["w_ff"], 16)

            def spread(b):
                need(sp, "dbl_ready", b, 1)
                sp.dma_start(of(bc_dram, b), dbl[DR:, :]).then_inc(sem["bc_out"], 16)
                if isinstance(b, int) and b == 0:
                    feed_forward_weights(0)
                need(sp, "bc_out", b, 16)
                for c in range(DS // UN):
                    need(sp, "drive_ready", b, max(2 * c - 2, 0))
                    sp.dma_start(brow[:, c % 2], of(bc_dram, b)[c * UN:(c + 1) * UN].partition_broadcast(P)
                                 ).then_inc(sem[f"b_in{c % 2}"], 16)
                    need(sp, "out_ready", b, max(2 * c - 2, 0))
                    sp.dma_start(crow[:, c % 2], of(bc_dram, b)[DS + c * UN:DS + (c + 1) * UN].partition_broadcast(P)
                                 ).then_inc(sem[f"c_in{c % 2}"], 16)
                    if isinstance(b, int) and b == 0:
                        if c == 0:
                            masks()
                        else:
                            feed_forward_weights(c)

            def reload(b):
                need(sp, "gen_filled", b - 1, LATER.index("IN") + 1)
                sp.dma_start(ctx_sb[:], of(ctxT, b)).then_inc(sem["ctx_in"], 16)
                need(sp, "gen_filled", b - 1, LATER.index("GATE") + 1)
                sp.dma_start(xT_sb[:], of(xT, b)).then_inc(sem["x_in"], 16)
                need(sp, "r1_ready", b - 1, 1)
                sp.dma_start(xn_sb[:], of(x, b)).then_inc(sem["xn_in"], 16)

            def store(fb):
                need(sp, "y_ready", fb, 2)
                sp.dma_start(of(out, fb), yo[:]).then_inc(sem["y_out"], 16)

            spread(0)
            reload(1)
            with sp.Fori(1, B - 1) as b:
                spread(b)
                reload(b + 1)
                store(b - 1)
            spread(B - 1)
            store(B - 2)
            store(B - 1)
            need(sp, "y_out", B, 0)

        @block.gpsimd
        def _(pool):
            pc = sem["pool_const"]
            pool.memset(powrow, 0.0).then_inc(sem["pow_step"], 1)
            pool.memset(xpad[:], 0.0).then_inc(pc, 1)
            pool.memset(ident[:], 0.0).then_inc(pc, 1)
            pool.memset(headblk[:], 1.0).then_inc(pc, 1)
            pool.memset(mhalf[:], -0.5).then_inc(pc, 1)
            pool.memset(decay[:], 0.0).then_inc(pc, 1)
            pool.wait_ge(pc, 5)
            pool.affine_select(out=ident[:], in_=ident[:], compare_op=ALU.not_equal, fill=1.0, base=0,
                               pattern=[[-1, P]], channel_multiplier=1).then_inc(pc, 1)
            blk = headblk[:].rearrange("p (g r) -> p g r", r=DH)
            pool.affine_select(out=blk, in_=blk, compare_op=ALU.is_ge, fill=0.0, base=0,
                               pattern=[[-DH, GH], [0, DH]], channel_multiplier=1).then_inc(pc, 1)
            pool.memset(spread_raw, 0.0).then_inc(pc, 1)
            pool.wait_ge(pc, 8)
            pool.affine_select(out=blk, in_=blk, compare_op=ALU.is_ge, fill=0.0, base=DH - 1,
                               pattern=[[DH, GH], [0, DH]], channel_multiplier=-1).then_inc(pc, 1)
            pool.memset(vpad[:], 0.0).then_inc(pc, 1)
            pool.memset(geps[:], 0.0).then_inc(pc, 1)
            for e_ in range(E):
                pool.memset(slots8[:, e_:e_ + 1], float(E - e_)).then_inc(pc, 1)
            for i in range(8):
                view = spread_raw[:, min(i, 2 + i % 2 + 2) * P:(min(i, 2 + i % 2 + 2) + 1) * P].rearrange("q (e r) -> q e r", r=R)
                step, base = (-1, -(E * (i // 2) + 4 * (i % 2))) if i < 4 else (0, -(2 * E + i - 4))
                if i == 6:
                    pool.wait_ge(pc, 17 + E)
                pool.affine_select(out=view, in_=view, compare_op=ALU.not_equal, fill=1.0, base=base,
                                   pattern=[[step, 4], [0, R]], channel_multiplier=1).then_inc(pc, 1)
            pool.wait_ge(pc, 19 + E)
            pool.tensor_scalar_mul(headavg[:], headblk[:], 1.0 / DH).then_inc(pc, 1)

            def drive_unit(b, i):
                j, c = i % 2, i // 2
                if i == 0:
                    need(pool, "du_ready", b, 1)
                if j == 0:
                    need(pool, f"b_in{c % 2}", b, 16 * (c // 2 + 1))
                need(pool, "state_ready", b, max(i - 1, 0))
                pool.tensor_tensor(drive[:, i % 2], du[:, j].unsqueeze(1).broadcast_to([P, UN, S]),
                                   brow[:, c % 2], ALU.mult).then_inc(sem["drive_ready"], 1)

            def add_part(b, i):
                j = i % 2
                if i == 0:
                    need(pool, "y_init", b, 2)
                need(pool, "part_ready", b, i + 1)
                if i >= 2:
                    need(pool, "y_part", b, i - 1)
                pool.tensor_tensor(yT[:, j], yT[:, j], part[:, i % 2], ALU.add).then_inc(sem["y_part"], 1)

            def split_low(blocks):
                for k in blocks:
                    w, c = SPLIT_ORDER[k] // PER_W, SPLIT_ORDER[k] % PER_W
                    cs = slice(c * BLOCK, (c + 1) * BLOCK)
                    pool.wait_ge(sem["w_high"], k + 1)
                    pool.tensor_tensor(wflat[:, 1, w, cs], raw[w % 2][:, cs], wflat[:, 0, w, cs], ALU.subtract
                                       ).then_inc(sem["w_low"], 1)

            def bias(b):
                need(pool, "q_ready", b, 2)
                if isinstance(b, int):
                    pool.wait_ge(sem["mask_in"], 48)
                    pool.wait_ge(sem["w_rows"], 16)
                pool.tensor_tensor(qd[:], q_sb[:, :, P:], qdec[:], ALU.mult).then_inc(sem["qd_ready"], 1)
                need(pool, "xn_in", b, 16)
                pool.tensor_tensor(xb[:], xn_sb[:], bo_row.unsqueeze(1).broadcast_to([P, NT, H]), ALU.add
                                   ).then_inc(sem["xb_ready"], 1)

            def root(b, src, dst, ready, n, done):
                need(pool, ready, b, n)
                pool.tensor_tensor(dst[:], src[:], mhalf[:], ALU.pow).then_inc(sem[done], 1)

            def masked(b, i):
                t, chunk, h0 = i // 4, i % 2, 4 * (i // 2 % 2)
                need(pool, "gen_filled", b, G_SC + i - 1)
                pool.tensor_tensor(qm[:, i % 2], q_sb[:, t, chunk * P:(chunk + 1) * P].unsqueeze(1).broadcast_to([P, 4, P]),
                                   headblk[:].rearrange("p (h d) -> p h d", d=DH)[:, h0:h0 + 4, 0:1].broadcast_to([P, 4, P]),
                                   ALU.mult).then_inc(sem["qm_pool"], 1)

            def stage(b, fb):
                if b is not None and not isinstance(b, int):
                    bias(b)
                if b is not None:
                    need(pool, "dt_step", b, 4)
                    pool.tensor_tensor(du[:], delta[:], u[:], ALU.mult).then_inc(sem["du_ready"], 1)
                    drive_unit(b, 0)
                    drive_unit(b, 1)
                    if fb is not None:
                        for i in POOL_MASKED:
                            masked(b, i)
                if fb is not None:
                    need(pool, "am_ready", fb, 4)
                    pool.tensor_tensor(mkT[:, 1], mkT[:, 0], mkT[:, 1], ALU.add).then_inc(sem["mk1_ready"], 1)
                    for i in (2, 3):
                        need(pool, "amh_ready", fb, i + 1)
                        slot = AM_ORDER[i]
                        pool.tensor_tensor(am[:, 1, slot], am_full[:, slot], am[:, 0, slot], ALU.subtract
                                           ).then_inc(sem["aml_pool"], 1)
                for n, (m, k) in enumerate(MAIN):
                    if b is not None:
                        if n == 7:
                            root(b, gvar, grs, "gn_step", 9, "gn_pow")
                        if n == 8:
                            need(pool, "ro_lin", b, 2)
                            need(pool, "gate_ready", b, 1)
                            pool.tensor_tensor(ro[:], rlin[:], gate[:], ALU.mult).then_inc(sem["ro_ready"], 1)
                        if n == 11:
                            root(b, ve, rs, "r1_ready", 7, "r1_pow")
                        for i in SCANS[n]:
                            if i + 2 < UNITS:
                                drive_unit(b, i + 2)
                            if n == 0 and fb is None:
                                bias(b)
                                for k_ in POOL_MASKED:
                                    masked(b, k_)
                            if fb is not None and n != 11:
                                add_part(b, i)
                        if fb is None and n - 1 in SPLITS and SPLITS[n - 1] < 2 * PER_W:
                            split_low(range(SPLITS[n - 1], SPLITS[n - 1] + 2))
                    if fb is not None:
                        need(pool, "q3_ready", fb, n + 1)
                        if n == 0:
                            need(pool, "rw_ready", fb, 1)
                        need(pool, "xs_used", fb, max(n - 3, 0))
                        need(pool, "xsum_ready", fb, MAIN[n - 4][0] + 1 if n >= 4 else 0)
                        pool.tensor_tensor(xs[:, n % 4], fq[:, n % 2], rwT[:, k], ALU.mult).then_inc(sem["xs_ready"], 1)
                    if fb is not None:
                        if k == 1:
                            first = MAIN.index((m, 0))
                            need(pool, "xs_ready", fb, n + 1)
                            need(pool, "xsum_used", fb, max(m - 1, 0))
                            pool.tensor_tensor(xsum[:, m % 2], xs[:, first % 4], xs[:, n % 4], ALU.add
                                               ).then_inc(sem["xsum_ready"], 1)
                        if b is not None and n == 11:
                            add_part(b, UNITS - 1)
                    if b is not None and n == 13:
                        root(b, ve, rs, "r2_ready", 8, "r2_pow")
                        if fb is None:
                            split_low(range(3 * PER_W, BLOCKS))
                if fb is not None:
                    root(fb, ve3, rs3, "r3_ready", 7, "r3_pow")

            pool.wait_ge(pc, CONSTS)
            batches(pool, stage)

        @block.scalar
        def _(act):
            act.wait_ge(sem["w_vec"], 16)
            act.activation(nega[:], v_("alog").rearrange("p (j n) -> p j n", j=2), ACT.Exp).then_inc(sem["act_const"], 1)
            act.wait_ge(sem["dve_const"], 4)
            act.wait_ge(sem["pool_const"], 1)

            def decays(b, i):
                j, c = i % 2, i // 2
                if i == 0:
                    need(act, "dt_step", b, 4)
                need(act, "state_ready", b, max(i - 1, 0))
                for n in range(UN):
                    s_ = c * UN + n
                    act.activation(decay[:, i % 2, n, 1:], delta[:, j, 1:], ACT.Exp, scale=nega[:, j, s_:s_ + 1]
                                   ).then_inc(sem["decay_ready"], 1)

            def bank(b, name):
                i = order(b).index(name)
                need(act, "gen_filled", b, i + 1)
                return v3(gen[i % 2][:], S)

            def conv_input(b):
                g = bank(b, "IN")
                act.activation(xpad[:, :, DC - 1:], g, ACT.Copy).then_inc(sem["conv_in"], 1)
                for j in range(2):
                    act.activation(cv[:, j], g[:, j], ACT.Identity, bias=cbh[:, j:j + 1],
                                   scale=cwh[:, j, DC - 1:DC]).then_inc(sem["conv_in"], 1)

            def conv_tanh(b):
                need(act, "conv_step", b, 6)
                act.activation(cth, cv[:], ACT.Tanh).then_inc(sem["conv_tanh"], 1)

            def queries(b):
                g = bank(b, "Q")
                need(act, "qd_ready", b, 0)
                for t in range(2):
                    act.activation(q_sb[:, t], g[:, t], ACT.Identity, bias=v_("bq")[:, t:t + 1]).then_inc(sem["q_ready"], 1)

            def keys(b):
                g = bank(b, "K")
                for t in range(2):
                    act.activation(kT[:, t], g[:, t], ACT.Identity, bias=v_("bk")[:, t:t + 1]).then_inc(sem["k_ready"], 1)

            def low_rank(b):
                g = bank(b, "DBL")
                need(act, "bc_out", b, 0)
                act.activation(dbl[:], g[0:DR + 2 * DS, 0], ACT.Copy).then_inc(sem["dbl_ready"], 1)

            def positive(b, g):
                for j in range(2):
                    act.activation(dt_pos[:, j], g[:, j], ACT.Relu, bias=v_("dtb")[:, j:j + 1]).then_inc(sem["dt_parts"], 1)

            def softplus(b):
                g = bank(b, "DT")
                for j in range(2):
                    act.activation(dt_abs[:, j], g[:, j], ACT.Abs, bias=v_("dtb")[:, j:j + 1]).then_inc(sem["dt_parts"], 1)
                if isinstance(b, int):
                    positive(b, g)
                need(act, "dt_parts", b, 2)
                act.activation(dt_e, dt_abs[:], ACT.Exp, scale=-1.0).then_inc(sem["dt_exp"], 1)
                need(act, "dt_exp", b, 1)
                act.activation(dt_ln[:], dt_e, ACT.Ln, bias=1.0).then_inc(sem["dt_log"], 1)
                if not isinstance(b, int):
                    positive(b, g)

            def gate_linear(b):
                g = bank(b, "GATE")
                for t in range(2):
                    act.activation(glin[:, t], g[:, t], ACT.Identity, bias=bgh[:, t:t + 1], scale=0.5
                                   ).then_inc(sem["gate_lin"], 1)

            def gate_tanh(b):
                need(act, "gate_lin", b, 2)
                act.activation(gth[:], glin[:], ACT.Tanh).then_inc(sem["gate_tanh"], 1)

            def start_y(b):
                for j in range(2):
                    act.activation(yT[:, j], u[:, j], ACT.Copy, scale=v_("D")[:, j:j + 1]).then_inc(sem["y_init"], 1)

            def normed(b, src, dst, ready, done):
                need(act, ready, b, 1)
                for t in range(NT):
                    act.activation(dst[:, t], src[:, t], ACT.Identity, bias=nm[:, t:t + 1], scale=rs[:, t:t + 1]
                                   ).then_inc(sem[done], 1)

            def am_high(fb, which):
                for i in which:
                    need(act, "am_ready", fb, i + 1)
                    act.activation(am[:, 0, AM_ORDER[i]], am_full[:, AM_ORDER[i]], ACT.Copy).then_inc(sem["amh_ready"], 1)

            def masked(b, i):
                t, chunk = i // 4, i % 2
                need(act, "gen_filled", b, G_SC + i - 1 if i >= 2 else 0)
                if i == 0:
                    need(act, "q_ready", b, 2)
                for h in range(4):
                    row = DH * (4 * (i // 2 % 2) + h)
                    last = act.activation(qm[:, i % 2, h], q_sb[:, t, chunk * P:(chunk + 1) * P], ACT.Copy,
                                          scale=headblk[:, row:row + 1])
                last.then_inc(sem["qm_ready"], 1)

            def split_high(blocks):
                for k in blocks:
                    w, c = SPLIT_ORDER[k] // PER_W, SPLIT_ORDER[k] % PER_W
                    cs = slice(c * BLOCK, (c + 1) * BLOCK)
                    if c == 0:
                        act.wait_ge(sem[f"w_raw{w % 2}"], 16 * (w // 2 + 1))
                    act.activation(wflat[:, 0, w, cs], raw[w % 2][:, cs], ACT.Copy).then_inc(sem["w_high"], 1)

            def first(b):
                conv_input(b)
                conv_tanh(b)
                queries(b)
                low_rank(b)
                softplus(b)
                keys(b)
                act.wait_ge(sem["pool_const"], CONSTS)
                decays(b, 0)
                decays(b, 1)
                gate_linear(b)
                gate_tanh(b)
                masked(b, 0)
                masked(b, 1)
                start_y(b)
                act.activation(spreadw[:].rearrange("q i p -> q (i p)"), spread_raw, ACT.Copy).then_inc(sem["spread_const"], 1)

            def later(b, fb):
                if b is not None:
                    conv_input(b)
                    queries(b)
                if fb is not None:
                    need(act, "xf_filled", fb, X_X2 + 1)
                    need(act, "xs_ready", fb, 0)
                    act.wait_ge(sem["w_low_b3"], PER_W)
                    act.activation(x2T, xf[XF_BANK[X_X2]][:], ACT.Copy).then_inc(sem["x2T_ready"], 1)
                    act.activation(x2s[:, 0], xf[XF_BANK[X_X2]][:], ACT.Copy).then_inc(sem["x2T_ready"], 1)
                if b is not None:
                    conv_tanh(b)
                    keys(b)
                    masked(b, 0)
                if fb is not None:
                    need(act, "rt_step", fb, 2)
                    act.activation(le[:], lg[:], ACT.Exp).then_inc(sem["lg_exp"], 1)
                if b is not None:
                    low_rank(b)
                    softplus(b)
                    masked(b, 1)
                    gate_linear(b)
                need(act, "xf_filled", fb, X_RT + 1)
                act.activation(rtT[:], xf[XF_BANK[X_RT]][0:NR, 0], ACT.Copy).then_inc(sem["rtT_ready"], 1)
                need(act, "a2_ready", fb, 0)
                for i in range(2):
                    need(act, "xf_filled", fb, X_MK + i + 1)
                    act.activation(mkT[:, i], xf[XF_BANK[X_MK + i]][:], ACT.Copy).then_inc(sem["mk_ready"], 1)
                need(act, "xf_filled", fb, X_RW + 1)
                need(act, "xs_ready", fb, 0)
                act.activation(rwT[:], xf[XF_BANK[X_RW]][:], ACT.Copy).then_inc(sem["rw_ready"], 1)
                am_high(fb, (0, 1))
                if b is not None:
                    gate_tanh(b)
                    decays(b, 0)
                am_high(fb, (2, 3))
                if b is not None:
                    decays(b, 1)

            def stage(b, fb):
                if fb is None:
                    first(b)
                else:
                    later(b, fb)
                for n in range(len(MAIN)):
                    if fb is not None:
                        need(act, "xf_filled", fb, X_MAIN + n + 1)
                        need(act, "s_ready", fb, max(n - 1, 0))
                        if n == 0 and b is not None:
                            need(act, "gate_ready", b, 1)
                        act.activation(fth[:, n % 2], xf[XF_BANK[X_MAIN + n]][:, 0], ACT.Tanh, scale=0.5
                                       ).then_inc(sem["th_ready"], 1)
                    if b is not None:
                        if n in (1, 2):
                            masked(b, 2 * n + 2)
                            masked(b, 2 * n + 3)
                        if n == 0 and fb is not None:
                            start_y(b)
                        for i in SCANS[n]:
                            if i + 2 < UNITS:
                                decays(b, i + 2)
                        if n == 7:
                            need(act, "gn_step", b, 12)
                            for t in range(2):
                                act.activation(rlin[:, t], ret[:, t], ACT.Identity, bias=gshift[:, t:t + 1],
                                               scale=gscale[:, t:t + 1]).then_inc(sem["ro_lin"], 1)
                        if fb is None and n in SPLITS:
                            split_high(range(SPLITS[n], SPLITS[n] + 2))
                        if fb is None and SPLITS.get(n - 2, -1) + 2 in (PER_W, 2 * PER_W):
                            k = SPLITS[n - 2] + 2
                            act.wait_ge(sem["w_low"], k)
                            i = k // PER_W + 1
                            act.dma_start(raw[i % 2], wsp[i]).then_inc(sem[f"w_raw{i % 2}"], 16)
                        if n == 12:
                            normed(b, r1, x1, "r1_shift", "x1_ready")
                            need(act, "x1_ready", b, 2)
                            act.activation(zth[:], x1[:], ACT.Tanh, scale=0.5).then_inc(sem["z_tanh"], 1)
                    if fb is not None and n == 4:
                        need(act, "r3_ready", fb, 0)
                        need(act, "y_out", fb, 0)
                        act.activation(keep[:], x2[:], ACT.Copy).then_inc(sem["keep_ready"], 1)
                if b is not None:
                    need(act, "keep_ready", b, 0)
                    normed(b, r2, x2, "r2_shift", "x2_ready")

            batches(act, stage)

        @block.tensor
        def _(pe):
            def mm(o, l, r, **kw):
                return pe.matmul(o, l, r, skip_group_check=True, **kw)

            def gen_free(b, i):
                readers = [READ[name] for name in order(b)] + GEN_END
                if i >= 2:
                    name, n = readers[i - 2]
                    need(pe, name, b, n)
                else:
                    last = max(k for k in range(len(readers)) if k % 2 == i % 2)
                    need(pe, readers[last][0], b, 0)

            def xf_free(fb, i):
                before = [k for k in range(i) if XF_BANK[k] == XF_BANK[i]]
                if before:
                    name, n = XF[before[-1]]
                    need(pe, name, fb, n)
                else:
                    need(pe, ("q3_ready", "q3_ready", "r3_ready")[XF_BANK[i]], fb, 0)

            def gen_bank(b, name, n):
                i = order(b).index(name)
                gen_free(b, i)
                return v3(gen[i % 2][:], n)

            def project(b, name, w):
                g = gen_bank(b, name, S)
                for t in range(2):
                    for k in range(2):
                        last = mm(g[:, t], w[:, k, t * P:(t + 1) * P], xT_sb[:, k], start=(k == 0), stop=(k == 1))
                last.then_inc(sem["gen_filled"], 1)

            def context(b):
                need(pe, "ctx_in", b, 16)
                g = gen_bank(b, "IN", S)
                for j in range(2):
                    last = mm(g[:, j], w_in[:, j * P:(j + 1) * P], ctx_sb[:], start=True, stop=True)
                last.then_inc(sem["gen_filled"], 1)

            def low_rank(b):
                g = gen_bank(b, "DBL", S)
                need(pe, "u_ready", b, 1)
                for j in range(2):
                    last = mm(g[0:DR + 2 * DS, 0], w_xp[:, j], u[:, j], start=(j == 0), stop=(j == 1))
                last.then_inc(sem["gen_filled"], 1)

            def step_size(b):
                g = gen_bank(b, "DT", S)
                need(pe, "dbl_ready", b, 1)
                for j in range(2):
                    last = mm(g[:, j], wdt_sb[:, j * P:(j + 1) * P], dbl[0:DR, :], start=True, stop=True)
                last.then_inc(sem["gen_filled"], 1)

            def token_values(b):
                g = gen_bank(b, "V", H)
                for t in range(NT):
                    for k in range(2):
                        last = mm(g[:, t], xT_sb[:, k, t * P:(t + 1) * P], wv[:, k], start=(k == 0), stop=(k == 1))
                last.then_inc(sem["gen_filled"], 1)

            def token_keys(b):
                g = gen_bank(b, "KN", H)
                need(pe, "k_ready", b, 2)
                for t in range(2):
                    last = pe.transpose(g[:, 0, t * P:(t + 1) * P], kT[:, t, 0:P], ident[:])
                last.then_inc(sem["gen_filled"], 1)

            def chunk_state(b):
                g = gen_bank(b, "KV", P)
                need(pe, "kd_ready", b, 1)
                need(pe, "v_ready", b, 4)
                for t in range(2):
                    for p_ in range(2):
                        last = mm(g[:, t], kd[:, t * P:(t + 1) * P], vpad[:, 0, p_, t * P:(t + 1) * P],
                                  start=(p_ == 0), stop=(p_ == 1))
                last.then_inc(sem["gen_filled"], 1)

            def add_states(b, i):
                need(pe, "out_ready", b, i + 1)
                terms = (state, part)[i % 2]
                mm(acc[:, i % 2], ident[:], terms[:, 0], start=(i == 0), stop=False).then_inc(sem["part_ready"], 1)
                mm(acc[:, i % 2], ident[:], terms[:, 1], start=False, stop=(i >= UNITS - 2)).then_inc(sem["y_part"], 1)

            def base(fb, n):
                m, k = MAIN[n]
                xf_free(fb, X_MAIN + n)
                if n == 0:
                    pe.wait_ge(sem["w_high"], BLOCKS)
                    pe.wait_ge(sem["w_low"], BLOCKS - PER_W)
                    pe.wait_ge(sem["w_low_b3"], PER_W)
                    need(pe, "xl_ready", fb, 1)
                for half in range(2):
                    for t in range(2):
                        for i, (wp, xp) in enumerate(PARTS):
                            mm(xf[XF_BANK[X_MAIN + n]][:, half], wsplit[:, wp, half, t, m * P:(m + 1) * P], x2s[:, xp, t],
                               start=(half == 0 and t == 0 and i == 0), stop=False)

            def hidden(fb, n, based):
                m, k = MAIN[n]
                if k == 1:
                    xf_free(fb, X_MAIN + n)
                o = xf[XF_BANK[X_MAIN + n]]
                fs_ = slice(m * P, (m + 1) * P)
                if k == 0 and not based:
                    base(fb, n)
                for half in range(2):
                    if n == 0:
                        need(pe, "aml_ready", fb, half + 1)
                    if n == 2:
                        need(pe, "aml_pool", fb, half + 1)
                    for t in range(2):
                        for wp, xp in PARTS:
                            last = mm(o[:, half], wsplit[:, wp, 2 + half, t, fs_], am[:, xp, 2 * half + k, t], start=False,
                                      stop=(t == 1 and wp == 1))
                last.then_inc(sem["xf_filled"], 1)

            def shrink(fb, n):
                m, k = MAIN[n]
                need(pe, "xs_ready", fb, n + 1)
                if n == 0:
                    need(pe, "am_ready", fb, 4)
                for t in range(2):
                    last = mm(a2p[k][:, t], A2[:, m, t * P:(t + 1) * P], xs[:, n % 4], start=(m == 0 and t == 0),
                              stop=(m == FM - 1))
                last.then_inc(sem["xs_used"], 1)
                if k == 1:
                    need(pe, "xsum_ready", fb, m + 1)
                    if m == 0:
                        need(pe, "r3_ready", fb, 0)
                    for t in range(NT):
                        last = mm(acc[:, t], xsum[:, m % 2, t * P:(t + 1) * P], W2[:, m], start=(m == 0 and t == 0),
                                  stop=False)
                    last.then_inc(sem["xsum_used"], 1)

            def spread_rows(fb, i):
                xf_free(fb, i)
                for t in range(2):
                    last = mm(xf[XF_BANK[i]][:, t], spreadw[:, 2 * (i - X_MK) + t], rtT[:], start=True, stop=True)
                last.then_inc(sem["xf_filled"], 1)

            def scores(b, i):
                t, chunk = i // 4, i % 2
                gen_free(b, G_SC + i)
                if i == 0:
                    need(pe, "k_ready", b, 2)
                if i in POOL_MASKED:
                    need(pe, "qm_pool", b, POOL_MASKED.index(i) + 1)
                else:
                    need(pe, "qm_ready", b, i + 1 - sum(k < i for k in POOL_MASKED))
                cs = slice(chunk * P, (chunk + 1) * P)
                mm(gen[(G_SC + i) % 2][:].rearrange("p (h i) -> p h i", h=4), kT[:, t, cs], qm[:, i % 2],
                   start=True, stop=True).then_inc(sem["gen_filled"], 1)

            def values(b, i):
                t, chunk, g = i // 4, i % 2, i // 2
                need(pe, "sc_ready", b, i + 1)
                if i == 0:
                    need(pe, "ro_lin", b, 0)
                    need(pe, "v_ready", b, 4)
                cs = slice(chunk * P, (chunk + 1) * P)
                for p_ in range(2):
                    for pair in range(2):
                        w = 2 * (g % 2) + pair
                        last = mm(ret[32 * w:32 * w + 32, t, cs], vpad[:, chunk, p_, t * P + 32 * w:t * P + 32 * w + 32],
                                  sc[:, i % 2, 2 * pair + p_], start=(t == 0 and chunk == 0 and p_ == 0),
                                  stop=(p_ == 1 and chunk == 0))
                if i % 4 == 3:
                    if i == 3:
                        need(pe, "kv_ready", b, 1)
                        need(pe, "qd_ready", b, 1)
                    last = mm(ret[:, t, P:], kv[:, t], qd[:, t], start=False, stop=True)
                last.then_inc(sem["av_done"], 1)

            def token_y(b):
                gen_free(b, G_Y)
                need(pe, "yT_ready", b, 1)
                g = v3(gen[G_Y % 2][:], H)
                for t in range(NT):
                    for j in range(2):
                        last = pe.transpose(g[:, t, j * P:(j + 1) * P], yT[:, j, t * P:(t + 1) * P], ident[:])
                last.then_inc(sem["gen_filled"], 1)

            def expert_inputs(half, w):
                for t in range(2):
                    for k in range(2):
                        last = mm(a2p[half][:, t], w[:, k, t * P:(t + 1) * P], x2T[:, k], start=(k == 0), stop=(k == 1))
                last.then_inc(sem["a_filled"], 1)

            def first(b):
                pe.wait_ge(sem["w_ssm"], 16)
                context(b)
                pe.wait_ge(sem["w_attn"], 16)
                need(pe, "x_in", b, 16)
                project(b, "Q", wq)
                low_rank(b)
                pe.wait_ge(sem["w_dt"], 16)
                step_size(b)
                project(b, "K", wk)
                token_values(b)
                pe.wait_ge(sem["pool_const"], CONSTS)
                token_keys(b)
                project(b, "GATE", wg)
                chunk_state(b)

            def later(b, fb):
                if b is not None:
                    context(b)
                    need(pe, "x_in", b, 16)
                    project(b, "Q", wq)
                xf_free(fb, X_X2)
                need(pe, "x2_ready", fb, 2)
                o = xf[XF_BANK[X_X2]]
                for t in range(NT):
                    for k in range(2):
                        last = pe.transpose(o[:, k, t * P:(t + 1) * P], x2[:, t, k * P:(k + 1) * P], ident[:])
                last.then_inc(sem["xf_filled"], 1)
                if b is not None:
                    project(b, "K", wk)
                xf_free(fb, X_LG)
                need(pe, "x2T_ready", fb, 1)
                pe.wait_ge(sem["w_route"], 16)
                for t in range(NT):
                    for k in range(2):
                        last = mm(xf[XF_BANK[X_LG]][:, 0, t * E:(t + 1) * E], x2T[:, k, t * P:(t + 1) * P], wroute_sb[:, k],
                                  start=(k == 0), stop=(k == 1))
                last.then_inc(sem["xf_filled"], 1)
                if b is not None:
                    token_values(b)
                    low_rank(b)
                    token_keys(b)
                pe.wait_ge(sem["w_ff"], 16 * len(FFW))
                need(pe, "a2_ready", fb, 0)
                expert_inputs(0, A1)
                if b is not None:
                    step_size(b)
                expert_inputs(1, A3)
                if b is not None:
                    project(b, "GATE", wg)
                base(fb, 0)
                xf_free(fb, X_RT)
                need(pe, "rt_step", fb, 24)
                for n in range(NT):
                    last = mm(xf[XF_BANK[X_RT]][0:NR, 0, n * P:(n + 1) * P], rt[:, n], ident[:], start=True, stop=True)
                last.then_inc(sem["xf_filled"], 1)
                if b is not None:
                    chunk_state(b)
                need(pe, "rtT_ready", fb, 1)
                spread_rows(fb, X_MK)
                spread_rows(fb, X_MD)
                if b is not None:
                    scores(b, 0)
                spread_rows(fb, X_RW)
                if b is not None:
                    scores(b, 1)
                else:
                    base(fb, 1)

            def stage(b, fb):
                if fb is None:
                    first(b)
                else:
                    later(b, fb)
                for n in range(len(MAIN)):
                    if fb is not None:
                        if n == len(MAIN) - 1:
                            shrink(fb, n - LAG)
                        hidden(fb, n, n == 0 or n == 1 and b is None)
                    if b is not None and 1 <= n <= 4:
                        values(b, 2 * n - 2)
                    if b is not None and n < 4 and (n > 0 or fb is None):
                        scores(b, 2 * n)
                    if fb is not None and n >= LAG:
                        shrink(fb, n - LAG + (n == len(MAIN) - 1))
                    if b is not None and n == len(MAIN) - 1:
                        token_y(b)
                    if b is not None:
                        if 1 <= n <= 4:
                            values(b, 2 * n - 1)
                        if n < 4 and (n > 0 or fb is None):
                            scores(b, 2 * n + 1)
                        if n == 5:
                            gen_free(b, G_MEAN)
                            need(pe, "gn_step", b, 5)
                            mm(gen[G_MEAN % 2][:, 0:4], headavg[:], gmv[:].rearrange("p t s -> p (t s)"), start=True, stop=True
                               ).then_inc(sem["gen_filled"], 1)
                        if n == 6:
                            gen_free(b, G_VAR)
                            need(pe, "gn_step", b, 8)
                            mm(gen[G_VAR % 2][:, 0:2], headavg[:], gsq[:], start=True, stop=True).then_inc(sem["gen_filled"], 1)
                        if fb is None:
                            for i in SCANS[n]:
                                add_states(b, i)
                        if n == 9:
                            gen_free(b, G_OUT)
                            need(pe, "ro_ready", b, 1)
                            g = v3(gen[G_OUT % 2][:], H)
                            for t in range(NT):
                                for k in range(2):
                                    last = mm(g[:, t], ro[:, k, t * P:(t + 1) * P], wo[:, k], start=(k == 0), stop=(k == 1))
                            last.then_inc(sem["gen_filled"], 1)
                if fb is not None:
                    shrink(fb, len(MAIN) - 1)
                    need(pe, "a2_ready", fb, 3)
                    for t in range(NT):
                        for k in range(2):
                            last = mm(acc[:, t], a2m[:, 0, k, t * P:(t + 1) * P], B2[:, k], start=False, stop=(k == 1))
                    last.then_inc(sem["down_done"], 1)

            batches(pe, stage)

        @block.vector
        def _(dve):
            dc = sem["dve_const"]
            dve.wait_ge(sem["w_gamma"], 16)
            dve.wait_ge(sem["pow_step"], 1)
            one = P - 1
            dve.memset(powrow[:, one:one + 1], 1.0)
            dve.tensor_copy(powrow[:, one + 1:one + 2], gamma_sb[:]).then_inc(sem["pow_step"], 1)
            known = 1
            while known < P:
                dve.wait_ge(sem["pow_step"], 2 + known.bit_length() - 1)
                dve.tensor_scalar(powrow[:, one + 1 + known:one + 1 + 2 * known], powrow[:, one + 1:one + 1 + known],
                                  powrow[:, one + known:one + known + 1], None, ALU.mult).then_inc(sem["pow_step"], 1)
                known *= 2
            dve.wait_ge(sem["w_vec"], 16)
            dve.tensor_scalar(bgh[:], v_("bg"), 0.5, None, ALU.mult).then_inc(dc, 1)
            dve.tensor_scalar(cwh[:].rearrange("p j k -> p (j k)"), v_("cw"), 0.5, None, ALU.mult).then_inc(dc, 1)
            dve.tensor_scalar(cbh[:], v_("cb"), 0.5, None, ALU.mult).then_inc(dc, 1)
            dve.wait_ge(sem["act_const"], 1)
            dve.tensor_scalar(nega[:], nega[:], -1.0, None, ALU.mult).then_inc(dc, 1)
            dve.wait_ge(dc, 4)

            def bank(b, i, n):
                if isinstance(i, str):
                    i = order(b).index(i)
                need(dve, "gen_filled", b, i + 1)
                return v3(gen[i % 2][:], n)

            def conv(b):
                need(dve, "conv_in", b, 3)
                for k in range(DC - 1):
                    for j in range(2):
                        i = 2 * k + j
                        if i >= 2:
                            need(dve, "conv_step", b, i - 1)
                        dve.scalar_tensor_tensor(cv[:, j], xpad[:, j, k:k + S], cwh[:, j, k:k + 1], cv[:, j],
                                                 ALU.mult, ALU.add).then_inc(sem["conv_step"], 1)
                need(dve, "conv_tanh", b, 1)
                dve.scalar_tensor_tensor(u[:], cth, 1.0, cv[:], ALU.add, ALU.mult).then_inc(sem["u_ready"], 1)

            def token_values(b):
                g = bank(b, "V", H)
                pairs = lambda ap: ap.rearrange("p (w a d) -> p w a d", a=2, d=DH)
                for t in range(NT):
                    for p_ in range(2):
                        dve.tensor_tensor(pairs(vpad[:, t, p_])[:, :, p_], pairs(g[:, t])[:, :, p_],
                                          pairs(bv_row)[:, :, p_], ALU.add).then_inc(sem["v_ready"], 1)

            def token_keys(b):
                g = bank(b, "KN", H)
                heads = lambda ap: ap.rearrange("p (h d) -> p h d", d=DH)
                dve.tensor_tensor(heads(kd), heads(g[:, 0]), dmask[:, :, P - 1:P].broadcast_to([P, HEADS, DH]), ALU.mult
                                  ).then_inc(sem["kd_ready"], 1)

            def step_size(b):
                need(dve, "dt_exp", b, 1)
                dve.tensor_scalar(dt_w[:], dt_e, 1.0, -1.0, ALU.add, ALU.add).then_inc(sem["dt_step"], 1)
                need(dve, "dt_step", b, 1)
                dve.tensor_tensor(dt_w[:], dt_e, dt_w[:], ALU.subtract).then_inc(sem["dt_step"], 1)
                need(dve, "dt_step", b, 2)
                need(dve, "dt_log", b, 1)
                dve.tensor_tensor(dt_w[:], dt_w[:], dt_ln[:], ALU.add).then_inc(sem["dt_step"], 1)
                need(dve, "dt_step", b, 3)
                need(dve, "dt_parts", b, 4)
                dve.tensor_tensor(delta[:], dt_w[:], dt_pos[:], ALU.add).then_inc(sem["dt_step"], 1)

            def chunk_state(b):
                g = bank(b, "KV", P)
                dve.tensor_tensor(kv[:], g[:, 0:2], headblk[:].unsqueeze(1).broadcast_to([P, 2, P]), ALU.mult
                                  ).then_inc(sem["kv_ready"], 1)

            def gate_silu(b):
                need(dve, "gate_tanh", b, 1)
                dve.scalar_tensor_tensor(gate[:], gth[:], 1.0, glin[:], ALU.add, ALU.mult).then_inc(sem["gate_ready"], 1)

            def slot(b, i):
                return part if isinstance(b, int) and i % 2 else state

            def scan(b, i):
                flat = lambda ap: ap.rearrange("p n t -> p (n t)")
                need(dve, "decay_ready", b, UN * (i + 1))
                need(dve, "drive_ready", b, i + 1)
                if isinstance(b, int):
                    need(dve, "y_part", b, max(i - 1, 0))
                else:
                    need(dve, "part_ready", b, i)
                dve.tensor_tensor_scan(flat(slot(b, i)[:]), flat(decay[:, i % 2]), flat(drive[:, i % 2]), 0.0,
                                       ALU.mult, ALU.add).then_inc(sem["state_ready"], 1)

            def times_c(b, i):
                j, c = i % 2, i // 2
                if j == 0:
                    need(dve, f"c_in{c % 2}", b, 16 * (c // 2 + 1))
                need(dve, "state_ready", b, i + 1)
                dve.tensor_tensor(slot(b, i)[:], slot(b, i)[:], crow[:, c % 2], ALU.mult).then_inc(sem["out_ready"], 1)

            def pair(b, i):
                need(dve, "out_ready", b, i + 1)
                need(dve, "y_part", b, max(i - 1, 0))
                dve.tensor_tensor(part[:, i % 2], state[:, 0], state[:, 1], ALU.add
                                  ).then_inc(sem["part_ready"], 1)

            def decayed(b, i):
                need(dve, "gen_filled", b, G_SC + i + 1)
                need(dve, "av_done", b, max(i - 1, 0))
                h0 = 4 * (i // 2)
                dve.tensor_tensor(sc[:, i % 2], gen[(G_SC + i) % 2][:].rearrange("p (h i) -> p h i", h=4),
                                  dmask[:, h0:h0 + 4], ALU.mult).then_inc(sem["sc_ready"], 1)

            def masked_inputs(fb, which):
                for i in which:
                    slot = AM_ORDER[i]
                    need(dve, "mk_ready", fb, slot % 2 + 1)
                    dve.tensor_tensor(am_full[:, slot], a2p[slot // 2][:], mkT[:, slot % 2], ALU.mult
                                      ).then_inc(sem["am_ready"], 1)

            def norm_stats(b, src, st_, mv_, ve_, ready, n):
                need(dve, ready, b, n)
                for t in range(NT):
                    dve.bn_stats(st_[:, t], src[:, t]).then_inc(sem[ready], 1)
                need(dve, ready, b, n + 2)
                dve.memset(ve_[:], EPS).then_inc(sem[ready], 1)
                for t in range(NT):
                    dve.bn_aggr(mv_[:, t], st_[:, t]).then_inc(sem[ready], 1)
                need(dve, ready, b, n + 5)
                dve.tensor_tensor(ve_[:], mv_[:, :, 1], ve_[:], ALU.add).then_inc(sem[ready], 1)

            def norm_shift(b, mv_, rs_, nm_, pow_, done):
                need(dve, pow_, b, 1)
                dve.scalar_tensor_tensor(nm_[:], mv_[:, :, 0], -1.0, rs_[:], ALU.mult, ALU.mult).then_inc(sem[done], 1)

            def norm_apply(b, src, mv_, rs_, dst, pow_, done):
                need(dve, pow_, b, 1)
                for t in range(NT):
                    dve.tensor_scalar(dst[:, t], src[:, t], mv_[:, t, 0:1], rs_[:, t:t + 1], ALU.subtract, ALU.mult
                                      ).then_inc(sem[done], 1)

            def first(b):
                conv(b)
                step_size(b)
                dve.wait_ge(sem["w_rows"], 16)
                dve.wait_ge(sem["pool_const"], CONSTS)
                token_values(b)

            def later(b, fb):
                if b is not None:
                    conv(b)
                    token_values(b)
                need(dve, "x2T_ready", fb, 2)
                dve.tensor_tensor(x2s[:, 1], xf[XF_BANK[X_X2]][:], x2s[:, 0], ALU.subtract).then_inc(sem["xl_ready"], 1)
                route(fb, 0)
                if b is not None:
                    token_keys(b)
                route(fb, 1)
                if b is not None:
                    step_size(b)
                    chunk_state(b)
                need(dve, "a_filled", fb, 2)
                dve.wait_ge(sem["w_low"], BLOCKS - PER_W)
                masked_inputs(fb, (0, 1))
                for i in range(2):
                    need(dve, "amh_ready", fb, i + 1)
                    slot = AM_ORDER[i]
                    dve.tensor_tensor(am[:, 1, slot], am_full[:, slot], am[:, 0, slot], ALU.subtract
                                      ).then_inc(sem["aml_ready"], 1)
                masked_inputs(fb, (2, 3))
                if b is not None:
                    gate_silu(b)

            def split_low(blocks):
                for k in blocks:
                    w, c = SPLIT_ORDER[k] // PER_W, SPLIT_ORDER[k] % PER_W
                    cs = slice(c * BLOCK, (c + 1) * BLOCK)
                    dve.wait_ge(sem["w_high"], k + 1)
                    dve.tensor_tensor(wflat[:, 1, w, cs], raw[w % 2][:, cs], wflat[:, 0, w, cs], ALU.subtract
                                      ).then_inc(sem["w_low_b3"], 1)

            def stage(b, fb):
                if fb is None:
                    first(b)
                else:
                    later(b, fb)
                for n in range(len(MAIN)):
                    units = SCANS[n] if b is not None else []
                    if units:
                        scan(b, units[0])
                    if n == 0 and fb is None:
                        dve.wait_ge(sem["mask_in"], 48)
                        token_keys(b)
                        times_c(b, 0)
                        chunk_state(b)
                    if b is not None and n < 4:
                        decayed(b, 2 * n)
                    last = n == 11
                    if units and not last and not (n == 0 and fb is None):
                        times_c(b, units[0])
                    if n == 0 and fb is None:
                        gate_silu(b)
                    if fb is not None:
                        o = xf[XF_BANK[X_MAIN + n]]
                        need(dve, "th_ready", fb, n + 1)
                        dve.scalar_tensor_tensor(fs[:, n % 2], fth[:, n % 2], 1.0, o[:, 0], ALU.add, ALU.mult
                                                 ).then_inc(sem["s_ready"], 1)
                    if units and fb is not None and not last:
                        pair(b, units[0])
                    if fb is not None:
                        need(dve, "s_ready", fb, n + 1)
                        need(dve, "xs_ready", fb, max(n - 1, 0))
                        dve.tensor_tensor(fq[:, n % 2], fs[:, n % 2], o[:, 1], ALU.mult).then_inc(sem["q3_ready"], 1)
                    if units and last:
                        norm_shift(b, mv, rs, nm, "r1_pow", "r1_shift")
                        times_c(b, units[0])
                        if fb is not None:
                            pair(b, units[0])
                    if b is not None and n < 4:
                        decayed(b, 2 * n + 1)
                    for i in units[1:]:
                        scan(b, i)
                        times_c(b, i)
                        if fb is not None:
                            pair(b, i)
                    if b is not None:
                        if n == 4:
                            need(dve, "av_done", b, 8)
                            for t in range(2):
                                dve.bn_stats(gst[:, t], ret[:, t]).then_inc(sem["gn_step"], 1)
                            need(dve, "gn_step", b, 2)
                            dve.memset(geps[:, :, 1], EPS).then_inc(sem["gn_step"], 1)
                            for t in range(2):
                                dve.bn_aggr(gmv[:, t], gst[:, t]).then_inc(sem["gn_step"], 1)
                        if n == 5:
                            need(dve, "gen_filled", b, G_MEAN + 1)
                            dve.tensor_tensor(gavg[:], gen[G_MEAN % 2][:, 0:4].rearrange("p (t s) -> p t s", t=2), geps[:],
                                              ALU.add).then_inc(sem["gn_step"], 1)
                            need(dve, "gn_step", b, 6)
                            dve.tensor_tensor(gdev[:], gmv[:, :, 0], gavg[:, :, 0], ALU.subtract).then_inc(sem["gn_step"], 1)
                            need(dve, "gn_step", b, 7)
                            dve.tensor_tensor(gsq[:], gdev[:], gdev[:], ALU.mult).then_inc(sem["gn_step"], 1)
                        if n == 6:
                            need(dve, "gen_filled", b, G_VAR + 1)
                            dve.tensor_tensor(gvar[:], gen[G_VAR % 2][:, 0:2], gavg[:, :, 1], ALU.add).then_inc(sem["gn_step"], 1)
                        if n == 7:
                            need(dve, "gn_pow", b, 1)
                            dve.tensor_tensor(gscale[:], grs[:], v_("gnw"), ALU.mult).then_inc(sem["gn_step"], 1)
                            need(dve, "gn_step", b, 10)
                            dve.tensor_tensor(gms[:], gscale[:], gavg[:, :, 0], ALU.mult).then_inc(sem["gn_step"], 1)
                            need(dve, "gn_step", b, 11)
                            dve.tensor_tensor(gshift[:], v_("gnb"), gms[:], ALU.subtract).then_inc(sem["gn_step"], 1)
                        if n == 10:
                            g = bank(b, G_OUT, H)
                            need(dve, "xb_ready", b, 1)
                            need(dve, "decay_ready", b, 2 * DS)
                            dve.tensor_tensor(r1[:], g, xb[:], ALU.add).then_inc(sem["r1_ready"], 1)
                            norm_stats(b, r1, st, mv, ve, "r1_ready", 1)
                        if n == 11 and fb is None:
                            split_low(range(2 * PER_W, 3 * PER_W - 2))
                        if n == 12:
                            need(dve, "z_tanh", b, 1)
                            dve.scalar_tensor_tensor(zs[:], zth[:], 1.0, x1[:], ALU.add, ALU.mult).then_inc(sem["r2_ready"], 1)
                            need(dve, "y_part", b, UNITS)
                            if fb is None:
                                need(dve, "y_init", b, 2)
                                dve.tensor_tensor(yT[:], yT[:], acc[:], ALU.add).then_inc(dc, 1)
                                dve.wait_ge(dc, 5)
                            need(dve, "r2_ready", b, 1)
                            dve.scalar_tensor_tensor(yT[:], zs[:], 0.5, yT[:], ALU.mult, ALU.mult).then_inc(sem["yT_ready"], 1)
                            if fb is None:
                                split_low(range(3 * PER_W - 2, 3 * PER_W))
                        if n == 13:
                            g = bank(b, G_Y, H)
                            dve.tensor_tensor(r2[:], g, x1[:], ALU.add).then_inc(sem["r2_ready"], 1)
                            if fb is not None:
                                second_input(fb, 0)
                            norm_stats(b, r2, st, mv, ve, "r2_ready", 2)
                    elif n == 13:
                        second_input(fb, 0)
                if fb is not None:
                    second_input(fb, 1)
                    need(dve, "a2_ready", fb, 2)
                    dve.tensor_tensor(a2m[:, 0], a2m[:, 0], a2m[:, 1], ALU.add).then_inc(sem["a2_ready"], 1)
                if b is not None:
                    norm_shift(b, mv, rs, nm, "r2_pow", "r2_shift")
                if fb is not None:
                    need(dve, "down_done", fb, 1)
                    need(dve, "keep_ready", fb, 1)
                    dve.tensor_tensor(r3[:], acc[:], keep[:], ALU.add).then_inc(sem["r3_ready"], 1)
                    norm_stats(fb, r3, st3, mv3, ve3, "r3_ready", 1)
                    norm_apply(fb, r3, mv3, rs3, yo, "r3_pow", "y_ready")

            def second_input(fb, k):
                need(dve, "xs_used", fb, len(MAIN) - 1 + k)
                need(dve, "mk1_ready", fb, 1)
                dve.tensor_tensor(a2m[:, k], a2p[k][:], mkT[:, k], ALU.mult).then_inc(sem["a2_ready"], 1)

            def route(b, part_):
                step = [2 * part_]

                def did(ins):
                    step[0] += 1
                    ins.then_inc(sem["rt_step"], 1)
                    need(dve, "rt_step", b, step[0])

                wide = lambda ap: ap.unsqueeze(2).broadcast_to([P, NT, E])
                if part_ == 0:
                    need(dve, "xf_filled", b, X_LG + 1)
                    dve.tensor_copy(lg[:], xf[XF_BANK[X_LG]][:, 0, 0:NT * E].rearrange("p (t e) -> p t e", t=NT)
                                    ).then_inc(sem["lg_ready"], 1)
                    need(dve, "lg_ready", b, 1)
                    did(dve.tensor_reduce(t1[:], lg[:], AX.X, ALU.max))
                    did(dve.tensor_tensor(lg[:], lg[:], wide(t1[:]), ALU.subtract))
                if part_ == 1:
                    need(dve, "lg_exp", b, 1)
                    did(dve.tensor_reduce(t1[:], le[:], AX.X, ALU.add))
                    did(dve.reciprocal(t2[:], t1[:]))
                    did(dve.tensor_tensor(pr[:], le[:], wide(t2[:]), ALU.mult))
                    for k in range(2):
                        did(dve.tensor_reduce(top[:, :, k], pr[:], AX.X, ALU.max))
                        did(dve.tensor_tensor(eq[:], pr[:], wide(top[:, :, k]), ALU.is_equal))
                        did(dve.tensor_tensor(eq[:], eq[:], slots8[:].unsqueeze(1).broadcast_to([P, NT, E]), ALU.mult))
                        did(dve.tensor_reduce(t1[:], eq[:], AX.X, ALU.max))
                        did(dve.tensor_tensor((mk0, mk1[:])[k], eq[:], wide(t1[:]), ALU.is_equal))
                        if k == 0:
                            did(dve.scalar_tensor_tensor(pr[:], mk0, -4.0, pr[:], ALU.mult, ALU.add))
                    did(dve.tensor_tensor(md, mk1[:], mk0, ALU.subtract))
                    did(dve.tensor_tensor(t1[:], top[:, :, 0], top[:, :, 1], ALU.add))
                    did(dve.reciprocal(t2[:], t1[:]))
                    for k in range(2):
                        did(dve.scalar_tensor_tensor(rw[:, :, k], top[:, :, k], 0.5, t2[:], ALU.mult, ALU.mult))
                    did(dve.tensor_copy(rwr[:], rw[:]))
                    did(dve.tensor_copy(rwh, rwr[:]))
                    did(dve.tensor_tensor(rwl, rw[:], rwr[:], ALU.subtract))

            batches(dve, stage)


def kernel(**inputs):
    import numpy as np
    import concourse.bacc as bacc
    from concourse import mybir
    from concourse.bass_utils import run_bass_kernel_spmd

    a = {k: np.asarray(v) for k, v in inputs.items()}
    g = lambda n: a["L0_" + n]

    def cols(m):
        m = m.reshape(m.shape[0], -1)
        return m.reshape(-1, P, m.shape[1]).transpose(1, 0, 2).reshape(P, -1)

    flatT = lambda m: m.reshape(-1, m.shape[-1]).T
    vecs = np.concatenate([cols(g(n)) for n in ("attn_bq", "attn_bk", "attn_bg", "attn_gn_w", "attn_gn_b", "xattn_conv_w",
                                                "xattn_conv_b", "xattn_dt_proj_b", "xattn_D", "xattn_A_log")], axis=1)
    rows = np.stack([g("attn_bv"), g("attn_bo")])
    wattn = np.concatenate([cols(g(n)) for n in ("attn_wq", "attn_wk", "attn_wv", "attn_wg", "attn_wo")], axis=1)
    wssm = np.concatenate([flatT(g("xattn_in_proj_w")), cols(flatT(g("xattn_x_proj_w")))], axis=1)
    lora = lambda m: m.transpose(0, 2, 1).reshape(E * R, -1)
    wff = np.concatenate([cols(m) for m in (
        flatT(g("ffn_A1")), flatT(g("ffn_A3")), flatT(g("ffn_A2")), flatT(g("ffn_W2")), lora(g("ffn_B2")))], axis=1)
    x = a["x"]
    arrays = {
        "x": x.reshape(B, NT, P, H).transpose(0, 2, 1, 3),
        "xT": x.transpose(0, 2, 1).reshape(B, 2, P, S).transpose(0, 2, 1, 3),
        "ctxT": a["ctx_1024"].transpose(0, 2, 1),
        "vec": vecs, "rows": rows, "gamma": g("attn_gamma").reshape(HEADS, 1), "wattn": wattn, "wssm": wssm,
        "wdt": flatT(g("xattn_dt_proj_w")), "wroute": cols(flatT(g("ffn_Wg"))), "wff": wff,
        "wsp": np.stack([cols(m) for m in (flatT(g("ffn_W1")), flatT(g("ffn_W3")), lora(g("ffn_B1")), lora(g("ffn_B3")))]),
    }
    arrays = {"in_" + k: np.ascontiguousarray(v) for k, v in arrays.items()}
    nc = bacc.Bacc("TRN2", target_bir_lowering=False, num_devices=1)
    args = [nc.dram_tensor(k, v.shape, mybir.dt.from_np(v.dtype), kind="ExternalInput").ap() for k, v in arrays.items()]
    out = nc.dram_tensor("out_y", (B, P, NT, H), mybir.dt.float32, kind="ExternalOutput").ap()
    decoder_layer(nc, *args, out)
    got = run_bass_kernel_spmd(nc, [arrays], core_ids=[0]).results[0]["out_y"]
    return got.transpose(0, 2, 1, 3).reshape(B, S, H)
```
